# Optimizing a Trainium2 kernel written in Bass

```python
import numpy as np
import jax
import jax.numpy as jnp

def _softmax(x, axis=-1):
    return jax.nn.softmax(x, axis=axis)

def _gelu(x):
    return jax.nn.gelu(x, approximate=True)

def _silu(x):
    return jax.nn.silu(x)

def _sigmoid(x):
    return jax.nn.sigmoid(x)

def _layernorm(x, axis=-1, eps=1e-05):
    m = jnp.mean(x, axis=axis, keepdims=True)
    v = jnp.var(x, axis=axis, keepdims=True)
    return (x - m) / jnp.sqrt(v + eps)

def _scatter_add(tgt, idx, src, axis=0):
    return tgt.at[idx].add(src)

def _segment_sum(src, seg, n):
    return jax.ops.segment_sum(src, seg, n)
kernel_name = 'mk_vit_tower_d1_tok_img256_r4_f01844'

def setup_inputs(seed: int=0):
    np.random.seed(seed)
    _w = jnp.asarray

    def _rec_inputs():
        import jax
        import jax.numpy as jnp
        _rk = jax.random.key(seed)
        x = -0.000596345 + 1.00056 * jax.random.normal(jax.random.fold_in(_rk, 1), (128, 64, 64, 3), jnp.float32)
        return x
    x = _rec_inputs()

    def _L0_tok_setup():
        import jax, jax.numpy as jnp
        import numpy as np
        B, H, W = (16, 64, 64)
        WIDTH, LAYERS, M1, M2 = (32, 4, 12, 12)
        EPS = 1e-05

        def layer_norm(x, g, b):
            mu = jnp.mean(x, axis=-1, keepdims=True)
            var = jnp.mean((x - mu) ** 2, axis=-1, keepdims=True)
            return (x - mu) * jax.lax.rsqrt(var + EPS) * g + b

        def gelu(x):
            return jax.nn.gelu(x, approximate=False)

        def spectral_conv(x, w1, w2):
            b, c, h, w = x.shape
            x_ft = jnp.fft.rfft2(x)
            out_ft = jnp.zeros((b, w1.shape[1], h, w // 2 + 1), dtype=x_ft.dtype)
            out_ft = out_ft.at[:, :, :M1, :M2].set(jnp.einsum('bixy,ioxy->boxy', x_ft[:, :, :M1, :M2], w1))
            out_ft = out_ft.at[:, :, -M1:, :M2].set(jnp.einsum('bixy,ioxy->boxy', x_ft[:, :, -M1:, :M2], w2))
            return jnp.fft.irfft2(out_ft, s=(h, w))
        key = jax.random.key(seed)
        ks = jax.random.split(key, 16)
        scale = 1.0 / (WIDTH * WIDTH)
        d = {'x': jax.random.normal(ks[0], (B, H, W, 3), jnp.float32), 'fc0_w': jax.random.normal(ks[1], (3, WIDTH), jnp.float32) * 0.5, 'fc0_b': jnp.zeros((WIDTH,), jnp.float32), 'ln0_g': jnp.ones((WIDTH,), jnp.float32), 'ln0_b': jnp.zeros((WIDTH,), jnp.float32), 'w1r': jax.random.uniform(ks[2], (LAYERS, WIDTH, WIDTH, M1, M2), jnp.float32) * scale, 'w1i': jax.random.uniform(ks[3], (LAYERS, WIDTH, WIDTH, M1, M2), jnp.float32) * scale, 'w2r': jax.random.uniform(ks[4], (LAYERS, WIDTH, WIDTH, M1, M2), jnp.float32) * scale, 'w2i': jax.random.uniform(ks[5], (LAYERS, WIDTH, WIDTH, M1, M2), jnp.float32) * scale, 'conv_w': jax.random.normal(ks[6], (LAYERS, WIDTH, WIDTH), jnp.float32) * (1.0 / np.sqrt(WIDTH)), 'conv_b': jnp.zeros((LAYERS, WIDTH), jnp.float32), 'ln_g': jnp.ones((LAYERS, WIDTH), jnp.float32), 'ln_b': jnp.zeros((LAYERS, WIDTH), jnp.float32), 'fc1_w': jax.random.normal(ks[7], (WIDTH, 128), jnp.float32) * (1.0 / np.sqrt(WIDTH)), 'fc1_b': jnp.zeros((128,), jnp.float32), 'fc2_w': jax.random.normal(ks[8], (128, 64), jnp.float32) * (1.0 / np.sqrt(128)), 'fc2_b': jnp.zeros((64,), jnp.float32), 'fc3_w': jax.random.normal(ks[9], (64, 1), jnp.float32) * (1.0 / np.sqrt(64)), 'fc3_b': jnp.zeros((1,), jnp.float32)}
        return d
    _L0_tok_all = _L0_tok_setup()
    _L0_tok_in = {k: v for k, v in _L0_tok_all.items() if k in ('fc0_w', 'fc0_b', 'ln0_g', 'ln0_b', 'w1r', 'w1i', 'w2r', 'w2i', 'conv_w', 'conv_b', 'ln_g', 'ln_b', 'fc1_w', 'fc1_b', 'fc2_w', 'fc2_b', 'fc3_w', 'fc3_b')}
    del _L0_tok_all

    def _L0_attn_setup():
        import jax, jax.numpy as jnp
        import numpy as np
        EMBED_DIM = 64
        BATCH = 2
        SEQ = 256
        key = jax.random.key(seed)
        ks = jax.random.split(key, 9)
        d = EMBED_DIM
        s = 1.0 / np.sqrt(d)
        return {'x': jax.random.normal(ks[0], (BATCH, SEQ, d), dtype=jnp.float32), 'Wq': jax.random.uniform(ks[1], (d, d), jnp.float32, -s, s), 'bq': jax.random.uniform(ks[2], (d,), jnp.float32, -s, s), 'Wk': jax.random.uniform(ks[3], (d, d), jnp.float32, -s, s), 'bk': jax.random.uniform(ks[4], (d,), jnp.float32, -s, s), 'Wv': jax.random.uniform(ks[5], (d, d), jnp.float32, -s, s), 'bv': jax.random.uniform(ks[6], (d,), jnp.float32, -s, s), 'Wo': jax.random.uniform(ks[7], (d, d), jnp.float32, -s, s), 'bo': jax.random.uniform(ks[8], (d,), jnp.float32, -s, s)}
    _L0_attn_all = _L0_attn_setup()
    _L0_attn_in = {k: v for k, v in _L0_attn_all.items() if k in ('Wq', 'bq', 'Wk', 'bk', 'Wv', 'bv', 'Wo', 'bo')}
    del _L0_attn_all

    def _L0_ffn_setup():
        import jax, jax.numpy as jnp
        import numpy as np
        E = 8
        K = 2
        D = 64
        H = 128
        DOUT = 64
        EPS = 1e-05
        key = jax.random.key(seed)
        ks = jax.random.split(key, 9)
        s = 0.02
        return {'x': jax.random.normal(ks[0], (4, 2048, D), jnp.float32), 'gamma': 1.0 + 0.05 * jax.random.normal(ks[1], (D,), jnp.float32), 'beta': 0.05 * jax.random.normal(ks[2], (D,), jnp.float32), 'Wr': 0.01 * jax.random.normal(ks[3], (D, E), jnp.float32), 'br': jnp.zeros((E,), jnp.float32), 'W1': s * jax.random.normal(ks[4], (E, D, H), jnp.float32), 'b1': s * jax.random.normal(ks[5], (E, H), jnp.float32), 'W2': s * jax.random.normal(ks[6], (E, H, DOUT), jnp.float32), 'b2': s * jax.random.normal(ks[7], (E, DOUT), jnp.float32)}
    _L0_ffn_all = _L0_ffn_setup()
    _L0_ffn_in = {k: v for k, v in _L0_ffn_all.items() if k in ('gamma', 'beta', 'Wr', 'br', 'W1', 'b1', 'W2', 'b2')}
    del _L0_ffn_all
    return {'x': x, 'L0_tok_fc0_w': _L0_tok_in['fc0_w'], 'L0_tok_fc0_b': _L0_tok_in['fc0_b'], 'L0_tok_ln0_g': _L0_tok_in['ln0_g'], 'L0_tok_ln0_b': _L0_tok_in['ln0_b'], 'L0_tok_w1r': _L0_tok_in['w1r'], 'L0_tok_w1i': _L0_tok_in['w1i'], 'L0_tok_w2r': _L0_tok_in['w2r'], 'L0_tok_w2i': _L0_tok_in['w2i'], 'L0_tok_conv_w': _L0_tok_in['conv_w'], 'L0_tok_conv_b': _L0_tok_in['conv_b'], 'L0_tok_ln_g': _L0_tok_in['ln_g'], 'L0_tok_ln_b': _L0_tok_in['ln_b'], 'L0_tok_fc1_w': _L0_tok_in['fc1_w'], 'L0_tok_fc1_b': _L0_tok_in['fc1_b'], 'L0_tok_fc2_w': _L0_tok_in['fc2_w'], 'L0_tok_fc2_b': _L0_tok_in['fc2_b'], 'L0_tok_fc3_w': _L0_tok_in['fc3_w'], 'L0_tok_fc3_b': _L0_tok_in['fc3_b'], 'L0_attn_Wq': _L0_attn_in['Wq'], 'L0_attn_bq': _L0_attn_in['bq'], 'L0_attn_Wk': _L0_attn_in['Wk'], 'L0_attn_bk': _L0_attn_in['bk'], 'L0_attn_Wv': _L0_attn_in['Wv'], 'L0_attn_bv': _L0_attn_in['bv'], 'L0_attn_Wo': _L0_attn_in['Wo'], 'L0_attn_bo': _L0_attn_in['bo'], 'L0_ffn_gamma': _L0_ffn_in['gamma'], 'L0_ffn_beta': _L0_ffn_in['beta'], 'L0_ffn_Wr': _L0_ffn_in['Wr'], 'L0_ffn_br': _L0_ffn_in['br'], 'L0_ffn_W1': _L0_ffn_in['W1'], 'L0_ffn_b1': _L0_ffn_in['b1'], 'L0_ffn_W2': _L0_ffn_in['W2'], 'L0_ffn_b2': _L0_ffn_in['b2']}

def reference(x, L0_tok_fc0_w, L0_tok_fc0_b, L0_tok_ln0_g, L0_tok_ln0_b, L0_tok_w1r, L0_tok_w1i, L0_tok_w2r, L0_tok_w2i, L0_tok_conv_w, L0_tok_conv_b, L0_tok_ln_g, L0_tok_ln_b, L0_tok_fc1_w, L0_tok_fc1_b, L0_tok_fc2_w, L0_tok_fc2_b, L0_tok_fc3_w, L0_tok_fc3_b, L0_attn_Wq, L0_attn_bq, L0_attn_Wk, L0_attn_bk, L0_attn_Wv, L0_attn_bv, L0_attn_Wo, L0_attn_bo, L0_ffn_gamma, L0_ffn_beta, L0_ffn_Wr, L0_ffn_br, L0_ffn_W1, L0_ffn_b1, L0_ffn_W2, L0_ffn_b2):
    import jax
    import jax.numpy as jnp

    def _L0_tok_ref(x, fc0_w, fc0_b, ln0_g, ln0_b, w1r, w1i, w2r, w2i, conv_w, conv_b, ln_g, ln_b, fc1_w, fc1_b, fc2_w, fc2_b, fc3_w, fc3_b):
        import jax, jax.numpy as jnp
        import numpy as np
        B, H, W = (16, 64, 64)
        WIDTH, LAYERS, M1, M2 = (32, 4, 12, 12)
        EPS = 1e-05

        def layer_norm(x, g, b):
            mu = jnp.mean(x, axis=-1, keepdims=True)
            var = jnp.mean((x - mu) ** 2, axis=-1, keepdims=True)
            return (x - mu) * jax.lax.rsqrt(var + EPS) * g + b

        def gelu(x):
            return jax.nn.gelu(x, approximate=False)

        def spectral_conv(x, w1, w2):
            b, c, h, w = x.shape
            x_ft = jnp.fft.rfft2(x)
            out_ft = jnp.zeros((b, w1.shape[1], h, w // 2 + 1), dtype=x_ft.dtype)
            out_ft = out_ft.at[:, :, :M1, :M2].set(jnp.einsum('bixy,ioxy->boxy', x_ft[:, :, :M1, :M2], w1))
            out_ft = out_ft.at[:, :, -M1:, :M2].set(jnp.einsum('bixy,ioxy->boxy', x_ft[:, :, -M1:, :M2], w2))
            return jnp.fft.irfft2(out_ft, s=(h, w))
        h = layer_norm(x @ fc0_w + fc0_b, ln0_g, ln0_b)
        h = jnp.transpose(h, (0, 3, 1, 2))
        for i in range(LAYERS):
            w1 = w1r[i] + 1j * w1i[i]
            w2 = w2r[i] + 1j * w2i[i]
            x1 = spectral_conv(h, w1, w2)
            x2 = jnp.einsum('bchw,oc->bohw', h, conv_w[i]) + conv_b[i][None, :, None, None]
            h = x1 + x2
            h = jnp.transpose(h, (0, 2, 3, 1))
            h = layer_norm(h, ln_g[i], ln_b[i])
            if i < LAYERS - 1:
                h = gelu(h)
            h = jnp.transpose(h, (0, 3, 1, 2))
        h = jnp.transpose(h, (0, 2, 3, 1))
        h = gelu(h @ fc1_w + fc1_b)
        h = gelu(h @ fc2_w + fc2_b)
        h = h @ fc3_w + fc3_b
        return h[..., 0]

    def _L0_attn_ref(x, Wq, bq, Wk, bk, Wv, bv, Wo, bo):
        import jax, jax.numpy as jnp
        import numpy as np
        EMBED_DIM = 64
        BATCH = 2
        SEQ = 256
        d = x.shape[-1]
        Q = x @ Wq.T + bq
        K = x @ Wk.T + bk
        V = x @ Wv.T + bv
        diff = Q[:, :, None, :] - K[:, None, :, :]
        dist = jnp.sqrt(jnp.sum(diff * diff, axis=-1))
        attn = jax.nn.softmax(-dist / jnp.sqrt(jnp.float32(d)), axis=-1)
        attended = jnp.einsum('bqk,bkd->bqd', attn, V)
        return attended @ Wo.T + bo

    def _L0_ffn_ref(x, gamma, beta, Wr, br, W1, b1, W2, b2):
        import jax, jax.numpy as jnp
        import numpy as np
        E = 8
        K = 2
        D = 64
        H = 128
        DOUT = 64
        EPS = 1e-05
        mu = jnp.mean(x, axis=-1, keepdims=True)
        var = jnp.mean(jnp.square(x - mu), axis=-1, keepdims=True)
        xn = (x - mu) * jax.lax.rsqrt(var + EPS) * gamma + beta
        logits = jnp.einsum('bsd,de->bse', xn, Wr) + br
        top_vals, top_idx = jax.lax.top_k(logits, K)
        w = jax.nn.softmax(top_vals, axis=-1)
        w_full = jnp.einsum('bsk,bske->bse', w, jax.nn.one_hot(top_idx, E, dtype=w.dtype))
        y = jnp.zeros(x.shape[:-1] + (DOUT,), x.dtype)
        for e in range(E):
            h = jax.nn.gelu(jnp.einsum('bsd,dh->bsh', xn, W1[e]) + b1[e], approximate=False)
            y_e = jnp.einsum('bsh,hd->bsd', h, W2[e]) + b2[e]
            y = y + y_e * w_full[..., e, None]
        return y
    h = _L0_tok_ref(x, L0_tok_fc0_w, L0_tok_fc0_b, L0_tok_ln0_g, L0_tok_ln0_b, L0_tok_w1r, L0_tok_w1i, L0_tok_w2r, L0_tok_w2i, L0_tok_conv_w, L0_tok_conv_b, L0_tok_ln_g, L0_tok_ln_b, L0_tok_fc1_w, L0_tok_fc1_b, L0_tok_fc2_w, L0_tok_fc2_b, L0_tok_fc3_w, L0_tok_fc3_b)
    h = h + _L0_attn_ref(_layernorm(h, axis=-1), L0_attn_Wq, L0_attn_bq, L0_attn_Wk, L0_attn_bk, L0_attn_Wv, L0_attn_bv, L0_attn_Wo, L0_attn_bo)
    h = h + _L0_ffn_ref(_layernorm(h, axis=-1), L0_ffn_gamma, L0_ffn_beta, L0_ffn_Wr, L0_ffn_br, L0_ffn_W1, L0_ffn_b1, L0_ffn_W2, L0_ffn_b2)
    return h

_drawn_inputs = setup_inputs


def setup_inputs(seed=0):
    import zlib

    import numpy as np

    out = dict(_drawn_inputs(seed))
    spreads = {'L0_tok_fc0_b': (0.0, 0.1),
     'L0_tok_ln0_g': (1.0, 0.2),
     'L0_tok_ln0_b': (0.0, 0.1),
     'L0_tok_conv_b': (0.0, 0.1),
     'L0_tok_ln_g': (1.0, 0.2),
     'L0_tok_ln_b': (0.0, 0.1),
     'L0_tok_fc1_b': (0.0, 0.1),
     'L0_tok_fc2_b': (0.0, 0.1),
     'L0_ffn_br': (0.0, 0.1)}
    factors = {'L0_tok_w1r': 8.0,
     'L0_tok_w1i': 22.735,
     'L0_tok_w2r': 25.283,
     'L0_tok_w2i': 24.374,
     'L0_attn_Wq': 8.0,
     'L0_attn_bq': 22.969,
     'L0_attn_Wk': 7.484,
     'L0_attn_bk': 24.677,
     'L0_ffn_gamma': 8.0,
     'L0_ffn_beta': 8.0,
     'L0_ffn_b1': 8.0}
    for name, (base, spread) in spreads.items():
        noise = np.random.default_rng([zlib.crc32(name.encode()), seed]).standard_normal(out[name].shape)
        drawn = base * np.exp(spread * noise) if base else spread * noise
        out[name] = jnp.asarray(drawn.astype(out[name].dtype))
    for name, factor in factors.items():
        out[name] = (out[name] * factor).astype(out[name].dtype)
    return out
```

```python
import concourse.bass as bass
from concourse import mybir
from contextlib import ExitStack

B, HH, WW, CH, LAYERS, M = 128, 64, 64, 32, 4, 12
QUADS = B // 4
UNITS = 8
KX = M + 1
MODES = KX * M
COMP = 4
EPS = 1e-5
F1, F2 = 128, 64
LAG_XH, LAG_T1, LAG_T2, LAG_F = 4, 5, 6, 7
OCH = 8
ROUNDS = 2 * (CH // OCH)
GROUPS = MODES // 4
D, E, H = 64, 8, 128
PAIRS = 8
STEPS = B // 2 // PAIRS


def vit_tower(nc, x, p, cst, out, scratch):
    f32, i32 = mybir.dt.float32, mybir.dt.int32
    ALU, ACT, AX = mybir.AluOpType, mybir.ActivationFunctionType, mybir.AxisListType
    xmodes, ymodes, hstore, tok, fc0_rows = scratch

    ctx = ExitStack()
    with ctx:
        def sb(name, shape, dt=f32):
            return ctx.enter_context(nc.sbuf_tensor(name, shape, dt))

        def sem(name):
            return ctx.enter_context(nc.semaphore(name))

        wslot = sb("wslot", [128, COMP, CH, MODES])
        big = sb("big", [128, B * MODES])
        modes = big[:, :].rearrange("p (i m) -> p i m", m=MODES)
        taken = [0]

        def carve(n):
            at = taken[0]
            taken[0] += n
            assert taken[0] <= B * MODES
            return big[:, at:at + n]

        h_in = [carve(2048) for _ in range(2)]
        h_new = [carve(2048) for _ in range(2)]
        y_sb = [carve(512) for _ in range(8)]
        y_sq = [carve(512) for _ in range(2)]
        xhat = [carve(512) for _ in range(2)]
        h_px = [carve(512) for _ in range(2)]
        z_kx = carve(2048).rearrange("p (j n) -> p j n", j=2)
        t_w = carve(2048).rearrange("p (j n) -> p j n", j=2)
        fw_sb = sb("fw_sb", [128, 832])
        tok_sb = big[0:64, 4096:8192]
        gelu1 = [t_w[:, 0, 0:512], t_w[:, 0, 512:1024]]
        gelu2 = [t_w[:, 1, 0:512], t_w[:, 1, 512:1024]]
        y_raw = sb("y_raw", [128, COMP * MODES])
        y_kk = sb("y_kk", [128, 1024])
        y_kt = sb("y_kt", [128, 1024])
        x_out = sb("x_out", [128, COMP, KX, M])
        x_in = sb("x_in", [128, 2, WW * 3])
        x_cur = sb("x_cur", [128, 2, WW * 3])
        x_tr = sb("x_tr", [64, 2, 128])
        ss = sb("ss", [128, 2, 64])
        var = sb("var", [128, 64])
        nt = sb("nt", [128, 64])
        rstd = sb("rstd", [128, 2, 64])
        w1_raw = sb("w1_raw", [128, OCH, M * M])
        w2_raw = sb("w2_raw", [128, OCH, M * M])
        w2_sg = sb("w2_sg", [128, OCH, M * M])

        ident = sb("ident", [128, 128])
        c_center = sb("c_center", [128, 128])
        c_fwh = sb("c_fwh", [128, 64])
        c_fww = sb("c_fww", [128, 2, 128])
        c_inw = sb("c_inw", [128, 2, 128])
        c_inh = sb("c_inh", [128, 2, 128])
        c_sign = sb("c_sign", [128, 8])
        fc0_bd = sb("fc0_bd", [64, 512])
        fc0_t = sb("fc0_t", [32, 4])
        fc0_c = sb("fc0_c", [4, 32])
        conv_w = sb("conv_w", [32, LAYERS, 32])
        conv_bd = sb("conv_bd", [128, LAYERS, 128])
        conv_now = sb("conv_now", [128, 128])
        bias_raw = sb("bias_raw", [128, LAYERS])
        bias_now = sb("bias_now", [128, 1])
        g_all = sb("g_all", [128, 2, 5])
        g_now = sb("g_now", [128, 2])
        fc1_w = sb("fc1_w", [128, 4, F1])
        fc1_b = sb("fc1_b", [128, 1])
        fc2_w = sb("fc2_w", [128, F2])
        fc2_b = sb("fc2_b", [128, 1])
        fc3_w = sb("fc3_w", [128, 32])
        fc3_b = sb("fc3_b", [64, 1])

        ps = [ctx.enter_context(nc.psum_tensor(f"bank{i}", [128, 512], f32)) for i in range(4)]
        ps_y, ps_t1, ps_t2 = [ps[0], ps[1]], ps[2], ps[3]
        ps_s = ctx.enter_context(nc.psum_tensor("ps_s", [128, 2, 512], f32))
        ps_f = ctx.enter_context(nc.psum_tensor("ps_f", [128, 2, 512], f32))

        s = {n: sem(n) for n in (
            "const_in", "const_zero", "fc0_center", "fc0_copied", "fc0_stored", "fc0_placed", "conv_center", "conv_placed",
            "x_loaded", "x_ready", "x_turned", "x_copied",
            "h_loaded0", "h_loaded1", "h_stored0", "h_stored1", "yraw_loaded", "xmodes_stored",
            "y_done", "sq_done", "y_read", "ss_done", "norm_step", "xhat_done", "t1_done", "act_done", "t2_done",
            "px_done", "f_done", "tw_done", "fw_done", "fw_read", "xout_done",
            "yc_done", "ykk_done", "ykt_done", "iw_done", "iw_read",
            "now_done", "modes_loaded", "mix_done", "mix_act", "mix_dve", "ymodes_stored",
            "w_raw", "w_step",
            "fc1_done", "g1_done", "fc2_done", "g2_done", "fc3_done", "tok_done", "tok_stored")}
        h_loaded = [s["h_loaded0"], s["h_loaded1"]]
        h_stored = [s["h_stored0"], s["h_stored1"]]

        primed = [s[n] for n in ("iw_read", "yc_done", "ykt_done", "iw_done", "mix_done", "fw_read", "xout_done", "xmodes_stored",
                                 "h_stored0", "h_stored1")]

        def wait(eng, name, value):
            if isinstance(value, int) and value <= 0:
                return
            which = s[name] if isinstance(name, str) else name
            eng.wait_ge(which, value + 1 if any(which is p_ for p_ in primed) else value)

        def then(eng, name, value):
            wait(eng, name, value)
            if not isinstance(value, int):
                eng.nop(nofuse=True)

        block = ctx.enter_context(nc.Block())

        def run_phase(eng, base, kind, body):
            body(kind, 0, base, first=True, more=True)
            with eng.Fori(1, QUADS - 1) as q:
                body(kind, q, base + q, first=False, more=True)
            body(kind, QUADS - 1, base + QUADS - 1, first=False, more=False)
            body(kind, QUADS, base + QUADS, first=False, more=False, drain=True)

        def there(k, lag, first, drain):
            return not drain if k >= lag else not first

        consts, zeroed = [], []

        free = [0]

        def work(n, rows=128):
            at = free[0]
            free[0] += n
            assert free[0] <= B * MODES, free[0]
            return big[0:rows, at:at + n]

        kept = [0]
        wflat = wslot[:, :, :, :].rearrange("p a o m -> p (a o m)")

        def keep(n, rows=128):
            at = kept[0]
            kept[0] += n
            return wflat[0:rows, at:at + n]

        TOK = PAIRS * 128
        q_wt, k_wt, v_wt, o_wt = (keep(D, D) for _ in range(4))
        q_b, k_b, q_b2 = keep(1, D), keep(1, D), keep(1, D)
        v_b, o_b = keep(D, D), keep(D)
        gamma, beta, r_b, lower = keep(D), keep(D), keep(E), keep(E * E)
        r_w = keep(E, D)
        e_w1, e_w2 = keep(E * H, D).rearrange("p (e h) -> p e h", e=E), keep(E * D).rearrange("p (e d) -> p e d", e=E)
        e_b1, e_b2 = keep(E), keep(D, E)
        pick = keep(E * 128, E).rearrange("p (e h) -> p e h", e=E)
        ones = keep(D, D)

        tok_t, h_tok, cen, sqr, nrm = (work(512) for _ in range(5))
        nrm_t, q2_t, qs_t, k_t, ks_t, v_tok = (work(TOK, D) for _ in range(6))
        d2, dist, prob, pnorm = (work(512) for _ in range(4))
        prob_t, att_t = work(TOK, D), qs_t
        h_res, nrm2, feat = work(512), work(512), work(512)
        feat_t = work(TOK, D)
        logit, expw, mask, wfull = (work(PAIRS * E) for _ in range(4))
        beats, ties = work(512), work(512)
        w_t = work(TOK, E)
        hid = [work(512) for _ in range(2)]
        hidw = [work(512) for _ in range(2)]
        y_t = ks_t
        o_tok = work(512)
        a_mean, a_var, a_nt, a_rs = (work(PAIRS) for _ in range(4))
        a = {n: sem("a_" + n) for n in (
            "const", "in", "h", "nrm", "nrmt", "nrmtc", "q", "k", "v", "qc", "kc", "vc", "s", "d2", "dist", "dm", "p", "pn", "pt",
            "ptc", "at", "atc", "o", "feat", "featt", "feattc", "logit", "ex", "exc", "w", "wt", "wtc", "up", "bc", "g", "gw",
            "down", "yc", "yt", "out", "stored", "step", "ones", "qb2")}
        primed += [a["yt"], a["h"], a["stored"]]
        DVE_STEPS = 69
        a_consts = []

        def attention_load(sp):
            lst = [(q_wt, p["attn_Wq"].rearrange("o i -> i o")), (k_wt, p["attn_Wk"].rearrange("o i -> i o")),
                   (v_wt, p["attn_Wv"].rearrange("o i -> i o")), (o_wt, p["attn_Wo"].rearrange("o i -> i o")),
                   (q_b, p["attn_bq"].unsqueeze(1)), (k_b, p["attn_bk"].unsqueeze(1)),
                   (v_b, p["attn_bv"].unsqueeze(0).to_broadcast([D, D])), (o_b, p["attn_bo"].unsqueeze(0).to_broadcast([128, D])),
                   (gamma, p["ffn_gamma"].unsqueeze(0).to_broadcast([128, D])),
                   (beta, p["ffn_beta"].unsqueeze(0).to_broadcast([128, D])),
                   (r_b, p["ffn_br"].unsqueeze(0).to_broadcast([128, E])), (lower, cst["lower"]),
                   (r_w, p["ffn_Wr"]), (e_w1, p["ffn_W1"].rearrange("e d h -> d e h")),
                   (e_w2, p["ffn_W2"].rearrange("e h d -> h e d")), (e_b1, p["ffn_b1"].rearrange("e h -> h e")),
                   (e_b2, p["ffn_b2"]), (pick, cst["pick"].rearrange("p (e h) -> p e h", e=E))]
            for dst, src in lst:
                sp.dma_start(dst, src, allow_slow_non_contiguous=True).then_inc(a["const"], 16)
            a_consts.append(16 * len(lst))

        def attention_sync(sp):
            with sp.Fori(0, STEPS) as it:
                then(sp, a["h"], it)
                for i in range(2):
                    sp.dma_start(tok_t[64 * i:64 * i + 64, :].rearrange("w (n h) -> w n h", n=PAIRS),
                                 tok[bass.ds(it * 2 * PAIRS, 2 * PAIRS)].rearrange("(n i) q (w h) -> i (q w) n h", i=2, h=HH)[i]
                                 ).then_inc(a["in"], 16)
                then(sp, a["out"], it + 1)
                for i in range(2):
                    sp.dma_start(out[bass.ds(it * 2 * PAIRS, 2 * PAIRS)].rearrange("(n i) s d -> i s n d", i=2)[i],
                                 o_tok[64 * i:64 * i + 64, :].rearrange("p (n d) -> p n d", n=PAIRS)
                                 ).then_inc(a["stored"], 16)
            wait(sp, a["stored"], 32 * STEPS)

        def attention_pool(pool):
            wait(pool, "mix_done", LAYERS * GROUPS)
            nc.gpsimd.memset(ones, 1.0).then_inc(a["ones"], 1)

        s_flat, f_flat = (t[:, :, :].rearrange("p a n -> p (a n)") for t in (ps_s, ps_f))

        def attention_tensor(pe):
            mm = nc.tensor.matmul
            pe.wait_ge(a["const"], a_consts[0])
            pe.wait_ge(a["ones"], 1)

            def turn(dst, src, rows, width):
                for n in range(PAIRS):
                    last = mm(dst[0:width, 128 * n:128 * n + 128], src[:, width * n:width * n + width], ident[:, :],
                              start=True, stop=True)
                return last

            with pe.Fori(0, STEPS) as it:
                pe.wait_ge(a["in"], 32 * it + 32)
                then(pe, a["yt"], it)
                for n in range(PAIRS):
                    for i in range(2):
                        r = slice(64 * i, 64 * i + 64)
                        last = mm(ps[0][r, 64 * n:64 * n + 64], tok_t[r, 64 * n:64 * n + 64], ident[r, r], start=True, stop=True)
                last.then_inc(a["h"], 1)
                pe.wait_ge(a["nrm"], it + 1)
                turn(s_flat, nrm, 128, D).then_inc(a["nrmt"], 1)
                then(pe, a["nrmtc"], it + 1)
                for c in range(2):
                    last = mm(ps_f[0:D, c, :], q_wt, nrm_t[:, 512 * c:512 * c + 512], start=True, stop=True)
                last.then_inc(a["q"], 1)
                for c in range(2):
                    last = mm(ps_s[0:D, c, :], k_wt, nrm_t[:, 512 * c:512 * c + 512], start=True, stop=True)
                last.then_inc(a["k"], 1)
                for i in range(2 * PAIRS):
                    last = mm(ps[1 + i // PAIRS][0:D, 64 * (i % PAIRS):64 * (i % PAIRS) + 64], nrm_t[:, 64 * i:64 * i + 64], v_wt,
                              start=True, stop=True)
                last.then_inc(a["v"], 1)
                pe.wait_ge(a["qc"], it + 1)
                then(pe, a["kc"], it + 1)
                for n in range(PAIRS):
                    for i in range(2):
                        c = slice(128 * n + 64 * i, 128 * n + 64 * i + 64)
                        dst = ps[3][64 * i:64 * i + 64, 64 * n:64 * n + 64]
                        mm(dst, q2_t[:, c], k_t[:, c], start=True, stop=False)
                        mm(dst, ones, ks_t[:, c], start=False, stop=False)
                        last = mm(dst, qs_t[:, c], ones, start=False, stop=True)
                last.then_inc(a["s"], 1)
                pe.wait_ge(a["pn"], it + 1)
                turn(f_flat, pnorm, 128, 64).then_inc(a["pt"], 1)
                pe.wait_ge(a["ptc"], it + 1)
                then(pe, a["vc"], it + 1)
                for i in range(2 * PAIRS):
                    c = slice(64 * i, 64 * i + 64)
                    last = mm(s_flat[0:D, c], v_tok[:, c], prob_t[:, c], start=True, stop=True)
                last.then_inc(a["at"], 1)
                pe.wait_ge(a["atc"], it + 1)
                for n in range(PAIRS):
                    last = mm(ps[1][:, 64 * n:64 * n + 64], att_t[:, 128 * n:128 * n + 128], o_wt, start=True, stop=True)
                last.then_inc(a["o"], 1)
                pe.wait_ge(a["feat"], it + 1)
                turn(s_flat, feat, 128, D).then_inc(a["featt"], 1)
                pe.wait_ge(a["feattc"], it + 1)
                for n in range(PAIRS):
                    last = mm(ps[2][:, E * n:E * n + E], feat_t[:, 128 * n:128 * n + 128], r_w, start=True, stop=True)
                last.then_inc(a["logit"], 1)
                pe.wait_ge(a["w"], it + 1)
                turn(f_flat, wfull, 128, E).then_inc(a["wt"], 1)
                pe.wait_ge(a["wtc"], it + 1)

                def down(t):
                    c, e = t // E, t % E
                    pe.wait_ge(a["gw"], it * 2 * E + t + 1)
                    if e == 0:
                        mm(ps_f[0:D, c, :], e_b2, w_t[:, 512 * c:512 * c + 512], start=True, stop=False)
                    mm(ps_f[0:D, c, :], e_w2[:, e, :], hidw[t % 2], start=False, stop=(e == E - 1)).then_inc(a["down"], 1)

                for t in range(2 * E):
                    c, e = t // E, t % E
                    if t >= 2:
                        pe.wait_ge(a["gw"], it * 2 * E + t - 1)
                    mm(ps[t % 2][:, :], e_w1[:, e, :], feat_t[:, 512 * c:512 * c + 512], start=True, stop=True).then_inc(a["up"], 1)
                    mm(ps[2 + t % 2][:, :], pick[:, e, :], w_t[:, 512 * c:512 * c + 512], start=True, stop=True).then_inc(a["bc"], 1)
                    if t:
                        down(t - 1)
                down(2 * E - 1)
                pe.wait_ge(a["yc"], it + 1)
                for n in range(PAIRS):
                    last = mm(ps[3][:, 64 * n:64 * n + 64], y_t[:, 128 * n:128 * n + 128], ident[0:D, 0:D], start=True, stop=True)
                last.then_inc(a["yt"], 1)

        def attention_scalar(act):
            af = nc.scalar.activation
            act.wait_ge(a["const"], a_consts[0])
            af(q_b2, q_b, ACT.Copy, scale=-2.0).then_inc(a["qb2"], 1)
            act.wait_ge(a["qb2"], 1)
            with act.Fori(0, STEPS) as it:
                act.wait_ge(a["nrmt"], it + 1)
                af(nrm_t, s_flat[0:D, :], ACT.Copy).then_inc(a["nrmtc"], 1)
                act.wait_ge(a["q"], it + 1)
                af(q2_t, f_flat[0:D, :], ACT.Identity, bias=q_b2, scale=-2.0)
                af(qs_t, f_flat[0:D, :], ACT.Square, bias=q_b).then_inc(a["qc"], 1)
                act.wait_ge(a["k"], it + 1)
                af(k_t, s_flat[0:D, :], ACT.Identity, bias=k_b)
                af(ks_t, s_flat[0:D, :], ACT.Square, bias=k_b).then_inc(a["kc"], 1)
                act.wait_ge(a["d2"], it + 1)
                af(dist, d2, ACT.Sqrt).then_inc(a["dist"], 1)
                act.wait_ge(a["dm"], it + 1)
                af(prob, d2, ACT.Exp, scale=-1.0 / D ** 0.5).then_inc(a["p"], 1)
                act.wait_ge(a["pt"], it + 1)
                af(prob_t, f_flat[0:D, :], ACT.Copy).then_inc(a["ptc"], 1)
                act.wait_ge(a["at"], it + 1)
                af(att_t, s_flat[0:D, :], ACT.Copy).then_inc(a["atc"], 1)
                act.wait_ge(a["featt"], it + 1)
                af(feat_t, s_flat[0:D, :], ACT.Copy).then_inc(a["feattc"], 1)
                act.wait_ge(a["ex"], it + 1)
                af(expw, mask, ACT.Exp).then_inc(a["exc"], 1)
                act.wait_ge(a["wt"], it + 1)
                af(w_t, f_flat[0:E, :], ACT.Copy).then_inc(a["wtc"], 1)
                for t in range(2 * E):
                    act.wait_ge(a["up"], it * 2 * E + t + 1)
                    if t >= 2:
                        act.wait_ge(a["gw"], it * 2 * E + t - 1)
                    af(hid[t % 2], ps[t % 2][:, :], ACT.Gelu, bias=e_b1[:, t % E:t % E + 1]).then_inc(a["g"], 1)
                act.wait_ge(a["down"], (it + 1) * 2 * E)
                af(y_t, f_flat[0:D, :], ACT.Copy).then_inc(a["yc"], 1)

        def attention_vector(dve, newton):
            v_ = nc.vector

            def groups(t, w=D):
                return t.rearrange("p (n d) -> p n d", d=w)

            def spread(t, w=D):
                return t.unsqueeze(2).to_broadcast([128, PAIRS, w])

            def row(t, rows=128, n=PAIRS):
                return t.unsqueeze(1).to_broadcast([rows, n, t.shape[-1]])

            with dve.Fori(0, STEPS) as it:
                c = [0]

                def link(ins):
                    c[0] += 1
                    ins.then_inc(a["step"], 1)
                    dve.wait_ge(a["step"], it * DVE_STEPS + c[0])

                def norm(dst, src):
                    link(v_.tensor_reduce(a_mean, groups(src), AX.X, ALU.add))
                    link(v_.tensor_scalar(a_mean, a_mean, 1.0 / D, None, ALU.mult))
                    link(v_.tensor_tensor(groups(cen), groups(src), spread(a_mean), ALU.subtract))
                    link(v_.tensor_tensor(sqr, cen, cen, ALU.mult))
                    link(v_.tensor_reduce(a_var, groups(sqr), AX.X, ALU.add))
                    v_.tensor_scalar(a_var, a_var, 1.0 / D, EPS, ALU.mult, ALU.add).then_inc(a["step"], 1)
                    newton(dve, a["step"], it * DVE_STEPS + c[0] + 1, a_rs, a_nt, a_var)
                    c[0] += 12
                    dve.wait_ge(a["step"], it * DVE_STEPS + c[0])
                    return v_.tensor_tensor(groups(dst), groups(cen), spread(a_rs), ALU.mult)

                wait(dve, a["h"], it + 1)
                link(v_.tensor_copy(h_tok, ps[0][:, :]))
                norm(nrm, h_tok).then_inc(a["nrm"], 1)
                dve.wait_ge(a["v"], it + 1)
                for i in range(2):
                    last = v_.tensor_tensor(groups(v_tok[:, 512 * i:512 * i + 512]), groups(ps[1 + i][0:D, :]), row(v_b, D), ALU.add)
                last.then_inc(a["vc"], 1)
                dve.wait_ge(a["s"], it + 1)
                v_.tensor_scalar(d2, ps[3][:, :], 0.0, None, ALU.max).then_inc(a["d2"], 1)
                dve.wait_ge(a["dist"], it + 1)
                link(v_.tensor_reduce(a_mean, groups(dist), AX.X, ALU.min))
                v_.tensor_tensor(groups(d2), groups(dist), spread(a_mean), ALU.subtract).then_inc(a["dm"], 1)
                dve.wait_ge(a["p"], it + 1)
                link(v_.tensor_reduce(a_var, groups(prob), AX.X, ALU.add))
                link(v_.reciprocal(a_rs, a_var))
                v_.tensor_tensor(groups(pnorm), groups(prob), spread(a_rs), ALU.mult).then_inc(a["pn"], 1)
                dve.wait_ge(a["o"], it + 1)
                link(v_.tensor_tensor(h_res, ps[1][:, :], h_tok, ALU.add))
                link(v_.tensor_tensor(groups(h_res), groups(h_res), row(o_b), ALU.add))
                link(norm(nrm2, h_res))
                link(norm(nrm2, nrm2))
                link(v_.tensor_tensor(groups(feat), groups(nrm2), row(gamma), ALU.mult))
                v_.tensor_tensor(groups(feat), groups(feat), row(beta), ALU.add).then_inc(a["feat"], 1)
                dve.wait_ge(a["logit"], it + 1)
                link(v_.tensor_tensor(groups(logit, E), groups(ps[2][:, 0:PAIRS * E], E), row(r_b), ALU.add))
                mine = groups(logit, E).unsqueeze(3).to_broadcast([128, PAIRS, E, E])
                other = groups(logit, E).unsqueeze(2).to_broadcast([128, PAIRS, E, E])
                four = lambda t: t.rearrange("p (n e f) -> p n e f", e=E, f=E)
                v_.tensor_tensor(four(beats), other, mine, ALU.is_gt)
                link(v_.tensor_tensor(four(ties), other, mine, ALU.is_equal))
                link(v_.tensor_tensor(groups(ties, E * E), groups(ties, E * E), row(lower), ALU.mult))
                link(v_.tensor_tensor(beats, beats, ties, ALU.add))
                link(v_.tensor_reduce(wfull, four(beats), AX.X, ALU.add))
                link(v_.tensor_reduce(a_mean, groups(logit, E), AX.X, ALU.max))
                v_.tensor_tensor(groups(mask, E), groups(logit, E), spread(a_mean, E), ALU.subtract).then_inc(a["ex"], 1)
                dve.wait_ge(a["exc"], it + 1)
                link(v_.scalar_tensor_tensor(wfull, wfull, 1.5, expw, ALU.is_lt, ALU.mult))
                link(v_.tensor_reduce(a_var, groups(wfull, E), AX.X, ALU.add))
                link(v_.reciprocal(a_rs, a_var))
                v_.tensor_tensor(groups(wfull, E), groups(wfull, E), spread(a_rs, E), ALU.mult).then_inc(a["w"], 1)
                for t in range(2 * E):
                    dve.wait_ge(a["g"], it * 2 * E + t + 1)
                    dve.wait_ge(a["bc"], it * 2 * E + t + 1)
                    if t >= 2:
                        dve.wait_ge(a["down"], it * 2 * E + t - 1)
                    v_.tensor_tensor(hidw[t % 2], hid[t % 2], ps[2 + t % 2][:, :], ALU.mult).then_inc(a["gw"], 1)
                wait(dve, a["yt"], it + 1)
                wait(dve, a["stored"], 32 * it)
                v_.tensor_tensor(o_tok, ps[3][:, :], h_res, ALU.add).then_inc(a["out"], 1)
                assert c[0] == DVE_STEPS, c[0]

        @block.sync
        def _(sp):
            plain = [
                (ident[:, :], cst["ident"]), (c_center[:, :], cst["center"]), (c_fwh[:, :], cst["fwd_h"]),
                (c_fww[:, :, :], cst["fwd_w"]), (c_inw[:, :, :], cst["inv_w"]), (c_inh[:, :, :], cst["inv_h"]),
                (c_sign[:, :], cst["sign"]),
                (fc0_t[:, 0:3], p["tok_fc0_w"].rearrange("c o -> o c")), (fc0_t[:, 3:4], p["tok_fc0_b"].unsqueeze(1)),
                (conv_w[:, :, :], p["tok_conv_w"].rearrange("l o c -> o l c")),
                (fc1_b[:, :], p["tok_fc1_b"].unsqueeze(1)), (fc2_w[:, :], p["tok_fc2_w"]),
                (fc2_b[0:64, :], p["tok_fc2_b"].unsqueeze(1)), (fc2_b[64:128, :], p["tok_fc2_b"].unsqueeze(1)),
                (fc3_b[:, :], p["tok_fc3_b"].unsqueeze(0).to_broadcast([64, 1]))]
            for g in range(4):
                r = slice(32 * g, 32 * g + 32)
                plain += [(g_all[r, 0, 0:1], p["tok_ln0_g"].unsqueeze(1)), (g_all[r, 1, 0:1], p["tok_ln0_b"].unsqueeze(1)),
                          (g_all[r, 0, 1:5], p["tok_ln_g"].rearrange("l c -> c l")),
                          (g_all[r, 1, 1:5], p["tok_ln_b"].rearrange("l c -> c l"))]
            placed = [(fc1_w[32 * g:32 * g + 32, g, :], p["tok_fc1_w"]) for g in range(4)]
            placed += [(bias_raw[0:32, :], p["tok_conv_b"].rearrange("l o -> o l"))]
            placed += [(fc3_w[64 * g:64 * g + 64, g:g + 1], p["tok_fc3_w"]) for g in range(2)]
            for dst, src in plain:
                sp.dma_start(dst, src, allow_slow_non_contiguous=True).then_inc(s["const_in"], 16)
            sp.wait_ge(s["const_zero"], 1)
            for dst, src in placed:
                sp.dma_start(dst, src, allow_slow_non_contiguous=True).then_inc(s["const_in"], 16)
            consts.append(16 * len(plain + placed))
            sp.wait_ge(s["fc0_copied"], 1)
            sp.dma_start(fc0_rows, fc0_c[:, :]).then_inc(s["fc0_stored"], 16)
            sp.wait_ge(s["fc0_stored"], 16)
            for wq in range(4):
                for w in range(4):
                    r, c = (wq * 4 + w) * 3, (w * 4 + wq) * 32
                    sp.dma_start(fc0_bd[r:r + 3, c:c + 32], fc0_rows[0:3, :]).then_inc(s["fc0_placed"], 16)
                    sp.dma_start(fc0_bd[48:49, c:c + 32], fc0_rows[3:4, :]).then_inc(s["fc0_placed"], 16)

            def load_x(n):
                then(sp, "x_ready", n)
                for ip in range(2):
                    sp.dma_start(x_in[:, ip, :], x[bass.ds(4 * n + 2 * ip, 2)].rearrange("i h w c -> (i h) (w c)")
                                 ).then_inc(s["x_loaded"], 16)

            def load_h(q, n, j):
                then(sp, "y_done", (n - 1) * UNITS + 4 * j + 4)
                sp.dma_start(h_in[j], hstore[bass.ds(q, 1), :, j, :].rearrange("a p n -> (a p) n")
                             ).then_inc(h_loaded[j], 16)

            def load_y(q, n):
                then(sp, "yc_done", n - QUADS)
                sp.dma_start(y_raw[:, :], ymodes[bass.ds(q, 1)].rearrange("a p n -> (a p) n")
                             ).then_inc(s["yraw_loaded"], 16)

            def store_h(q, n, j):
                then(sp, s["act_done"], n * UNITS + 4 * j + 4)
                sp.dma_start(hstore[bass.ds(q, 1), :, j, :].rearrange("a p n -> (a p) n"), h_new[j]
                             ).then_inc(h_stored[j], 16)

            def store_modes(q, n):
                then(sp, s["xout_done"], n + 1)
                sp.dma_start(xmodes[bass.ds(q, 1)].rearrange("a p n -> (a p) n"),
                             x_out[:, :, :, :].rearrange("p a k m -> p (a k m)")).then_inc(s["xmodes_stored"], 16)

            def store_tok(q, n):
                then(sp, s["tok_done"], (n - LAYERS * QUADS) * UNITS + 8)
                for g in range(2):
                    sp.dma_start(tok[bass.ds(4 * q, 4), 2 * g:2 * g + 2, :].rearrange("i r n -> r i n"),
                                 tok_sb[32 * g:32 * g + 2, :].rearrange("r (i n) -> r i n", i=4)
                                 ).then_inc(s["tok_stored"], 16)

            def body(kind, q, n, first, more, drain=False):
                if kind == "stem" and more:
                    load_x(n + 1)
                if kind != "stem" and more:
                    load_y(q + 1, n + 1)
                if not first and kind != "head":
                    store_h(q - 1, n - 1, 0)
                if kind != "stem" and not drain:
                    load_h(q, n, 1)
                    if more:
                        load_h(q + 1, n + 1, 0)
                if not first and kind != "head":
                    store_h(q - 1, n - 1, 1)
                if not first:
                    if kind == "head":
                        store_tok(q - 1, n - 1)
                    else:
                        store_modes(q - 1, n - 1)

            def mix(ph):
                then(sp, s["xmodes_stored"], 16 * QUADS * ph)
                for j in range(2):
                    then(sp, h_stored[j], 16 * QUADS * ph)
                for c in range(COMP):
                    sp.dma_start(modes[32 * c:32 * c + 32, :, :],
                                 xmodes.rearrange("q (i c) (a m) -> a c (q i) m", i=4, a=COMP)[c]
                                 ).then_inc(s["modes_loaded"], 16)
                then(sp, s["mix_act"], 21 * ph)
                then(sp, s["mix_dve"], 19 * ph)
                for c in range(COMP):
                    sp.dma_start(ymodes.rearrange("q (i c) (a m) -> a c (q i) m", i=4, a=COMP)[c],
                                 modes[32 * c:32 * c + 32, :, :]).then_inc(s["ymodes_stored"], 16)
                then(sp, s["ymodes_stored"], 16 * COMP * ph)
                load_y(0, ph * QUADS)
                load_h(0, ph * QUADS, 0)

            load_x(0)
            run_phase(sp, 0, "stem", body)
            with sp.Fori(1, LAYERS) as ph:
                mix(ph)
                run_phase(sp, ph * QUADS, "layer", body)
            mix(LAYERS)
            attention_load(sp)
            run_phase(sp, LAYERS * QUADS, "head", body)
            sp.wait_ge(s["tok_stored"], 32 * QUADS)
            attention_sync(sp)

        @block.gpsimd
        def _(pool):
            for which in primed:
                pool.sem_inc(which, 1)
            for t in (fc1_w, fc3_w, fc0_bd, bias_raw, conv_bd, y_kk):
                nc.gpsimd.memset(t[:], 0.0)
            nc.gpsimd.memset(x_tr[:], 1.0).then_inc(s["const_zero"], 1)

            def weights(l):
                r = 0
                for slots, parts in (((0, 3), "riir"), ((1, 2), "irri")):
                    for oc in range(CH // OCH):
                        o0, rnd = oc * OCH, l * ROUNDS + r
                        for c, part in enumerate(parts):
                            rows = slice(32 * c, 32 * c + 32)
                            for dst, src in ((w1_raw, p[f"tok_w1{part}"]), (w2_raw, p[f"tok_w2{part}"])):
                                pool.dma_start(dst[rows, :, :].rearrange("p o m -> p (o m)"),
                                               src[bass.ds(l, 1), :, o0:o0 + OCH].rearrange("l i o k m -> (l i) (o k m)")
                                               ).then_inc(s["w_raw"], 16)
                        then(pool, s["w_raw"], 128 * rnd + 128)
                        for i, sl in enumerate(slots):
                            dst = wslot[:, sl, o0:o0 + OCH, :]
                            nc.gpsimd.memset(dst[:, :, M * M:MODES], 0.0)
                            nc.gpsimd.tensor_scalar(dst[:, :, 0:M * M], w1_raw[:, :, :], c_sign[:, sl:sl + 1], None, ALU.mult)
                            nc.gpsimd.tensor_scalar(w2_sg[:, :, :], w2_raw[:, :, :], c_sign[:, 4 + sl:5 + sl], None,
                                                    ALU.mult).then_inc(s["w_step"], 1)
                            then(pool, s["w_step"], 4 * rnd + 2 * i + 1)
                            view = dst[:, :, M:MODES].rearrange("p o (k m) -> p o k m", m=M)
                            rev = w2_sg[:, :, :].rearrange("p o (k m) -> p o k m", m=M)[:, :, ::-1, :]
                            nc.gpsimd.tensor_tensor(view, view, rev, ALU.add).then_inc(s["w_step"], 1)
                            then(pool, s["w_step"], 4 * rnd + 2 * i + 2)
                        r += 1

            pool.wait_ge(s["const_in"], consts[0])
            with pool.Fori(0, LAYERS) as l:
                then(pool, s["mix_done"], l * GROUPS)
                weights(l)
            attention_pool(pool)

        @block.tensor
        def _(pe):
            mm = nc.tensor.matmul
            pe.wait_ge(s["const_in"], consts[0])
            pe.wait_ge(s["const_zero"], 1)
            mm(ps_t1[0:4, 0:32], fc0_t[:, :], c_center[0:32, 0:32], start=True, stop=True).then_inc(s["fc0_center"], 1)
            for g in range(4):
                for l in range(LAYERS):
                    last = mm(ps_t2[32 * g:32 * g + 32, 32 * l:32 * l + 32], conv_w[:, l, :], c_center[0:32, 0:32],
                              start=True, stop=True)
            last.then_inc(s["conv_center"], 1)
            pe.wait_ge(s["fc0_placed"], 16 * 32)
            pe.wait_ge(s["conv_placed"], 1)

            def turn_x(n, k):
                g, ip = k // 2, k % 2
                if k == 0:
                    pe.wait_ge(s["x_ready"], n + 1)
                if k == 1:
                    wait(pe, "fw_read", n - 1)
                wait(pe, "x_copied", n * UNITS + k)
                mm(ps_s[0:48, 0, 0:128], x_cur[:, ip, 48 * g:48 * g + 48], ident[:, :], start=True, stop=True).then_inc(s["x_turned"], 1)

            def center(n):
                i = n - QUADS
                wait(pe, "yraw_loaded", 16 * i + 16)
                wait(pe, "iw_read", 2 * i)
                for sx in range(2):
                    last = mm(ps_s[:, sx, 0:312], c_center[:, :], y_raw[:, 312 * sx:312 * sx + 312], start=True, stop=True)
                last.then_inc(s["yc_done"], 1)

            def inv_w(n, j, forward):
                i = n - QUADS
                wait(pe, "ykt_done", i + 1)
                if j == 1:
                    wait(pe, "iw_read", 2 * i + 1)
                    if forward:
                        wait(pe, "fw_read", n - 1)
                for sx in range(2):
                    last = mm(ps_s[:, sx, :], c_inw[:, j, :], y_kt[:, 512 * sx:512 * sx + 512], start=True, stop=True)
                last.then_inc(s["iw_done"], 1)

            def start_layer(n):
                wait(pe, "fw_read", n)
                center(n)
                inv_w(n, 0, False)

            def body(kind, q, n, first, more, drain=False):
                for k in range(UNITS):
                    u = n * UNITS + k
                    j, g, ip = k // 4, k // 2, k % 2
                    if not drain:
                        if kind != "stem" and k == 0:
                            inv_w(n, 1, kind == "layer")
                        if kind == "stem":
                            if k < 7:
                                turn_x(n, k + 1)
                            elif more:
                                turn_x(n + 1, 0)
                            pe.wait_ge(s["x_copied"], u + 1)
                            wait(pe, "y_read", u - 1)
                            mm(ps_y[k % 2][:, :], x_tr[0:49, k % 2, :], fc0_bd[0:49, :],
                               start=True, stop=True).then_inc(s["y_done"], 1)
                        else:
                            if k % 4 == 0:
                                wait(pe, "iw_read", 2 * (n - QUADS) + j + 1)
                                wait(pe, h_loaded[j], 16 * (n - QUADS) + 16)
                            wait(pe, "y_read", u - 1)
                            mm(ps_y[k % 2][:, :], c_inh[:, ip, :], z_kx[:, j, 512 * (g % 2):512 * (g % 2) + 512],
                               start=True, stop=False)
                            for w in range(4):
                                at = ((g % 2) * 4 + w) * 256 + ip * 128
                                last = mm(ps_y[k % 2][:, 128 * w:128 * w + 128], h_in[j][:, at:at + 128], conv_now[:, :],
                                          start=False, stop=(w == 3))
                            last.then_inc(s["y_done"], 1)
                            if more and k == 4:
                                center(n + 1)
                            if more and k == 5:
                                inv_w(n + 1, 0, False)
                    if there(k, LAG_T1, first, drain):
                        v = u - LAG_T1
                        pe.wait_ge(s["xhat_done"], v + 1)
                        wait(pe, "act_done", v)
                        if kind == "head":
                            wait(pe, "tok_done", v - 1 - UNITS * QUADS * LAYERS)
                        for w in range(4):
                            last = nc.tensor.transpose(ps_t1[:, 128 * w:128 * w + 128],
                                                       xhat[(k - LAG_T1) % 2][:, 128 * w:128 * w + 128], ident[:, :])
                        last.then_inc(s["t1_done"], 1)
                    if kind == "head":
                        if there(k, LAG_T2, first, drain):
                            head_unit(u, k, drain)
                        continue
                    if there(k, LAG_T2, first, drain):
                        v, kk = u - LAG_T2, (k - LAG_T2) % 8
                        pe.wait_ge(s["act_done"], v + 1)
                        wait(pe, "px_done", v)
                        for w in range(4):
                            at = (((kk // 2) % 2) * 4 + w) * 256 + (kk % 2) * 128
                            last = nc.tensor.transpose(ps_t2[:, 128 * w:128 * w + 128], h_new[kk // 4][:, at:at + 128],
                                                       ident[:, :])
                        last.then_inc(s["t2_done"], 1)
                    if there(k, LAG_F, first, drain):
                        v, kk = u - LAG_F, (k - LAG_F) % 8
                        pe.wait_ge(s["px_done"], v + 1)
                        if kk % 4 == 0:
                            wait(pe, "tw_done", 2 * n if kk == 0 else 2 * n - 1)
                        mm(ps_f[64 * (kk % 2):64 * (kk % 2) + 64, (kk // 2) % 2, :], c_fwh[:, :], h_px[kk % 2],
                           start=True, stop=True).then_inc(s["f_done"], 1)
                    if k == 7 and not first:
                        fwd_w(kind, n, u, more, drain)

            def fwd_w(kind, n, u, more, drain):
                pe.wait_ge(s["tw_done"], 2 * n)
                if kind == "stem":
                    pe.wait_ge(s["x_copied"], u + 2 if more else (UNITS * QUADS if drain else u + 1))
                else:
                    wait(pe, "iw_read", 2 * (n - QUADS) + (3 if more else (0 if drain else 2)))
                wait(pe, "fw_read", n - 1)
                for sx in range(2):
                    for j in range(2):
                        last = mm(ps_s[:, sx, 0:KX * 32], c_fww[:, j, :], t_w[:, j, 512 * sx:512 * sx + KX * 32],
                                  start=(j == 0), stop=(j == 1))
                last.then_inc(s["fw_done"], 1)

            def fc1(v, vb, wq):
                wait(pe, "g1_done", 4 * v + wq - 1)
                dst = ps_f[:, 0, :] if wq % 2 else ps_t2[:, :]
                mm(dst, fc1_w[:, wq, :], h_px[vb], start=True, stop=True).then_inc(s["fc1_done"], 1)

            def fc2(v, wq):
                pe.wait_ge(s["g1_done"], 4 * v + wq + 1)
                if wq % 2 == 0:
                    wait(pe, "g2_done", 2 * v + wq // 2)
                mm(ps_f[64 * (wq % 2):64 * (wq % 2) + 64, 1, :], fc2_w[:, :], gelu1[wq % 2],
                   start=True, stop=True).then_inc(s["fc2_done"], 1)

            def fc3(v, pr):
                pe.wait_ge(s["g2_done"], 2 * v + pr + 1)
                mm(ps_t1[32 * pr:32 * pr + 32, :], fc3_w[:, :], gelu2[pr], start=True, stop=True).then_inc(s["fc3_done"], 1)

            def head_unit(u, k, drain):
                v, vb = u - LAG_T2 - UNITS * QUADS * LAYERS, (k - LAG_T2) % 2
                pe.wait_ge(s["act_done"], u - LAG_T2 + 1)
                fc1(v, vb, 0)
                fc1(v, vb, 1)
                fc2(v, 0)
                fc1(v, vb, 2)
                fc2(v, 1)
                fc1(v, vb, 3)
                fc2(v, 2)
                pe.wait_ge(s["act_done"], u - LAG_T1 + (0 if drain and k >= LAG_T1 else 1))
                wait(pe, "tok_done", v)
                fc3(v, 0)
                fc2(v, 3)
                fc3(v, 1)

            def mix(ph):
                pe.wait_ge(s["modes_loaded"], 16 * COMP * ph)
                pe.wait_ge(s["w_step"], 4 * ROUNDS * ph)
                pe.wait_ge(s["px_done"], UNITS * QUADS * ph)
                for t in range(GROUPS):
                    if t >= 4:
                        if t % 2 == 0:
                            pe.wait_ge(s["mix_act"], (ph - 1) * 21 + t // 2)
                        else:
                            pe.wait_ge(s["mix_dve"], (ph - 1) * 19 + t // 2 - 1)
                    for m in range(4):
                        last = mm(ps[t % 4][:, 128 * m:128 * m + 128], wslot[:, :, :, 4 * t + m], modes[:, :, 4 * t + m],
                                  start=True, stop=True)
                    last.then_inc(s["mix_done"], 1)

            turn_x(0, 0)
            run_phase(pe, 0, "stem", body)
            with pe.Fori(1, LAYERS) as ph:
                mix(ph)
                start_layer(ph * QUADS)
                run_phase(pe, ph * QUADS, "layer", body)
            mix(LAYERS)
            start_layer(LAYERS * QUADS)
            run_phase(pe, LAYERS * QUADS, "head", body)
            attention_tensor(pe)

        @block.scalar
        def _(act):
            af = nc.scalar.activation
            act.wait_ge(s["const_in"], consts[0])

            def take_x(n):
                act.wait_ge(s["x_loaded"], 32 * n + 32)
                wait(act, "x_turned", UNITS * n)
                for ip in range(2):
                    last = af(x_cur[:, ip, :].rearrange("p (g q w) -> p q g w", g=4, q=4),
                              x_in[:, ip, :].rearrange("p (q g w) -> p q g w", g=4, q=4), ACT.Copy)
                last.then_inc(s["x_ready"], 1)

            def order_y(n):
                i = n - QUADS
                wait(act, "yc_done", i + 1)
                wait(act, "ykt_done", i)
                for sx in range(2):
                    dst = y_kk[:, 512 * sx:512 * sx + 512].rearrange("p (k r) -> p k r", r=32)[:, 0:KX, 0:2 * M]
                    last = af(dst.rearrange("p k (a m) -> p a k m", a=2),
                              ps_s[:, sx, 0:312].rearrange("p (a k m) -> p a k m", a=2, k=KX), ACT.Copy)
                last.then_inc(s["ykk_done"], 1)

            def body(kind, q, n, first, more, drain=False):
                for k in range(UNITS):
                    u = n * UNITS + k
                    if kind == "stem" and k == 7 and more:
                        take_x(n + 1)
                    if not drain:
                        act.wait_ge(s["y_done"], u + 1)
                        wait(act, "ss_done", u - 1)
                        af(y_sq[k % 2], ps_y[k % 2][:, :], ACT.Square).then_inc(s["sq_done"], 1)
                        wait(act, "xhat_done", u - 7)
                        af(y_sb[k], ps_y[k % 2][:, :], ACT.Copy).then_inc(s["y_read"], 1)
                    if there(k, LAG_T1, first, drain):
                        v, kk = u - LAG_T1, (k - LAG_T1) % 8
                        act.wait_ge(s["t1_done"], v + 1)
                        if kind == "head":
                            wait(act, "fc1_done", 4 * (v - 1 - UNITS * QUADS * LAYERS))
                            af(h_px[kk % 2], ps_t1[:, :], ACT.Identity, bias=g_now[:, 1:2], scale=g_now[:, 0:1]
                               ).then_inc(s["act_done"], 1)
                        else:
                            if kk % 4 == 0:
                                wait(act, h_stored[kk // 4], 16 * (n if k >= LAG_T1 else n - 1))
                            dst = h_new[kk // 4].rearrange("p (w q) -> p w q", w=8)[:, 4 * ((kk // 2) % 2):4 * ((kk // 2) % 2) + 4,
                                                                                    128 * (kk % 2):128 * (kk % 2) + 128]
                            af(dst, ps_t1[:, :].rearrange("p (w q) -> p w q", w=4), ACT.Identity if kind == "stem" else ACT.Gelu,
                               bias=g_now[:, 1:2], scale=g_now[:, 0:1]).then_inc(s["act_done"], 1)
                    if kind == "head":
                        if there(k, LAG_T2, first, drain):
                            head_unit(u, k)
                        if more and k == 4:
                            order_y(n + 1)
                        continue
                    if there(k, LAG_T2, first, drain):
                        v = u - LAG_T2
                        act.wait_ge(s["t2_done"], v + 1)
                        wait(act, "f_done", v - 1)
                        af(h_px[(k - LAG_T2) % 2], ps_t2[:, :], ACT.Copy).then_inc(s["px_done"], 1)
                    if kind == "layer" and more and k == 4:
                        order_y(n + 1)
                    if k == 7 and not first:
                        wait(act, "fw_read", n)
                        wait(act, "xmodes_stored", 16 * (n - 1))
                        for sx in range(2):
                            src = fw_sb[:, 416 * sx:416 * sx + 416].rearrange("p (k r) -> p k r", r=32)[:, :, 0:2 * M]
                            last = af(x_out[:, 2 * sx:2 * sx + 2, :, :], src.rearrange("p k (a m) -> p a k m", a=2), ACT.Copy)
                        last.then_inc(s["xout_done"], 1)

            def head_unit(u, k):
                v = u - LAG_T2 - UNITS * QUADS * LAYERS

                def g1(wq):
                    act.wait_ge(s["fc1_done"], 4 * v + wq + 1)
                    wait(act, "fc2_done", 4 * v + wq - 1)
                    src = ps_f[:, 0, :] if wq % 2 else ps_t2[:, :]
                    af(gelu1[wq % 2], src, ACT.Gelu, bias=fc1_b[:, :]).then_inc(s["g1_done"], 1)

                def g2(pr):
                    act.wait_ge(s["fc2_done"], 4 * v + 2 * pr + 2)
                    wait(act, "fc3_done", 2 * v + pr - 1)
                    af(gelu2[pr], ps_f[:, 1, :], ACT.Gelu, bias=fc2_b[:, :]).then_inc(s["g2_done"], 1)

                g1(0)
                g1(1)
                g1(2)
                g2(0)
                g1(3)
                g2(1)

            def mix(ph):
                act.wait_ge(s["now_done"], ph)
                base = (ph - 1) * GROUPS
                for t in range(0, GROUPS, 2):
                    wait(act, "mix_done", base + t + 1)
                    src = ps[t % 4][:, :].rearrange("p (m i) -> p i m", m=4)
                    if t == 0:
                        af(modes[:, :, 0:1], src[:, :, 0:1], ACT.Identity, bias=bias_now[:, :]).then_inc(s["mix_act"], 1)
                        af(modes[:, :, 1:4], src[:, :, 1:4], ACT.Copy).then_inc(s["mix_act"], 1)
                    else:
                        af(modes[:, :, 4 * t:4 * t + 4], src, ACT.Copy).then_inc(s["mix_act"], 1)

            take_x(0)
            run_phase(act, 0, "stem", body)
            with act.Fori(1, LAYERS) as ph:
                mix(ph)
                act.wait_ge(s["ymodes_stored"], 16 * COMP * ph)
                order_y(ph * QUADS)
                run_phase(act, ph * QUADS, "layer", body)
            mix(LAYERS)
            act.wait_ge(s["ymodes_stored"], 16 * COMP * LAYERS)
            order_y(LAYERS * QUADS)
            run_phase(act, LAYERS * QUADS, "head", body)
            attention_scalar(act)

        @block.vector
        def _(dve):
            v_ = nc.vector
            dve.wait_ge(s["const_in"], consts[0])
            dve.wait_ge(s["fc0_center"], 1)
            v_.tensor_copy(fc0_c[:, :], ps_t1[0:4, 0:32]).then_inc(s["fc0_copied"], 1)
            dve.wait_ge(s["conv_center"], 1)
            dve.wait_ge(s["const_zero"], 1)
            v_.tensor_copy(g_now[:, :], g_all[:, :, 0])
            for g in range(4):
                r = slice(32 * g, 32 * g + 32)
                last = v_.tensor_copy(conv_bd[r, :, 32 * g:32 * g + 32], ps_t2[r, 0:128].rearrange("p (l o) -> p l o", l=LAYERS))
            last.then_inc(s["conv_placed"], 1)

            def copy_x(n, k):
                u = n * UNITS + k
                dve.wait_ge(s["x_turned"], u + 1)
                wait(dve, "y_done", u - 1)
                v_.tensor_copy(x_tr[0:48, k % 2, :], ps_s[0:48, 0, 0:128]).then_inc(s["x_copied"], 1)

            def turn_y(n):
                i = n - QUADS
                wait(dve, "ykk_done", i + 1)
                wait(dve, "iw_done", 2 * i)
                v_.transpose(y_kt[:, :], y_kk[:, :]).then_inc(s["ykt_done"], 1)

            def turn_z(n, j):
                i = n - QUADS
                wait(dve, "iw_done", 2 * i + j + 1)
                wait(dve, "y_done", (n - 1) * UNITS + 4 * j + 4)
                v_.transpose(z_kx[:, j, :].rearrange("p (w o) -> p o w", o=32),
                             ps_s[:, :, :].rearrange("p a n -> p (a n)").rearrange("p (k o) -> p o k", o=32)
                             ).then_inc(s["iw_read"], 1)

            def turn_w(n, j):
                dve.wait_ge(s["f_done"], n * UNITS + 4 * j + 4)
                wait(dve, "fw_done", n)
                v_.transpose(t_w[:, j, :].rearrange("p (k c) -> p c k", c=32),
                             ps_f[:, :, :].rearrange("p a n -> p (a n)").rearrange("p (w c) -> p c w", c=32)
                             ).then_inc(s["tw_done"], 1)

            def body(kind, q, n, first, more, drain=False):
                for k in range(UNITS):
                    u, j = n * UNITS + k, k // 4
                    if kind != "stem" and not drain and k == 0:
                        turn_z(n, 1)
                    if kind == "stem" and not drain:
                        if k < 7:
                            copy_x(n, k + 1)
                        elif more:
                            copy_x(n + 1, 0)
                    if kind != "head" and not first and k in (3, 7):
                        turn_w(n - 1, k // 4)
                    if there(k, LAG_XH, first, drain):
                        v, kk = u - LAG_XH, (k - LAG_XH) % 8
                        dve.wait_ge(s["y_read"], v + 1)
                        dve.wait_ge(s["norm_step"], 12 * (2 * n + (1 if k >= LAG_XH else 0)))
                        wait(dve, "t1_done", v - 1)
                        v_.tensor_tensor(xhat[kk % 2].rearrange("p (a c) -> p a c", c=32),
                                         y_sb[kk].rearrange("p (a c) -> p a c", c=32),
                                         rstd[:, kk // 4, 16 * (kk % 4):16 * (kk % 4) + 16].unsqueeze(2).to_broadcast([128, 16, 32]),
                                         ALU.mult).then_inc(s["xhat_done"], 1)
                    if not drain:
                        dve.wait_ge(s["sq_done"], u + 1)
                        v_.tensor_reduce(ss[:, j, 16 * (k % 4):16 * (k % 4) + 16], y_sq[k % 2].rearrange("p (a c) -> p a c", c=32),
                                         AX.X, ALU.add).then_inc(s["ss_done"], 1)
                        if k % 4 == 3:
                            rsqrt_half(n, k)
                        if kind != "stem" and more and k == 4:
                            turn_y(n + 1)
                        if kind != "stem" and more and k == 5:
                            turn_z(n + 1, 0)
                    if kind == "head" and there(k, LAG_T2, first, drain):
                        v, kk = u - LAG_T2 - UNITS * QUADS * LAYERS, (k - LAG_T2) % 8
                        dve.wait_ge(s["fc3_done"], 2 * v + 2)
                        if kk == 0:
                            wait(dve, "tok_stored", 32 * ((n if k >= LAG_T2 else n - 1) - QUADS * LAYERS))
                        dst = tok_sb[:, :].rearrange("p (q i w h) -> p q w i h", q=2, i=2, w=16)[
                            :, kk % 2, 4 * (kk // 2):4 * (kk // 2) + 4, :, :]
                        v_.tensor_scalar(dst, ps_t1[0:64, :].rearrange("p (w i h) -> p w i h", w=4, i=2), fc3_b[:, :], None,
                                         ALU.add).then_inc(s["tok_done"], 1)
                    if kind != "head" and k == 7 and not first:
                        dve.wait_ge(s["fw_done"], n)
                        wait(dve, "xout_done", n - 1)
                        v_.transpose(fw_sb[:, :], ps_s[:, :, 0:KX * 32]).then_inc(s["fw_read"], 1)

            def rsqrt_half(n, k):
                j = k // 4
                at = 12 * (2 * n + j)
                dve.wait_ge(s["ss_done"], n * UNITS + k + 1)
                v_.tensor_scalar(var[:, :], ss[:, j, :], 1.0 / CH, EPS, ALU.mult, ALU.add).then_inc(s["norm_step"], 1)
                newton(dve, s["norm_step"], at + 1, rstd[:, j, :], nt[:, :], var[:, :])

            def newton(eng, step, at, r, t, v):
                eng.wait_ge(step, at)
                v_.tensor_scalar(t.bitcast(i32), v.bitcast(i32), 1, None, ALU.logical_shift_right).then_inc(step, 1)
                eng.wait_ge(step, at + 1)
                v_.tensor_scalar(r.bitcast(i32), t.bitcast(i32), -1, 0x5F3759DF, ALU.mult, ALU.add).then_inc(step, 1)
                for i in range(3):
                    eng.wait_ge(step, at + 2 + 3 * i)
                    v_.tensor_tensor(t, r, r, ALU.mult).then_inc(step, 1)
                    eng.wait_ge(step, at + 3 + 3 * i)
                    v_.scalar_tensor_tensor(t, t, -0.5, v, ALU.mult, ALU.mult).then_inc(step, 1)
                    eng.wait_ge(step, at + 4 + 3 * i)
                    v_.scalar_tensor_tensor(r, t, 1.5, r, ALU.add, ALU.mult).then_inc(step, 1)

            def mix(ph):
                dve.wait_ge(s["y_done"], UNITS * QUADS * ph)
                dve.wait_ge(s["act_done"], UNITS * QUADS * ph)
                v_.tensor_copy(conv_now[:, :], conv_bd[:, bass.ds(ph - 1, 1), :].rearrange("p l o -> p (l o)"))
                v_.tensor_copy(g_now[:, :], g_all[:, :, bass.ds(ph, 1)].rearrange("p a l -> p (a l)"))
                v_.tensor_scalar(bias_now[:, :], bias_raw[:, bass.ds(ph - 1, 1)], float(HH * WW), None,
                                 ALU.mult).then_inc(s["now_done"], 1)
                base = (ph - 1) * GROUPS
                for t in range(1, GROUPS, 2):
                    wait(dve, "mix_done", base + t + 1)
                    v_.tensor_copy(modes[:, :, 4 * t:4 * t + 4], ps[t % 4][:, :].rearrange("p (m i) -> p i m", m=4)
                                   ).then_inc(s["mix_dve"], 1)

            def start_layer(ph):
                dve.wait_ge(s["ymodes_stored"], 16 * COMP * ph)
                turn_y(ph * QUADS)
                turn_z(ph * QUADS, 0)

            copy_x(0, 0)
            run_phase(dve, 0, "stem", body)
            with dve.Fori(1, LAYERS) as ph:
                mix(ph)
                start_layer(ph)
                run_phase(dve, ph * QUADS, "layer", body)
            mix(LAYERS)
            start_layer(LAYERS)
            run_phase(dve, LAYERS * QUADS, "head", body)
            attention_vector(dve, newton)


def transform_tables():
    import numpy as np
    k, ky, h = np.arange(KX), np.arange(M), np.arange(HH)
    ch, sh = np.cos(2 * np.pi * np.outer(h, k) / HH), np.sin(2 * np.pi * np.outer(h, k) / HH)
    fwd_h, inv_h = np.zeros((2, HH, 2, 32)), np.zeros((4, 32, 2, 2, HH))
    for i in range(2):
        fwd_h[i, :, i, 0:KX], fwd_h[i, :, i, 16:16 + KX] = ch, sh
    for i in range(4):
        inv_h[i, 0:KX, i // 2, i % 2, :], inv_h[i, 16:16 + KX, i // 2, i % 2, :] = ch.T, sh.T
    fwd_w, inv_w = np.zeros((4, 32, 2, 4, 32)), np.zeros((4, 32, 2, 4, 32))
    scale = np.where(ky == 0, 1.0, 2.0) / (HH * WW)
    for j in range(2):
        r = np.arange(32)
        w = 16 * (r % 4) + 8 * j + r // 4
        cw, sw = np.cos(2 * np.pi * np.outer(w, ky) / WW), np.sin(2 * np.pi * np.outer(w, ky) / WW)
        for i in range(4):
            fwd_w[i, :, j, i, 0:M], fwd_w[i, :, j, i, M:2 * M] = cw, sw
            inv_w[i, 0:M, j, i, :], inv_w[i, M:2 * M, j, i, :] = (cw * scale).T, (sw * scale).T
    center = np.zeros((4, 32, 4, 32))
    for i in range(4):
        center[i, :, i, :] = np.eye(32) - 1.0 / 32
    s1 = np.array([[1, -1, -1, -1], [1, 1, 1, -1], [1, 1, 1, -1], [-1, 1, 1, 1]])
    s2 = np.array([[1, -1, 1, 1], [1, 1, -1, 1], [-1, -1, 1, -1], [1, -1, 1, 1]])
    sign = np.repeat(np.concatenate([s1, s2], 1), 32, 0)
    pick = np.repeat(np.eye(E)[:, :, None], 128, 2)
    lower = np.repeat(np.tril(np.ones((E, E)), -1).reshape(1, -1), 128, 0)
    tables = {"ident": np.eye(128), "center": center, "fwd_h": fwd_h, "fwd_w": fwd_w, "inv_w": inv_w, "inv_h": inv_h,
              "sign": sign, "pick": pick, "lower": lower}
    shapes = {"center": (128, 128), "fwd_h": (128, 64), "fwd_w": (128, 2, 128), "inv_w": (128, 2, 128), "inv_h": (128, 2, 128),
              "pick": (E, E * 128)}
    return {n: np.ascontiguousarray(t.reshape(shapes.get(n, t.shape)), dtype=np.float32) for n, t in tables.items()}


_PARAMS = ["tok_fc0_w", "tok_fc0_b", "tok_ln0_g", "tok_ln0_b", "tok_w1r", "tok_w1i", "tok_w2r", "tok_w2i", "tok_conv_w",
           "tok_conv_b", "tok_ln_g", "tok_ln_b", "tok_fc1_w", "tok_fc1_b", "tok_fc2_w", "tok_fc2_b", "tok_fc3_w", "tok_fc3_b",
           "attn_Wq", "attn_bq", "attn_Wk", "attn_bk", "attn_Wv", "attn_bv", "attn_Wo", "attn_bo",
           "ffn_gamma", "ffn_beta", "ffn_Wr", "ffn_br", "ffn_W1", "ffn_b1", "ffn_W2", "ffn_b2"]


def kernel(**inputs):
    import numpy as _np
    import concourse.bacc as _bacc
    from concourse import mybir as _mybir
    from concourse.bass_utils import run_bass_kernel_spmd as _run

    nc = _bacc.Bacc("TRN2", target_bir_lowering=False, num_devices=1)
    f32 = _mybir.dt.float32
    arrays = {"x_dram": _np.ascontiguousarray(inputs["x"])}
    x = nc.dram_tensor("x_dram", arrays["x_dram"].shape, f32, kind="ExternalInput").ap()
    p, cst = {}, {}
    for name in _PARAMS:
        arr = _np.ascontiguousarray(inputs[f"L0_{name}"])
        arrays[f"in_{name}"] = arr
        p[name] = nc.dram_tensor(f"in_{name}", arr.shape, f32, kind="ExternalInput").ap()
    for name, arr in transform_tables().items():
        arrays[f"table_{name}"] = arr
        cst[name] = nc.dram_tensor(f"table_{name}", arr.shape, f32, kind="ExternalInput").ap()
    out = nc.dram_tensor("out_dram", (B, HH, WW), f32, kind="ExternalOutput").ap()
    scratch = [nc.dram_tensor(n, shape, f32, kind="Internal").ap() for n, shape in (
        ("xmodes", (QUADS, 128, COMP * MODES)), ("ymodes", (QUADS, 128, COMP * MODES)), ("hstore", (QUADS, 128, 2, 2048)),
        ("tok", (B, 4, 16 * HH)), ("fc0_rows", (4, 32)))]
    vit_tower(nc, x, p, cst, out, scratch)
    r = _run(nc, [arrays], core_ids=[0])
    return r.results[0]["out_dram"]
```

```python
import concourse.bass as bass
from concourse import mybir
from contextlib import ExitStack

B, HH, WW, CH, LAYERS, M = 128, 64, 64, 32, 4, 12
QUADS = B // 4
UNITS = 8
KX = M + 1
MODES = KX * M
COMP = 4
EPS = 1e-5
F1, F2 = 128, 64
LAG_XH, LAG_T1, LAG_T2, LAG_F = 4, 5, 6, 7
OCH = 8
ROUNDS = 2 * (CH // OCH)
GROUPS = MODES // 4
D, E, H = 64, 8, 128
PAIRS = 8
STEPS = B // 2 // PAIRS


def vit_tower(nc, x, p, cst, out, scratch):
    f32, i32, f32r = mybir.dt.float32, mybir.dt.int32, mybir.dt.float32r
    ALU, ACT, AX = mybir.AluOpType, mybir.ActivationFunctionType, mybir.AxisListType
    xmodes, ymodes, hstore, tok, fc0_rows = scratch

    ctx = ExitStack()
    with ctx:
        def sb(name, shape, dt=f32):
            return ctx.enter_context(nc.sbuf_tensor(name, shape, dt))

        def sem(name):
            return ctx.enter_context(nc.semaphore(name))

        wslot = sb("wslot", [128, COMP, CH, MODES])
        big = sb("big", [128, B * MODES])
        modes = big[:, :].rearrange("p (i m) -> p i m", m=MODES)
        taken = [0]

        def carve(n):
            at = taken[0]
            taken[0] += n
            assert taken[0] <= B * MODES
            return big[:, at:at + n]

        h_in = [carve(2048) for _ in range(2)]
        h_new = [carve(2048) for _ in range(2)]
        y_sb = [carve(512) for _ in range(8)]
        y_sq = [carve(512) for _ in range(2)]
        xhat = [carve(512) for _ in range(2)]
        h_px = [carve(512) for _ in range(4)]
        ss, rstd = (carve(128).rearrange("p (j n) -> p j n", j=2) for _ in range(2))
        var, nt = carve(64), carve(64)
        z_kx = carve(1024)
        t_w = carve(2048).rearrange("p (j n) -> p j n", j=2)
        fw_sb = sb("fw_sb", [128, 832])
        tok_sb = big[0:64, 4096:8192]
        gelu1 = [t_w[:, i // 2, 512 * (i % 2):512 * (i % 2) + 512] for i in range(4)]
        spare = wslot[:, :, :, :].rearrange("p a o m -> p (a o m)")[:, 3 * CH * MODES:]
        gelu2 = [spare[:, 512 * i:512 * i + 512] for i in range(4)]
        y_raw = sb("y_raw", [128, COMP * MODES])
        y_kk = sb("y_kk", [128, 1024])
        y_kt = sb("y_kt", [128, 1024])
        x_out = sb("x_out", [128, COMP, KX, M])
        z_hl = sb("z_hl", [128, 2, 2, 1024], f32r)
        x_in = h_in[0][:, 0:2 * WW * 3].rearrange("p (i w) -> p i w", i=2)
        x_cur = h_in[0][:, 384:384 + 2 * WW * 3].rearrange("p (i w) -> p i w", i=2)
        x_tr = h_in[0][0:64, 768:1024].rearrange("p (i w) -> p i w", i=2)
        fc0_bd = h_in[0][0:64, 1024:1536]
        c_inh = h_in[0][:, 1536:1664]
        w1_raw = sb("w1_raw", [128, OCH, M * M])
        w2_raw = sb("w2_raw", [128, OCH, M * M])

        ident = sb("ident", [128, 128])
        c_center = sb("c_center", [128, 128])
        c_fwh = sb("c_fwh", [128, 64])
        c_fww = sb("c_fww", [128, 2, 128])
        c_inw = sb("c_inw", [128, 2, 128])
        c_inh_hl = sb("c_inh_hl", [128, 2, 128], f32r)
        c_sign = sb("c_sign", [128, 8])
        fc0_t = sb("fc0_t", [32, 4])
        fc0_c = sb("fc0_c", [4, 32])
        conv_w = sb("conv_w", [32, LAYERS, 32])
        conv_bd = sb("conv_bd", [128, LAYERS, 128])
        conv_now = sb("conv_now", [128, 128])
        bias_raw = sb("bias_raw", [128, LAYERS])
        bias_now = sb("bias_now", [128, 1])
        g_all = sb("g_all", [128, 2, 5])
        g_now = sb("g_now", [128, 2])
        fc1_w = sb("fc1_w", [128, 4, F1])
        fc1_b = sb("fc1_b", [128, 1])
        fc2_w = sb("fc2_w", [128, F2])
        fc2_b = sb("fc2_b", [128, 1])
        fc3_w = sb("fc3_w", [128, 32])
        fc3_b = sb("fc3_b", [64, 1])

        ps = [ctx.enter_context(nc.psum_tensor(f"bank{i}", [128, 512], f32)) for i in range(4)]
        ps_y, ps_t1, ps_t2 = [ps[0], ps[1]], ps[2], ps[3]
        ps_s = ctx.enter_context(nc.psum_tensor("ps_s", [128, 2, 512], f32))
        ps_f = ctx.enter_context(nc.psum_tensor("ps_f", [128, 2, 512], f32))

        s = {n: sem(n) for n in (
            "const_in", "const_zero", "fc0_center", "fc0_copied", "fc0_stored", "fc0_placed", "conv_center", "conv_placed",
            "x_loaded", "x_ready", "x_turned", "x_copied",
            "h_loaded0", "h_loaded1", "h_stored0", "h_stored1", "yraw_loaded", "xmodes_stored",
            "y_done", "sq_done", "y_read", "ss_done", "norm_step", "xhat_done", "t1_done", "act_done", "t2_done",
            "px_done", "f_done", "tw_done", "fw_done", "fw_read", "xout_done",
            "yc_done", "ykk_done", "ykt_done", "iw_done", "iw_read",
            "now_done", "modes_loaded", "mix_done", "mix_act", "mix_dve", "ymodes_stored",
            "w_raw", "w_step",
            "z_high", "z_done", "table_split", "fc1_done", "g1_done", "fc2_done", "g2_done", "fc3_done", "tok_done", "tok_stored0",
            "tok_stored1")}
        h_loaded = [s["h_loaded0"], s["h_loaded1"]]
        h_stored = [s["h_stored0"], s["h_stored1"]]
        tok_stored = [s["tok_stored0"], s["tok_stored1"]]

        primed = [(s[n], 1) for n in ("iw_read", "yc_done", "ykt_done", "iw_done", "mix_done", "fw_read", "xout_done",
                                      "xmodes_stored", "h_stored0", "h_stored1", "z_done", "tok_stored0", "tok_stored1")]
        primed += [(s["f_done"], 3)]

        def wait(eng, name, value):
            if isinstance(value, int) and value <= 0:
                return
            which = s[name] if isinstance(name, str) else name
            eng.wait_ge(which, value + sum(start for other, start in primed if other is which))

        def then(eng, name, value):
            wait(eng, name, value)
            if not isinstance(value, int):
                eng.nop(nofuse=True)

        block = ctx.enter_context(nc.Block())

        def run_phase(eng, base, kind, body):
            body(kind, 0, base, first=True, more=True)
            with eng.Fori(1, QUADS - 1) as q:
                body(kind, q, base + q, first=False, more=True)
            body(kind, QUADS - 1, base + QUADS - 1, first=False, more=False)
            body(kind, QUADS, base + QUADS, first=False, more=False, drain=True)

        def there(k, lag, first, drain):
            return not drain if k >= lag else not first

        consts, zeroed = [], []

        free = [0]

        def work(n, rows=128):
            at = free[0]
            free[0] += n
            assert free[0] <= B * MODES, free[0]
            return big[0:rows, at:at + n]

        kept = [0]
        wflat = wslot[:, :, :, :].rearrange("p a o m -> p (a o m)")

        def keep(n, rows=128):
            at = kept[0]
            kept[0] += n
            return wflat[0:rows, at:at + n]

        TOK = PAIRS * 128
        q_wt, k_wt, v_wt, o_wt = (keep(D, D) for _ in range(4))
        q_b, k_b, q_b2 = keep(1, D), keep(1, D), keep(1, D)
        v_b, o_b = keep(D, D), keep(D)
        gamma, beta, r_b, lower = keep(D), keep(D), keep(E), keep(E * E)
        r_w = keep(E, D)
        e_w1, e_w2 = keep(E * H, D).rearrange("p (e h) -> p e h", e=E), keep(E * D).rearrange("p (e d) -> p e d", e=E)
        e_b1, e_b2 = keep(E), keep(D, E)
        pick = keep(E * 128, E).rearrange("p (e h) -> p e h", e=E)
        ones = keep(D, D)

        tok_t, h_tok, cen, sqr, nrm = (work(512) for _ in range(5))
        nrm_t, q2_t, qs_t, k_t, ks_t, v_tok = (work(TOK, D) for _ in range(6))
        d2, dist, prob, pnorm = (work(512) for _ in range(4))
        prob_t, att_t = work(TOK, D), qs_t
        h_res, nrm2, feat = work(512), work(512), work(512)
        feat_t = work(TOK, D)
        logit, expw, mask, wfull = (work(PAIRS * E) for _ in range(4))
        beats, ties = work(512), work(512)
        w_t = work(TOK, E)
        hid = [work(512) for _ in range(2)]
        hidw = [work(512) for _ in range(2)]
        y_t = ks_t
        o_tok = work(512)
        a_mean, a_var, a_nt, a_rs = (work(PAIRS) for _ in range(4))
        a = {n: sem("a_" + n) for n in (
            "const", "in", "h", "nrm", "nrmt", "nrmtc", "q", "k", "v", "qc", "kc", "vc", "s", "d2", "dist", "dm", "p", "pn", "pt",
            "ptc", "at", "atc", "o", "feat", "featt", "feattc", "logit", "ex", "exc", "w", "wt", "wtc", "up", "bc", "g", "gw",
            "down", "yc", "yt", "out", "stored", "step", "ones", "qb2")}
        primed += [(a[n], 1) for n in ("yt", "h", "stored")]
        DVE_STEPS = 69
        a_consts = []

        def attention_load(sp):
            lst = [(q_wt, p["attn_Wq"].rearrange("o i -> i o")), (k_wt, p["attn_Wk"].rearrange("o i -> i o")),
                   (v_wt, p["attn_Wv"].rearrange("o i -> i o")), (o_wt, p["attn_Wo"].rearrange("o i -> i o")),
                   (q_b, p["attn_bq"].unsqueeze(1)), (k_b, p["attn_bk"].unsqueeze(1)),
                   (v_b, p["attn_bv"].unsqueeze(0).to_broadcast([D, D])), (o_b, p["attn_bo"].unsqueeze(0).to_broadcast([128, D])),
                   (gamma, p["ffn_gamma"].unsqueeze(0).to_broadcast([128, D])),
                   (beta, p["ffn_beta"].unsqueeze(0).to_broadcast([128, D])),
                   (r_b, p["ffn_br"].unsqueeze(0).to_broadcast([128, E])), (lower, cst["lower"]),
                   (r_w, p["ffn_Wr"]), (e_w1, p["ffn_W1"].rearrange("e d h -> d e h")),
                   (e_w2, p["ffn_W2"].rearrange("e h d -> h e d")), (e_b1, p["ffn_b1"].rearrange("e h -> h e")),
                   (e_b2, p["ffn_b2"]), (pick, cst["pick"].rearrange("p (e h) -> p e h", e=E))]
            for dst, src in lst:
                sp.dma_start(dst, src, allow_slow_non_contiguous=True).then_inc(a["const"], 16)
            a_consts.append(16 * len(lst))

        def attention_sync(sp):
            with sp.Fori(0, STEPS) as it:
                then(sp, a["h"], it)
                for i in range(2):
                    sp.dma_start(tok_t[64 * i:64 * i + 64, :].rearrange("w (n h) -> w n h", n=PAIRS),
                                 tok[bass.ds(it * 2 * PAIRS, 2 * PAIRS)].rearrange("(n i) q (w h) -> i (q w) n h", i=2, h=HH)[i]
                                 ).then_inc(a["in"], 16)
                then(sp, a["out"], it + 1)
                for i in range(2):
                    sp.dma_start(out[bass.ds(it * 2 * PAIRS, 2 * PAIRS)].rearrange("(n i) s d -> i s n d", i=2)[i],
                                 o_tok[64 * i:64 * i + 64, :].rearrange("p (n d) -> p n d", n=PAIRS)
                                 ).then_inc(a["stored"], 16)
            wait(sp, a["stored"], 32 * STEPS)

        def attention_pool(pool):
            wait(pool, "mix_done", LAYERS * GROUPS)
            nc.gpsimd.memset(ones, 1.0).then_inc(a["ones"], 1)

        s_flat, f_flat = (t[:, :, :].rearrange("p a n -> p (a n)") for t in (ps_s, ps_f))

        def attention_tensor(pe):
            mm = nc.tensor.matmul
            pe.wait_ge(a["const"], a_consts[0])
            pe.wait_ge(a["ones"], 1)

            def turn(dst, src, rows, width):
                for n in range(PAIRS):
                    last = mm(dst[0:width, 128 * n:128 * n + 128], src[:, width * n:width * n + width], ident[:, :],
                              start=True, stop=True)
                return last

            with pe.Fori(0, STEPS) as it:
                pe.wait_ge(a["in"], 32 * it + 32)
                then(pe, a["yt"], it)
                for n in range(PAIRS):
                    for i in range(2):
                        r = slice(64 * i, 64 * i + 64)
                        last = mm(ps[0][r, 64 * n:64 * n + 64], tok_t[r, 64 * n:64 * n + 64], ident[r, r], start=True, stop=True)
                last.then_inc(a["h"], 1)
                pe.wait_ge(a["nrm"], it + 1)
                turn(s_flat, nrm, 128, D).then_inc(a["nrmt"], 1)
                then(pe, a["nrmtc"], it + 1)
                for c in range(2):
                    last = mm(ps_f[0:D, c, :], q_wt, nrm_t[:, 512 * c:512 * c + 512], start=True, stop=True)
                last.then_inc(a["q"], 1)
                for c in range(2):
                    last = mm(ps_s[0:D, c, :], k_wt, nrm_t[:, 512 * c:512 * c + 512], start=True, stop=True)
                last.then_inc(a["k"], 1)
                for i in range(2 * PAIRS):
                    last = mm(ps[1 + i // PAIRS][0:D, 64 * (i % PAIRS):64 * (i % PAIRS) + 64], nrm_t[:, 64 * i:64 * i + 64], v_wt,
                              start=True, stop=True)
                last.then_inc(a["v"], 1)
                pe.wait_ge(a["qc"], it + 1)
                then(pe, a["kc"], it + 1)
                for n in range(PAIRS):
                    for i in range(2):
                        c = slice(128 * n + 64 * i, 128 * n + 64 * i + 64)
                        dst = ps[3][64 * i:64 * i + 64, 64 * n:64 * n + 64]
                        mm(dst, q2_t[:, c], k_t[:, c], start=True, stop=False)
                        mm(dst, ones, ks_t[:, c], start=False, stop=False)
                        last = mm(dst, qs_t[:, c], ones, start=False, stop=True)
                last.then_inc(a["s"], 1)
                pe.wait_ge(a["pn"], it + 1)
                turn(f_flat, pnorm, 128, 64).then_inc(a["pt"], 1)
                pe.wait_ge(a["ptc"], it + 1)
                then(pe, a["vc"], it + 1)
                for i in range(2 * PAIRS):
                    c = slice(64 * i, 64 * i + 64)
                    last = mm(s_flat[0:D, c], v_tok[:, c], prob_t[:, c], start=True, stop=True)
                last.then_inc(a["at"], 1)
                pe.wait_ge(a["atc"], it + 1)
                for n in range(PAIRS):
                    last = mm(ps[1][:, 64 * n:64 * n + 64], att_t[:, 128 * n:128 * n + 128], o_wt, start=True, stop=True)
                last.then_inc(a["o"], 1)
                pe.wait_ge(a["feat"], it + 1)
                turn(s_flat, feat, 128, D).then_inc(a["featt"], 1)
                pe.wait_ge(a["feattc"], it + 1)
                for n in range(PAIRS):
                    last = mm(ps[2][:, E * n:E * n + E], feat_t[:, 128 * n:128 * n + 128], r_w, start=True, stop=True)
                last.then_inc(a["logit"], 1)
                pe.wait_ge(a["w"], it + 1)
                turn(f_flat, wfull, 128, E).then_inc(a["wt"], 1)
                pe.wait_ge(a["wtc"], it + 1)

                def down(t):
                    c, e = t // E, t % E
                    pe.wait_ge(a["gw"], it * 2 * E + t + 1)
                    if e == 0:
                        mm(ps_f[0:D, c, :], e_b2, w_t[:, 512 * c:512 * c + 512], start=True, stop=False)
                    mm(ps_f[0:D, c, :], e_w2[:, e, :], hidw[t % 2], start=False, stop=(e == E - 1)).then_inc(a["down"], 1)

                for t in range(2 * E):
                    c, e = t // E, t % E
                    if t >= 2:
                        pe.wait_ge(a["gw"], it * 2 * E + t - 1)
                    mm(ps[t % 2][:, :], e_w1[:, e, :], feat_t[:, 512 * c:512 * c + 512], start=True, stop=True).then_inc(a["up"], 1)
                    mm(ps[2 + t % 2][:, :], pick[:, e, :], w_t[:, 512 * c:512 * c + 512], start=True, stop=True).then_inc(a["bc"], 1)
                    if t:
                        down(t - 1)
                down(2 * E - 1)
                pe.wait_ge(a["yc"], it + 1)
                for n in range(PAIRS):
                    last = mm(ps[3][:, 64 * n:64 * n + 64], y_t[:, 128 * n:128 * n + 128], ident[0:D, 0:D], start=True, stop=True)
                last.then_inc(a["yt"], 1)

        def attention_scalar(act):
            af = nc.scalar.activation
            act.wait_ge(a["const"], a_consts[0])
            af(q_b2, q_b, ACT.Copy, scale=-2.0).then_inc(a["qb2"], 1)
            act.wait_ge(a["qb2"], 1)
            with act.Fori(0, STEPS) as it:
                act.wait_ge(a["nrmt"], it + 1)
                af(nrm_t, s_flat[0:D, :], ACT.Copy).then_inc(a["nrmtc"], 1)
                act.wait_ge(a["q"], it + 1)
                af(q2_t, f_flat[0:D, :], ACT.Identity, bias=q_b2, scale=-2.0)
                af(qs_t, f_flat[0:D, :], ACT.Square, bias=q_b).then_inc(a["qc"], 1)
                act.wait_ge(a["k"], it + 1)
                af(k_t, s_flat[0:D, :], ACT.Identity, bias=k_b)
                af(ks_t, s_flat[0:D, :], ACT.Square, bias=k_b).then_inc(a["kc"], 1)
                act.wait_ge(a["d2"], it + 1)
                af(dist, d2, ACT.Sqrt).then_inc(a["dist"], 1)
                act.wait_ge(a["dm"], it + 1)
                af(prob, d2, ACT.Exp, scale=-1.0 / D ** 0.5).then_inc(a["p"], 1)
                act.wait_ge(a["pt"], it + 1)
                af(prob_t, f_flat[0:D, :], ACT.Copy).then_inc(a["ptc"], 1)
                act.wait_ge(a["at"], it + 1)
                af(att_t, s_flat[0:D, :], ACT.Copy).then_inc(a["atc"], 1)
                act.wait_ge(a["featt"], it + 1)
                af(feat_t, s_flat[0:D, :], ACT.Copy).then_inc(a["feattc"], 1)
                act.wait_ge(a["ex"], it + 1)
                af(expw, mask, ACT.Exp).then_inc(a["exc"], 1)
                act.wait_ge(a["wt"], it + 1)
                af(w_t, f_flat[0:E, :], ACT.Copy).then_inc(a["wtc"], 1)
                for t in range(2 * E):
                    act.wait_ge(a["up"], it * 2 * E + t + 1)
                    if t >= 2:
                        act.wait_ge(a["gw"], it * 2 * E + t - 1)
                    af(hid[t % 2], ps[t % 2][:, :], ACT.Gelu, bias=e_b1[:, t % E:t % E + 1]).then_inc(a["g"], 1)
                act.wait_ge(a["down"], (it + 1) * 2 * E)
                af(y_t, f_flat[0:D, :], ACT.Copy).then_inc(a["yc"], 1)

        def attention_vector(dve, newton):
            v_ = nc.vector

            def groups(t, w=D):
                return t.rearrange("p (n d) -> p n d", d=w)

            def spread(t, w=D):
                return t.unsqueeze(2).to_broadcast([128, PAIRS, w])

            def row(t, rows=128, n=PAIRS):
                return t.unsqueeze(1).to_broadcast([rows, n, t.shape[-1]])

            with dve.Fori(0, STEPS) as it:
                c = [0]

                def link(ins):
                    c[0] += 1
                    ins.then_inc(a["step"], 1)
                    dve.wait_ge(a["step"], it * DVE_STEPS + c[0])

                def norm(dst, src):
                    link(v_.tensor_reduce(a_mean, groups(src), AX.X, ALU.add))
                    link(v_.tensor_scalar(a_mean, a_mean, 1.0 / D, None, ALU.mult))
                    link(v_.tensor_tensor(groups(cen), groups(src), spread(a_mean), ALU.subtract))
                    link(v_.tensor_tensor(sqr, cen, cen, ALU.mult))
                    link(v_.tensor_reduce(a_var, groups(sqr), AX.X, ALU.add))
                    v_.tensor_scalar(a_var, a_var, 1.0 / D, EPS, ALU.mult, ALU.add).then_inc(a["step"], 1)
                    newton(dve, a["step"], it * DVE_STEPS + c[0] + 1, a_rs, a_nt, a_var)
                    c[0] += 12
                    dve.wait_ge(a["step"], it * DVE_STEPS + c[0])
                    return v_.tensor_tensor(groups(dst), groups(cen), spread(a_rs), ALU.mult)

                wait(dve, a["h"], it + 1)
                link(v_.tensor_copy(h_tok, ps[0][:, :]))
                norm(nrm, h_tok).then_inc(a["nrm"], 1)
                dve.wait_ge(a["v"], it + 1)
                for i in range(2):
                    last = v_.tensor_tensor(groups(v_tok[:, 512 * i:512 * i + 512]), groups(ps[1 + i][0:D, :]), row(v_b, D), ALU.add)
                last.then_inc(a["vc"], 1)
                dve.wait_ge(a["s"], it + 1)
                v_.tensor_scalar(d2, ps[3][:, :], 0.0, None, ALU.max).then_inc(a["d2"], 1)
                dve.wait_ge(a["dist"], it + 1)
                link(v_.tensor_reduce(a_mean, groups(dist), AX.X, ALU.min))
                v_.tensor_tensor(groups(d2), groups(dist), spread(a_mean), ALU.subtract).then_inc(a["dm"], 1)
                dve.wait_ge(a["p"], it + 1)
                link(v_.tensor_reduce(a_var, groups(prob), AX.X, ALU.add))
                link(v_.reciprocal(a_rs, a_var))
                v_.tensor_tensor(groups(pnorm), groups(prob), spread(a_rs), ALU.mult).then_inc(a["pn"], 1)
                dve.wait_ge(a["o"], it + 1)
                link(v_.tensor_tensor(h_res, ps[1][:, :], h_tok, ALU.add))
                link(v_.tensor_tensor(groups(h_res), groups(h_res), row(o_b), ALU.add))
                link(norm(nrm2, h_res))
                link(norm(nrm2, nrm2))
                link(v_.tensor_tensor(groups(feat), groups(nrm2), row(gamma), ALU.mult))
                v_.tensor_tensor(groups(feat), groups(feat), row(beta), ALU.add).then_inc(a["feat"], 1)
                dve.wait_ge(a["logit"], it + 1)
                link(v_.tensor_tensor(groups(logit, E), groups(ps[2][:, 0:PAIRS * E], E), row(r_b), ALU.add))
                mine = groups(logit, E).unsqueeze(3).to_broadcast([128, PAIRS, E, E])
                other = groups(logit, E).unsqueeze(2).to_broadcast([128, PAIRS, E, E])
                four = lambda t: t.rearrange("p (n e f) -> p n e f", e=E, f=E)
                v_.tensor_tensor(four(beats), other, mine, ALU.is_gt)
                link(v_.tensor_tensor(four(ties), other, mine, ALU.is_equal))
                link(v_.tensor_tensor(groups(ties, E * E), groups(ties, E * E), row(lower), ALU.mult))
                link(v_.tensor_tensor(beats, beats, ties, ALU.add))
                link(v_.tensor_reduce(wfull, four(beats), AX.X, ALU.add))
                link(v_.tensor_reduce(a_mean, groups(logit, E), AX.X, ALU.max))
                v_.tensor_tensor(groups(mask, E), groups(logit, E), spread(a_mean, E), ALU.subtract).then_inc(a["ex"], 1)
                dve.wait_ge(a["exc"], it + 1)
                link(v_.scalar_tensor_tensor(wfull, wfull, 1.5, expw, ALU.is_lt, ALU.mult))
                link(v_.tensor_reduce(a_var, groups(wfull, E), AX.X, ALU.add))
                link(v_.reciprocal(a_rs, a_var))
                v_.tensor_tensor(groups(wfull, E), groups(wfull, E), spread(a_rs, E), ALU.mult).then_inc(a["w"], 1)
                for t in range(2 * E):
                    dve.wait_ge(a["g"], it * 2 * E + t + 1)
                    dve.wait_ge(a["bc"], it * 2 * E + t + 1)
                    if t >= 2:
                        dve.wait_ge(a["down"], it * 2 * E + t - 1)
                    v_.tensor_tensor(hidw[t % 2], hid[t % 2], ps[2 + t % 2][:, :], ALU.mult).then_inc(a["gw"], 1)
                wait(dve, a["yt"], it + 1)
                wait(dve, a["stored"], 32 * it)
                v_.tensor_tensor(o_tok, ps[3][:, :], h_res, ALU.add).then_inc(a["out"], 1)
                assert c[0] == DVE_STEPS, c[0]

        @block.sync
        def _(sp):
            plain = [
                (ident[:, :], cst["ident"]), (c_center[:, :], cst["center"]), (c_fwh[:, :], cst["fwd_h"]),
                (c_fww[:, :, :], cst["fwd_w"]), (c_inw[:, :, :], cst["inv_w"]), (c_inh, cst["inv_h"]),
                (c_sign[:, :], cst["sign"]),
                (fc0_t[:, 0:3], p["tok_fc0_w"].rearrange("c o -> o c")), (fc0_t[:, 3:4], p["tok_fc0_b"].unsqueeze(1)),
                (conv_w[:, :, :], p["tok_conv_w"].rearrange("l o c -> o l c")),
                (fc1_b[:, :], p["tok_fc1_b"].unsqueeze(1)), (fc2_w[:, :], p["tok_fc2_w"]),
                (fc2_b[0:64, :], p["tok_fc2_b"].unsqueeze(1)), (fc2_b[64:128, :], p["tok_fc2_b"].unsqueeze(1)),
                (fc3_b[:, :], p["tok_fc3_b"].unsqueeze(0).to_broadcast([64, 1]))]
            for g in range(4):
                r = slice(32 * g, 32 * g + 32)
                plain += [(g_all[r, 0, 0:1], p["tok_ln0_g"].unsqueeze(1)), (g_all[r, 1, 0:1], p["tok_ln0_b"].unsqueeze(1)),
                          (g_all[r, 0, 1:5], p["tok_ln_g"].rearrange("l c -> c l")),
                          (g_all[r, 1, 1:5], p["tok_ln_b"].rearrange("l c -> c l"))]
            placed = [(fc1_w[32 * g:32 * g + 32, g, :], p["tok_fc1_w"]) for g in range(4)]
            placed += [(bias_raw[0:32, :], p["tok_conv_b"].rearrange("l o -> o l"))]
            placed += [(fc3_w[64 * g:64 * g + 64, g:g + 1], p["tok_fc3_w"]) for g in range(2)]
            for dst, src in plain:
                sp.dma_start(dst, src, allow_slow_non_contiguous=True).then_inc(s["const_in"], 16)
            sp.wait_ge(s["const_zero"], 1)
            for dst, src in placed:
                sp.dma_start(dst, src, allow_slow_non_contiguous=True).then_inc(s["const_in"], 16)
            consts.append(16 * len(plain + placed))
            sp.wait_ge(s["fc0_copied"], 1)
            sp.dma_start(fc0_rows, fc0_c[:, :]).then_inc(s["fc0_stored"], 16)
            sp.wait_ge(s["fc0_stored"], 16)
            for wq in range(4):
                for w in range(4):
                    r, c = (wq * 4 + w) * 3, (w * 4 + wq) * 32
                    sp.dma_start(fc0_bd[r:r + 3, c:c + 32], fc0_rows[0:3, :]).then_inc(s["fc0_placed"], 16)
                    sp.dma_start(fc0_bd[48:49, c:c + 32], fc0_rows[3:4, :]).then_inc(s["fc0_placed"], 16)

            def load_x(n):
                then(sp, "x_ready", n)
                for ip in range(2):
                    sp.dma_start(x_in[:, ip, :], x[bass.ds(4 * n + 2 * ip, 2)].rearrange("i h w c -> (i h) (w c)")
                                 ).then_inc(s["x_loaded"], 16)

            def load_h(q, n, j):
                then(sp, "y_done", (n - 1) * UNITS + 4 * j + 4)
                sp.dma_start(h_in[j], hstore[bass.ds(q, 1), :, j, :].rearrange("a p n -> (a p) n")
                             ).then_inc(h_loaded[j], 16)

            def load_y(q, n):
                then(sp, "yc_done", n - QUADS)
                sp.dma_start(y_raw[:, :], ymodes[bass.ds(q, 1)].rearrange("a p n -> (a p) n")
                             ).then_inc(s["yraw_loaded"], 16)

            def store_h(q, n, j):
                then(sp, s["act_done"], n * UNITS + 4 * j + 4)
                sp.dma_start(hstore[bass.ds(q, 1), :, j, :].rearrange("a p n -> (a p) n"), h_new[j]
                             ).then_inc(h_stored[j], 16)

            def store_modes(q, n):
                then(sp, s["xout_done"], n + 1)
                sp.dma_start(xmodes[bass.ds(q, 1)].rearrange("a p n -> (a p) n"),
                             x_out[:, :, :, :].rearrange("p a k m -> p (a k m)")).then_inc(s["xmodes_stored"], 16)

            def store_tok(q, n, j):
                then(sp, s["tok_done"], (n - LAYERS * QUADS) * UNITS + 4 * j + 4)
                for g in range(2):
                    sp.dma_start(tok[bass.ds(4 * q, 4), 2 * g:2 * g + 2, 512 * j:512 * j + 512].rearrange("i r n -> r i n"),
                                 tok_sb[32 * g:32 * g + 2, :].rearrange("r (i j n) -> r j i n", i=4, j=2)[:, j]
                                 ).then_inc(tok_stored[j], 16)

            def body(kind, q, n, first, more, drain=False):
                if kind == "stem" and more:
                    load_x(n + 1)
                if kind != "stem" and more:
                    load_y(q + 1, n + 1)
                if not first and kind != "head":
                    store_h(q - 1, n - 1, 0)
                if kind != "stem" and not drain:
                    load_h(q, n, 1)
                if kind == "head" and not first:
                    store_tok(q - 1, n - 1, 0)
                if kind != "stem" and more:
                    load_h(q + 1, n + 1, 0)
                if kind == "head" and not first:
                    store_tok(q - 1, n - 1, 1)
                if kind != "head" and not first:
                    store_h(q - 1, n - 1, 1)
                    store_modes(q - 1, n - 1)

            def mix(ph):
                then(sp, s["xmodes_stored"], 16 * QUADS * ph)
                for j in range(2):
                    then(sp, h_stored[j], 16 * QUADS * ph)
                for c in range(COMP):
                    sp.dma_start(modes[32 * c:32 * c + 32, :, :],
                                 xmodes.rearrange("q (i c) (a m) -> a c (q i) m", i=4, a=COMP)[c]
                                 ).then_inc(s["modes_loaded"], 16)
                then(sp, s["mix_act"], 21 * ph)
                then(sp, s["mix_dve"], 19 * ph)
                for c in range(COMP):
                    sp.dma_start(ymodes.rearrange("q (i c) (a m) -> a c (q i) m", i=4, a=COMP)[c],
                                 modes[32 * c:32 * c + 32, :, :]).then_inc(s["ymodes_stored"], 16)
                then(sp, s["ymodes_stored"], 16 * COMP * ph)
                load_y(0, ph * QUADS)
                load_h(0, ph * QUADS, 0)

            load_x(0)
            run_phase(sp, 0, "stem", body)
            with sp.Fori(1, LAYERS) as ph:
                mix(ph)
                run_phase(sp, ph * QUADS, "layer", body)
            mix(LAYERS)
            attention_load(sp)
            run_phase(sp, LAYERS * QUADS, "head", body)
            for j in range(2):
                wait(sp, tok_stored[j], 32 * QUADS)
            attention_sync(sp)

        @block.gpsimd
        def _(pool):
            for which, start in primed:
                pool.sem_inc(which, start)
            for t in (fc1_w[:, :, :], fc3_w[:, :], fc0_bd, bias_raw[:, :], conv_bd[:, :, :], y_kk[:, :]):
                nc.gpsimd.memset(t, 0.0)
            nc.gpsimd.memset(x_tr, 1.0).then_inc(s["const_zero"], 1)

            def weights(l):
                r = 0
                for slots, parts in (((0, 3), "riir"), ((1, 2), "irri")):
                    for oc in range(CH // OCH):
                        o0, rnd = oc * OCH, l * ROUNDS + r
                        for c, part in enumerate(parts):
                            rows = slice(32 * c, 32 * c + 32)
                            for dst, src in ((w1_raw, p[f"tok_w1{part}"]), (w2_raw, p[f"tok_w2{part}"])):
                                pool.dma_start(dst[rows, :, :].rearrange("p o m -> p (o m)"),
                                               src[bass.ds(l, 1), :, o0:o0 + OCH].rearrange("l i o k m -> (l i) (o k m)")
                                               ).then_inc(s["w_raw"], 16)
                        then(pool, s["w_raw"], 128 * rnd + 128)
                        for i, sl in enumerate(slots):
                            dst = wslot[:, sl, o0:o0 + OCH, :]
                            nc.gpsimd.memset(dst[:, :, M * M:MODES], 0.0)
                            nc.gpsimd.tensor_scalar(dst[:, :, 0:M * M], w1_raw[:, :, :], c_sign[:, sl:sl + 1], None, ALU.mult)
                            nc.gpsimd.tensor_scalar(w2_raw[:, :, :], w2_raw[:, :, :], c_sign[:, 4 + sl:5 + sl], None,
                                                    ALU.mult).then_inc(s["w_step"], 1)
                            then(pool, s["w_step"], 4 * rnd + 2 * i + 1)
                            view = dst[:, :, M:MODES].rearrange("p o (k m) -> p o k m", m=M)
                            rev = w2_raw[:, :, :].rearrange("p o (k m) -> p o k m", m=M)[:, :, ::-1, :]
                            nc.gpsimd.tensor_tensor(view, view, rev, ALU.add).then_inc(s["w_step"], 1)
                            then(pool, s["w_step"], 4 * rnd + 2 * i + 2)
                        r += 1

            pool.wait_ge(s["const_in"], consts[0])
            with pool.Fori(0, LAYERS) as l:
                then(pool, s["mix_done"], l * GROUPS)
                weights(l)
            attention_pool(pool)

        @block.tensor
        def _(pe):
            mm = nc.tensor.matmul
            pe.wait_ge(s["const_in"], consts[0])
            pe.wait_ge(s["const_zero"], 1)
            mm(ps_t1[0:4, 0:32], fc0_t[:, :], c_center[0:32, 0:32], start=True, stop=True).then_inc(s["fc0_center"], 1)
            for g in range(4):
                for l in range(LAYERS):
                    last = mm(ps_t2[32 * g:32 * g + 32, 32 * l:32 * l + 32], conv_w[:, l, :], c_center[0:32, 0:32],
                              start=True, stop=True)
            last.then_inc(s["conv_center"], 1)
            pe.wait_ge(s["fc0_placed"], 16 * 32)
            pe.wait_ge(s["conv_placed"], 1)
            pe.wait_ge(s["table_split"], 3)

            def turn_x(n, k):
                g, ip = k // 2, k % 2
                if k == 0:
                    pe.wait_ge(s["x_ready"], n + 1)
                if k == 1:
                    wait(pe, "fw_read", n - 1)
                wait(pe, "x_copied", n * UNITS + k)
                mm(ps_s[0:48, 0, 0:128], x_cur[:, ip, 48 * g:48 * g + 48], ident[:, :], start=True, stop=True).then_inc(s["x_turned"], 1)

            def center(n):
                i = n - QUADS
                wait(pe, "yraw_loaded", 16 * i + 16)
                wait(pe, "iw_read", 2 * i)
                for sx in range(2):
                    last = mm(ps_s[:, sx, 0:312], c_center[:, :], y_raw[:, 312 * sx:312 * sx + 312], start=True, stop=True)
                last.then_inc(s["yc_done"], 1)

            def inv_w(n, j, forward):
                i = n - QUADS
                wait(pe, "ykt_done", i + 1)
                if j == 1:
                    wait(pe, "iw_read", 2 * i + 1)
                    if forward:
                        wait(pe, "fw_read", n - 1)
                for sx in range(2):
                    last = mm(ps_s[:, sx, 0:KX * 32], c_inw[:, j, :], y_kt[:, 512 * sx:512 * sx + KX * 32],
                              start=True, stop=True)
                last.then_inc(s["iw_done"], 1)

            def start_layer(n):
                wait(pe, "fw_read", n)
                center(n)
                inv_w(n, 0, False)

            def body(kind, q, n, first, more, drain=False):
                for k in range(UNITS):
                    u = n * UNITS + k
                    j, g, ip = k // 4, k // 2, k % 2
                    if not drain:
                        if kind != "stem" and k == 0:
                            inv_w(n, 1, kind == "layer")
                        if kind == "stem":
                            if k < 7:
                                turn_x(n, k + 1)
                            elif more:
                                turn_x(n + 1, 0)
                            pe.wait_ge(s["x_copied"], u + 1)
                            wait(pe, "y_read", u - 1)
                            mm(ps_y[k % 2][:, :], x_tr[0:49, k % 2, :], fc0_bd[0:49, :],
                               start=True, stop=True).then_inc(s["y_done"], 1)
                        else:
                            if k % 4 == 0:
                                wait(pe, "z_done", 2 * (n - QUADS) + j + 1)
                                wait(pe, h_loaded[j], 16 * (n - QUADS) + 16)
                            wait(pe, "y_read", u - 1)
                            for part in range(2):
                                mm(ps_y[k % 2][:, :], c_inh_hl[:, part, :], z_hl[:, ip, j, 512 * (g % 2):512 * (g % 2) + 512],
                                   start=(part == 0), stop=False)
                            for w in range(4):
                                at = ((g % 2) * 4 + w) * 256 + ip * 128
                                last = mm(ps_y[k % 2][:, 128 * w:128 * w + 128], h_in[j][:, at:at + 128], conv_now[:, :],
                                          start=False, stop=(w == 3))
                            last.then_inc(s["y_done"], 1)
                            if more and k == 4:
                                center(n + 1)
                            if more and k == 5:
                                inv_w(n + 1, 0, False)
                    if there(k, LAG_T1, first, drain):
                        v = u - LAG_T1
                        pe.wait_ge(s["xhat_done"], v + 1)
                        wait(pe, "act_done", v)
                        if kind == "head":
                            wait(pe, "tok_done", v - 2 - UNITS * QUADS * LAYERS)
                        for w in range(4):
                            last = nc.tensor.transpose(ps_t1[:, 128 * w:128 * w + 128],
                                                       xhat[(k - LAG_T1) % 2][:, 128 * w:128 * w + 128], ident[:, :])
                        last.then_inc(s["t1_done"], 1)
                    if kind == "head":
                        head_unit(u, k, first, drain)
                        continue
                    if there(k, LAG_T2, first, drain):
                        v, kk = u - LAG_T2, (k - LAG_T2) % 8
                        pe.wait_ge(s["act_done"], v + 1)
                        wait(pe, "px_done", v)
                        for w in range(4):
                            at = (((kk // 2) % 2) * 4 + w) * 256 + (kk % 2) * 128
                            last = nc.tensor.transpose(ps_t2[:, 128 * w:128 * w + 128], h_new[kk // 4][:, at:at + 128],
                                                       ident[:, :])
                        last.then_inc(s["t2_done"], 1)
                    if k % 2 == 0 and not first:
                        pe.wait_ge(s["px_done"], (n - 1) * UNITS + k + 2)
                        if k % 4 == 0:
                            wait(pe, "tw_done", 2 * (n - 1) + k // 4)
                        for i in range(2):
                            mm(ps_f[64 * i:64 * i + 64, (k // 2) % 2, :], c_fwh[:, :], h_px[(k + i) % 4],
                               start=True, stop=True).then_inc(s["f_done"], 1)
                    if k == 7 and not first:
                        fwd_w(kind, n, u, more, drain)

            def fwd_w(kind, n, u, more, drain):
                pe.wait_ge(s["tw_done"], 2 * n)
                if kind == "stem":
                    pe.wait_ge(s["x_copied"], u + 2 if more else (UNITS * QUADS if drain else u + 1))
                else:
                    wait(pe, "iw_read", 2 * (n - QUADS) + (3 if more else (0 if drain else 2)))
                wait(pe, "fw_read", n - 1)
                for sx in range(2):
                    for j in range(2):
                        last = mm(ps_s[:, sx, 0:KX * 32], c_fww[:, j, :], t_w[:, j, 512 * sx:512 * sx + KX * 32],
                                  start=(j == 0), stop=(j == 1))
                last.then_inc(s["fw_done"], 1)

            def fc1(v, vb, pr):
                for i in range(2):
                    wait(pe, "g1_done", 4 * v + 2 * pr + i - 1)
                    dst = ps_f[:, 0, :] if i else ps_t2[:, :]
                    mm(dst, fc1_w[:, 2 * pr + i, :], h_px[vb], start=True, stop=True).then_inc(s["fc1_done"], 1)

            def fc2(v, pr):
                pe.wait_ge(s["g1_done"], 4 * v + 2 * pr + 2)
                wait(pe, "g2_done", 2 * v + pr)
                for i in range(2):
                    last = mm(ps_f[64 * i:64 * i + 64, 1, :], fc2_w[:, :], gelu1[2 * pr + i], start=True, stop=True)
                last.then_inc(s["fc2_done"], 1)

            def fc3(v, vb):
                pe.wait_ge(s["g2_done"], 2 * v + 2)
                for pr in range(2):
                    last = mm(ps_t1[32 * pr:32 * pr + 32, :], fc3_w[:, :], gelu2[2 * vb + pr], start=True, stop=True)
                last.then_inc(s["fc3_done"], 1)

            def head_unit(u, k, first, drain):
                v = u - LAG_T2 - UNITS * QUADS * LAYERS
                vb = (k - LAG_T2) % 2
                now, before = there(k, LAG_T2, first, drain), there(k, LAG_T2 + 1, first, drain)
                if now:
                    pe.wait_ge(s["act_done"], u - LAG_T2 + 1)
                    fc1(v, vb, 0)
                if before:
                    fc2(v - 1, 1)
                if now:
                    fc1(v, vb, 1)
                if before:
                    pe.wait_ge(s["act_done"], u - LAG_T1 + 1 - (k - LAG_T1 + 1 if drain and k >= LAG_T1 else 0))
                    wait(pe, "tok_done", v - 1)
                    fc3(v - 1, 1 - vb)
                if now:
                    fc2(v, 0)

            def mix(ph):
                pe.wait_ge(s["modes_loaded"], 16 * COMP * ph)
                pe.wait_ge(s["w_step"], 4 * ROUNDS * ph)
                pe.wait_ge(s["px_done"], UNITS * QUADS * ph)
                for t in range(GROUPS):
                    if t >= 4:
                        if t % 2 == 0:
                            pe.wait_ge(s["mix_act"], (ph - 1) * 21 + t // 2)
                        else:
                            pe.wait_ge(s["mix_dve"], (ph - 1) * 19 + t // 2 - 1)
                    for m in range(4):
                        last = mm(ps[t % 4][:, 128 * m:128 * m + 128], wslot[:, :, :, 4 * t + m], modes[:, :, 4 * t + m],
                                  start=True, stop=True)
                    last.then_inc(s["mix_done"], 1)

            turn_x(0, 0)
            run_phase(pe, 0, "stem", body)
            with pe.Fori(1, LAYERS) as ph:
                mix(ph)
                start_layer(ph * QUADS)
                run_phase(pe, ph * QUADS, "layer", body)
            mix(LAYERS)
            start_layer(LAYERS * QUADS)
            run_phase(pe, LAYERS * QUADS, "head", body)
            attention_tensor(pe)

        @block.scalar
        def _(act):
            af = nc.scalar.activation
            act.wait_ge(s["const_in"], consts[0])

            def take_x(n):
                act.wait_ge(s["x_loaded"], 32 * n + 32)
                wait(act, "x_turned", UNITS * n)
                for ip in range(2):
                    last = af(x_cur[:, ip, :].rearrange("p (g q w) -> p q g w", g=4, q=4),
                              x_in[:, ip, :].rearrange("p (q g w) -> p q g w", g=4, q=4), ACT.Copy)
                last.then_inc(s["x_ready"], 1)

            def order_y(n):
                i = n - QUADS
                wait(act, "yc_done", i + 1)
                wait(act, "ykt_done", i)
                for sx in range(2):
                    dst = y_kk[:, 512 * sx:512 * sx + 512].rearrange("p (k r) -> p k r", r=32)[:, 0:KX, 0:2 * M]
                    last = af(dst.rearrange("p k (a m) -> p a k m", a=2),
                              ps_s[:, sx, 0:312].rearrange("p (a k m) -> p a k m", a=2, k=KX), ACT.Copy)
                last.then_inc(s["ykk_done"], 1)

            def high_z(n, j):
                i = n - QUADS
                wait(act, "iw_read", 2 * i + j + 1)
                act.wait_ge(s["y_done"], (n - 1) * UNITS + 4 * j + 4)
                for ip in range(2):
                    r = slice(64 * ip, 64 * ip + 64)
                    last = af(z_hl[r, ip, j, :], z_kx[r, :], ACT.Copy)
                last.then_inc(s["z_high"], 1)

            def body(kind, q, n, first, more, drain=False):
                for k in range(UNITS):
                    u = n * UNITS + k
                    if kind == "stem" and k == 7 and more:
                        take_x(n + 1)
                    if kind != "stem" and k == 1 and not drain:
                        high_z(n, 1)
                    if kind != "stem" and k == 6 and more:
                        high_z(n + 1, 0)
                    if not drain:
                        act.wait_ge(s["y_done"], u + 1)
                        wait(act, "ss_done", u - 1)
                        af(y_sq[k % 2], ps_y[k % 2][:, :], ACT.Square).then_inc(s["sq_done"], 1)
                        wait(act, "xhat_done", u - 7)
                        af(y_sb[k], ps_y[k % 2][:, :], ACT.Copy).then_inc(s["y_read"], 1)
                    if there(k, LAG_T1, first, drain):
                        v, kk = u - LAG_T1, (k - LAG_T1) % 8
                        act.wait_ge(s["t1_done"], v + 1)
                        if kind == "head":
                            wait(act, "fc1_done", 4 * (v - 1 - UNITS * QUADS * LAYERS))
                            af(h_px[kk % 2], ps_t1[:, :], ACT.Identity, bias=g_now[:, 1:2], scale=g_now[:, 0:1]
                               ).then_inc(s["act_done"], 1)
                        else:
                            if kk % 4 == 0:
                                wait(act, h_stored[kk // 4], 16 * (n if k >= LAG_T1 else n - 1))
                            dst = h_new[kk // 4].rearrange("p (w q) -> p w q", w=8)[:, 4 * ((kk // 2) % 2):4 * ((kk // 2) % 2) + 4,
                                                                                    128 * (kk % 2):128 * (kk % 2) + 128]
                            af(dst, ps_t1[:, :].rearrange("p (w q) -> p w q", w=4), ACT.Identity if kind == "stem" else ACT.Gelu,
                               bias=g_now[:, 1:2], scale=g_now[:, 0:1]).then_inc(s["act_done"], 1)
                    if kind == "head":
                        head_unit(u, k, first, drain)
                        if more and k == 4:
                            order_y(n + 1)
                        continue
                    if there(k, LAG_T2, first, drain):
                        v = u - LAG_T2
                        act.wait_ge(s["t2_done"], v + 1)
                        wait(act, "f_done", v - 3)
                        af(h_px[(k - LAG_T2) % 4], ps_t2[:, :], ACT.Copy).then_inc(s["px_done"], 1)
                    if kind == "layer" and more and k == 4:
                        order_y(n + 1)
                    if k == 7 and not first:
                        wait(act, "fw_read", n)
                        wait(act, "xmodes_stored", 16 * (n - 1))
                        for sx in range(2):
                            src = fw_sb[:, 416 * sx:416 * sx + 416].rearrange("p (k r) -> p k r", r=32)[:, :, 0:2 * M]
                            last = af(x_out[:, 2 * sx:2 * sx + 2, :, :], src.rearrange("p k (a m) -> p a k m", a=2), ACT.Copy)
                        last.then_inc(s["xout_done"], 1)

            def head_unit(u, k, first, drain):
                v = u - LAG_T2 - UNITS * QUADS * LAYERS
                now, before = there(k, LAG_T2, first, drain), there(k, LAG_T2 + 1, first, drain)

                def g1(v, pr):
                    wait(act, "fc2_done", 2 * (v - 1) + pr + 1)
                    for i in range(2):
                        act.wait_ge(s["fc1_done"], 4 * v + 2 * pr + i + 1)
                        af(gelu1[2 * pr + i], ps_f[:, 0, :] if i else ps_t2[:, :], ACT.Gelu, bias=fc1_b[:, :]
                           ).then_inc(s["g1_done"], 1)

                def g2(v, vb, pr):
                    act.wait_ge(s["fc2_done"], 2 * v + pr + 1)
                    wait(act, "fc3_done", v - 1)
                    af(gelu2[2 * vb + pr], ps_f[:, 1, :], ACT.Gelu, bias=fc2_b[:, :]).then_inc(s["g2_done"], 1)

                vb = (k - LAG_T2) % 2
                if now:
                    g1(v, 0)
                if before:
                    g2(v - 1, 1 - vb, 1)
                if now:
                    g1(v, 1)
                    g2(v, vb, 0)

            def mix(ph):
                act.wait_ge(s["now_done"], ph)
                base = (ph - 1) * GROUPS
                for t in range(0, GROUPS, 2):
                    wait(act, "mix_done", base + t + 1)
                    src = ps[t % 4][:, :].rearrange("p (m i) -> p i m", m=4)
                    if t == 0:
                        af(modes[:, :, 0:1], src[:, :, 0:1], ACT.Identity, bias=bias_now[:, :]).then_inc(s["mix_act"], 1)
                        af(modes[:, :, 1:4], src[:, :, 1:4], ACT.Copy).then_inc(s["mix_act"], 1)
                    else:
                        af(modes[:, :, 4 * t:4 * t + 4], src, ACT.Copy).then_inc(s["mix_act"], 1)

            take_x(0)
            run_phase(act, 0, "stem", body)
            with act.Fori(1, LAYERS) as ph:
                mix(ph)
                act.wait_ge(s["ymodes_stored"], 16 * COMP * ph)
                order_y(ph * QUADS)
                high_z(ph * QUADS, 0)
                run_phase(act, ph * QUADS, "layer", body)
            mix(LAYERS)
            act.wait_ge(s["ymodes_stored"], 16 * COMP * LAYERS)
            order_y(LAYERS * QUADS)
            high_z(LAYERS * QUADS, 0)
            run_phase(act, LAYERS * QUADS, "head", body)
            attention_scalar(act)

        @block.vector
        def _(dve):
            v_ = nc.vector
            dve.wait_ge(s["const_in"], consts[0])
            dve.wait_ge(s["fc0_center"], 1)
            v_.tensor_copy(c_inh_hl[:, 0, :], c_inh).then_inc(s["table_split"], 1)
            v_.memset(ps_s[:, :, KX * 32:512], 0.0).then_inc(s["table_split"], 1)
            dve.wait_ge(s["table_split"], 2)
            v_.tensor_tensor(c_inh_hl[:, 1, :], c_inh, c_inh_hl[:, 0, :].bitcast(f32), ALU.subtract
                             ).then_inc(s["table_split"], 1)
            v_.tensor_copy(fc0_c[:, :], ps_t1[0:4, 0:32]).then_inc(s["fc0_copied"], 1)
            dve.wait_ge(s["conv_center"], 1)
            dve.wait_ge(s["const_zero"], 1)
            v_.tensor_copy(g_now[:, :], g_all[:, :, 0])
            for g in range(4):
                r = slice(32 * g, 32 * g + 32)
                last = v_.tensor_copy(conv_bd[r, :, 32 * g:32 * g + 32], ps_t2[r, 0:128].rearrange("p (l o) -> p l o", l=LAYERS))
            last.then_inc(s["conv_placed"], 1)

            def copy_x(n, k):
                u = n * UNITS + k
                dve.wait_ge(s["x_turned"], u + 1)
                wait(dve, "y_done", u - 1)
                v_.tensor_copy(x_tr[0:48, k % 2, :], ps_s[0:48, 0, 0:128]).then_inc(s["x_copied"], 1)

            def turn_y(n):
                i = n - QUADS
                wait(dve, "ykk_done", i + 1)
                wait(dve, "iw_done", 2 * i)
                v_.transpose(y_kt[:, :], y_kk[:, :]).then_inc(s["ykt_done"], 1)

            def turn_z(n, j):
                i = n - QUADS
                wait(dve, "iw_done", 2 * i + j + 1)
                wait(dve, "z_done", 2 * i + j)
                v_.transpose(z_kx.rearrange("p (w o) -> p o w", o=32),
                             ps_s[:, :, :].rearrange("p a n -> p (a n)").rearrange("p (k o) -> p o k", o=32)
                             ).then_inc(s["iw_read"], 1)

            def low_z(n, j):
                i = n - QUADS
                wait(dve, "z_high", 2 * i + j + 1)
                for ip in range(2):
                    r, other = slice(64 * ip, 64 * ip + 64), slice(64 - 64 * ip, 128 - 64 * ip)
                    last = v_.tensor_tensor(z_hl[other, ip, j, :], z_kx[r, :], z_hl[r, ip, j, :].bitcast(f32), ALU.subtract)
                last.then_inc(s["z_done"], 1)

            def turn_w(n, j):
                wait(dve, "f_done", n * UNITS + 4 * j + 4)
                wait(dve, "fw_done", n)
                v_.transpose(t_w[:, j, :].rearrange("p (k c) -> p c k", c=32),
                             ps_f[:, :, :].rearrange("p a n -> p (a n)").rearrange("p (w c) -> p c w", c=32)
                             ).then_inc(s["tw_done"], 1)

            def body(kind, q, n, first, more, drain=False):
                for k in range(UNITS):
                    u, j = n * UNITS + k, k // 4
                    if kind != "stem" and not drain and k == 0:
                        turn_z(n, 1)
                    if kind != "stem" and not drain and k == 1:
                        low_z(n, 1)
                    if kind != "stem" and more and k == 6:
                        low_z(n + 1, 0)
                    if kind == "stem" and not drain:
                        if k < 7:
                            copy_x(n, k + 1)
                        elif more:
                            copy_x(n + 1, 0)
                    if kind != "head" and not first and k in (3, 7):
                        turn_w(n - 1, k // 4)
                    if there(k, LAG_XH, first, drain):
                        v, kk = u - LAG_XH, (k - LAG_XH) % 8
                        dve.wait_ge(s["y_read"], v + 1)
                        dve.wait_ge(s["norm_step"], 12 * (2 * n + (1 if k >= LAG_XH else 0)))
                        wait(dve, "t1_done", v - 1)
                        v_.tensor_tensor(xhat[kk % 2].rearrange("p (a c) -> p a c", c=32),
                                         y_sb[kk].rearrange("p (a c) -> p a c", c=32),
                                         rstd[:, kk // 4, 16 * (kk % 4):16 * (kk % 4) + 16].unsqueeze(2).to_broadcast([128, 16, 32]),
                                         ALU.mult).then_inc(s["xhat_done"], 1)
                    if not drain:
                        dve.wait_ge(s["sq_done"], u + 1)
                        v_.tensor_reduce(ss[:, j, 16 * (k % 4):16 * (k % 4) + 16], y_sq[k % 2].rearrange("p (a c) -> p a c", c=32),
                                         AX.X, ALU.add).then_inc(s["ss_done"], 1)
                        if k % 4 == 3:
                            rsqrt_half(n, k)
                        if kind != "stem" and more and k == 4:
                            turn_y(n + 1)
                        if kind != "stem" and more and k == 5:
                            turn_z(n + 1, 0)
                    if kind == "head" and there(k, LAG_T2 + 1, first, drain):
                        v, kk = u - LAG_T2 - 1 - UNITS * QUADS * LAYERS, (k - LAG_T2 - 1) % 8
                        dve.wait_ge(s["fc3_done"], v + 1)
                        if kk % 4 == 0:
                            wait(dve, tok_stored[kk // 4], 32 * ((n if k > LAG_T2 else n - 1) - QUADS * LAYERS))
                        dst = tok_sb[:, :].rearrange("p (q i w h) -> p q w i h", q=2, i=2, w=16)[
                            :, kk % 2, 4 * (kk // 2):4 * (kk // 2) + 4, :, :]
                        v_.tensor_scalar(dst, ps_t1[0:64, :].rearrange("p (w i h) -> p w i h", w=4, i=2), fc3_b[:, :], None,
                                         ALU.add).then_inc(s["tok_done"], 1)
                    if kind != "head" and k == 7 and not first:
                        dve.wait_ge(s["fw_done"], n)
                        wait(dve, "xout_done", n - 1)
                        v_.transpose(fw_sb[:, :], ps_s[:, :, 0:KX * 32]).then_inc(s["fw_read"], 1)

            def rsqrt_half(n, k):
                j = k // 4
                at = 12 * (2 * n + j)
                dve.wait_ge(s["ss_done"], n * UNITS + k + 1)
                v_.tensor_scalar(var[:, :], ss[:, j, :], 1.0 / CH, EPS, ALU.mult, ALU.add).then_inc(s["norm_step"], 1)
                newton(dve, s["norm_step"], at + 1, rstd[:, j, :], nt[:, :], var[:, :])

            def newton(eng, step, at, r, t, v):
                eng.wait_ge(step, at)
                v_.tensor_scalar(t.bitcast(i32), v.bitcast(i32), 1, None, ALU.logical_shift_right).then_inc(step, 1)
                eng.wait_ge(step, at + 1)
                v_.tensor_scalar(r.bitcast(i32), t.bitcast(i32), -1, 0x5F3759DF, ALU.mult, ALU.add).then_inc(step, 1)
                for i in range(3):
                    eng.wait_ge(step, at + 2 + 3 * i)
                    v_.tensor_tensor(t, r, r, ALU.mult).then_inc(step, 1)
                    eng.wait_ge(step, at + 3 + 3 * i)
                    v_.scalar_tensor_tensor(t, t, -0.5, v, ALU.mult, ALU.mult).then_inc(step, 1)
                    eng.wait_ge(step, at + 4 + 3 * i)
                    v_.scalar_tensor_tensor(r, t, 1.5, r, ALU.add, ALU.mult).then_inc(step, 1)

            def mix(ph):
                dve.wait_ge(s["y_done"], UNITS * QUADS * ph)
                dve.wait_ge(s["act_done"], UNITS * QUADS * ph)
                v_.tensor_copy(conv_now[:, :], conv_bd[:, bass.ds(ph - 1, 1), :].rearrange("p l o -> p (l o)"))
                v_.tensor_copy(g_now[:, :], g_all[:, :, bass.ds(ph, 1)].rearrange("p a l -> p (a l)"))
                v_.tensor_scalar(bias_now[:, :], bias_raw[:, bass.ds(ph - 1, 1)], float(HH * WW), None,
                                 ALU.mult).then_inc(s["now_done"], 1)
                base = (ph - 1) * GROUPS
                for t in range(1, GROUPS, 2):
                    wait(dve, "mix_done", base + t + 1)
                    v_.tensor_copy(modes[:, :, 4 * t:4 * t + 4], ps[t % 4][:, :].rearrange("p (m i) -> p i m", m=4)
                                   ).then_inc(s["mix_dve"], 1)

            def start_layer(ph):
                dve.wait_ge(s["ymodes_stored"], 16 * COMP * ph)
                turn_y(ph * QUADS)
                turn_z(ph * QUADS, 0)
                low_z(ph * QUADS, 0)

            copy_x(0, 0)
            run_phase(dve, 0, "stem", body)
            with dve.Fori(1, LAYERS) as ph:
                mix(ph)
                start_layer(ph)
                run_phase(dve, ph * QUADS, "layer", body)
            mix(LAYERS)
            start_layer(LAYERS)
            run_phase(dve, LAYERS * QUADS, "head", body)
            attention_vector(dve, newton)


def transform_tables():
    import numpy as np
    k, ky, h = np.arange(KX), np.arange(M), np.arange(HH)
    ch, sh = np.cos(2 * np.pi * np.outer(h, k) / HH), np.sin(2 * np.pi * np.outer(h, k) / HH)
    fwd_h, inv_h = np.zeros((2, HH, 2, 32)), np.zeros((4, 32, 2, HH))
    for i in range(2):
        fwd_h[i, :, i, 0:KX], fwd_h[i, :, i, 16:16 + KX] = ch, sh
    for i in range(4):
        inv_h[i, 0:KX, i % 2, :], inv_h[i, 16:16 + KX, i % 2, :] = ch.T, sh.T
    fwd_w, inv_w = np.zeros((4, 32, 2, 4, 32)), np.zeros((4, 32, 2, 4, 32))
    scale = np.where(ky == 0, 1.0, 2.0) / (HH * WW)
    for j in range(2):
        r = np.arange(32)
        w = 16 * (r % 4) + 8 * j + r // 4
        cw, sw = np.cos(2 * np.pi * np.outer(w, ky) / WW), np.sin(2 * np.pi * np.outer(w, ky) / WW)
        for i in range(4):
            fwd_w[i, :, j, i, 0:M], fwd_w[i, :, j, i, M:2 * M] = cw, sw
            inv_w[i, 0:M, j, i, :], inv_w[i, M:2 * M, j, i, :] = (cw * scale).T, (sw * scale).T
    center = np.zeros((4, 32, 4, 32))
    for i in range(4):
        center[i, :, i, :] = np.eye(32) - 1.0 / 32
    s1 = np.array([[1, -1, -1, -1], [1, 1, 1, -1], [1, 1, 1, -1], [-1, 1, 1, 1]])
    s2 = np.array([[1, -1, 1, 1], [1, 1, -1, 1], [-1, -1, 1, -1], [1, -1, 1, 1]])
    s2[:, 3], s2[:, 2] = s2[:, 3] * s2[:, 0], s2[:, 2] * s2[:, 1]
    sign = np.repeat(np.concatenate([s1, s2], 1), 32, 0)
    pick = np.repeat(np.eye(E)[:, :, None], 128, 2)
    lower = np.repeat(np.tril(np.ones((E, E)), -1).reshape(1, -1), 128, 0)
    tables = {"ident": np.eye(128), "center": center, "fwd_h": fwd_h, "fwd_w": fwd_w, "inv_w": inv_w, "inv_h": inv_h,
              "sign": sign, "pick": pick, "lower": lower}
    shapes = {"center": (128, 128), "fwd_h": (128, 64), "fwd_w": (128, 2, 128), "inv_w": (128, 2, 128), "inv_h": (128, 128),
              "pick": (E, E * 128)}
    return {n: np.ascontiguousarray(t.reshape(shapes.get(n, t.shape)), dtype=np.float32) for n, t in tables.items()}


_PARAMS = ["tok_fc0_w", "tok_fc0_b", "tok_ln0_g", "tok_ln0_b", "tok_w1r", "tok_w1i", "tok_w2r", "tok_w2i", "tok_conv_w",
           "tok_conv_b", "tok_ln_g", "tok_ln_b", "tok_fc1_w", "tok_fc1_b", "tok_fc2_w", "tok_fc2_b", "tok_fc3_w", "tok_fc3_b",
           "attn_Wq", "attn_bq", "attn_Wk", "attn_bk", "attn_Wv", "attn_bv", "attn_Wo", "attn_bo",
           "ffn_gamma", "ffn_beta", "ffn_Wr", "ffn_br", "ffn_W1", "ffn_b1", "ffn_W2", "ffn_b2"]


def kernel(**inputs):
    import numpy as _np
    import concourse.bacc as _bacc
    from concourse import mybir as _mybir
    from concourse.bass_utils import run_bass_kernel_spmd as _run

    nc = _bacc.Bacc("TRN2", target_bir_lowering=False, num_devices=1)
    f32 = _mybir.dt.float32
    arrays = {"x_dram": _np.ascontiguousarray(inputs["x"])}
    x = nc.dram_tensor("x_dram", arrays["x_dram"].shape, f32, kind="ExternalInput").ap()
    p, cst = {}, {}
    for name in _PARAMS:
        arr = _np.ascontiguousarray(inputs[f"L0_{name}"])
        arrays[f"in_{name}"] = arr
        p[name] = nc.dram_tensor(f"in_{name}", arr.shape, f32, kind="ExternalInput").ap()
    for name, arr in transform_tables().items():
        arrays[f"table_{name}"] = arr
        cst[name] = nc.dram_tensor(f"table_{name}", arr.shape, f32, kind="ExternalInput").ap()
    out = nc.dram_tensor("out_dram", (B, HH, WW), f32, kind="ExternalOutput").ap()
    scratch = [nc.dram_tensor(n, shape, f32, kind="Internal").ap() for n, shape in (
        ("xmodes", (QUADS, 128, COMP * MODES)), ("ymodes", (QUADS, 128, COMP * MODES)), ("hstore", (QUADS, 128, 2, 2048)),
        ("tok", (B, 4, 16 * HH)), ("fc0_rows", (4, 32)))]
    vit_tower(nc, x, p, cst, out, scratch)
    r = _run(nc, [arrays], core_ids=[0])
    return r.results[0]["out_dram"]
```

```python
import concourse.bass as bass
from concourse import mybir
from contextlib import ExitStack

B, HH, WW, CH, LAYERS, M = 128, 64, 64, 32, 4, 12
QUADS = B // 4
UNITS = 8
KX = M + 1
MODES = KX * M
COMP = 4
EPS = 1e-5
F1, F2 = 128, 64
LAG_XH, LAG_T1, LAG_T2, LAG_F = 4, 5, 6, 7
OCH = 4
ROUNDS = 2 * (CH // OCH)
GROUPS = MODES // 4
D, E, H = 64, 8, 128
PAIRS = 8
STEPS = B // 2 // PAIRS


def vit_tower(nc, x, p, cst, out, scratch):
    f32, i32, f32r = mybir.dt.float32, mybir.dt.int32, mybir.dt.float32r
    ALU, ACT, AX = mybir.AluOpType, mybir.ActivationFunctionType, mybir.AxisListType
    xmodes, ymodes, hstore, tok, fc0_rows = scratch

    ctx = ExitStack()
    with ctx:
        def sb(name, shape, dt=f32):
            return ctx.enter_context(nc.sbuf_tensor(name, shape, dt))

        def sem(name):
            return ctx.enter_context(nc.semaphore(name))

        wslot = sb("wslot", [128, COMP, CH, MODES])
        big = sb("big", [128, B * MODES])
        modes = big[:, :].rearrange("p (i m) -> p i m", m=MODES)
        taken = [0]

        def carve(n):
            at = taken[0]
            taken[0] += n
            assert taken[0] <= B * MODES
            return big[:, at:at + n]

        h_in = [carve(2048) for _ in range(2)]
        h_new = [carve(2048) for _ in range(2)]
        y_sb = [carve(512) for _ in range(8)]
        y_sq = [carve(512) for _ in range(2)]
        xhat = [carve(512) for _ in range(2)]
        h_px = [carve(512) for _ in range(4)]
        ss, rstd = (carve(128).rearrange("p (j n) -> p j n", j=2) for _ in range(2))
        var, nt = carve(64), carve(64)
        z_kx = carve(1024)
        t_w = carve(2048).rearrange("p (j n) -> p j n", j=2)
        fw_sb = sb("fw_sb", [128, 832])
        tok_sb = big[0:64, 4096:8192]
        gelu1 = [t_w[:, i // 2, 512 * (i % 2):512 * (i % 2) + 512] for i in range(4)]
        spare = wslot[:, :, :, :].rearrange("p a o m -> p (a o m)")[:, 3 * CH * MODES:]
        gelu2 = [spare[:, 512 * i:512 * i + 512] for i in range(4)]
        y_raw = sb("y_raw", [128, COMP * MODES])
        y_kk = sb("y_kk", [128, 1024])
        y_kt = sb("y_kt", [128, 1024])
        x_out = sb("x_out", [128, COMP, KX, M])
        z_hl = sb("z_hl", [128, 2, 2, 1024], f32r)
        x_in = h_in[0][:, 0:2 * WW * 3].rearrange("p (i w) -> p i w", i=2)
        x_cur = h_in[0][:, 384:384 + 2 * WW * 3].rearrange("p (i w) -> p i w", i=2)
        x_tr = h_in[0][0:64, 768:1024].rearrange("p (i w) -> p i w", i=2)
        fc0_bd = h_in[0][0:64, 1024:1536]
        c_inh = h_in[0][:, 1536:1664]
        x_hl = sb("x_hl", [128, 2, 512], f32r)
        w1_raw = sb("w1_raw", [128, OCH, M * M])
        w2_raw = sb("w2_raw", [128, OCH, M * M])

        ident = sb("ident", [128, 128])
        c_center = sb("c_center", [128, 128])
        c_fwh = sb("c_fwh", [128, 64])
        c_fww = sb("c_fww", [128, 2, 128])
        c_inw = sb("c_inw", [128, 2, 128])
        c_inh_hl = sb("c_inh_hl", [128, 2, 128], f32r)
        c_sign = sb("c_sign", [128, 8])
        fc0_t = sb("fc0_t", [32, 4])
        fc0_c = sb("fc0_c", [4, 32])
        conv_w = sb("conv_w", [32, LAYERS, 32])
        conv_bd = sb("conv_bd", [128, LAYERS, 128])
        conv_now = sb("conv_now", [128, 128])
        bias_raw = sb("bias_raw", [128, LAYERS])
        bias_now = sb("bias_now", [128, 1])
        g_all = sb("g_all", [128, 2, 5])
        g_now = sb("g_now", [128, 2])
        fc1_hl = sb("fc1_hl", [128, 2, 2, F1], f32r)
        fc1_w = h_in[0][:, 1664:1664 + F1]
        fc1_b = sb("fc1_b", [128, 1])
        fc2_w = sb("fc2_w", [128, F2])
        fc2_b = sb("fc2_b", [128, 1])
        fc3_w = sb("fc3_w", [128, 32])
        fc3_b = sb("fc3_b", [64, 1])

        ps = [ctx.enter_context(nc.psum_tensor(f"bank{i}", [128, 512], f32)) for i in range(4)]
        ps_y, ps_t1, ps_t2 = [ps[0], ps[1]], ps[2], ps[3]
        ps_s = ctx.enter_context(nc.psum_tensor("ps_s", [128, 2, 512], f32))
        ps_f = ctx.enter_context(nc.psum_tensor("ps_f", [128, 2, 512], f32))

        s = {n: sem(n) for n in (
            "const_in", "const_zero", "fc0_center", "fc0_copied", "fc0_stored", "fc0_placed", "conv_center", "conv_placed",
            "x_loaded", "x_ready", "x_turned", "x_copied",
            "h_loaded0", "h_loaded1", "h_stored0", "h_stored1", "yraw_loaded", "xmodes_stored",
            "y_done", "sq_done", "y_read", "ss_done", "norm_step", "xhat_done", "t1_done", "act_done", "t2_done",
            "px_done", "f_done", "tw_done", "fw_done", "fw_read", "xout_done",
            "yc_done", "ykk_done", "ykt_done", "iw_done", "iw_read",
            "now_done", "modes_loaded", "mix_done", "mix_act", "mix_dve", "ymodes_stored",
            "w_raw", "w_step",
            "z_high", "z_high2", "z_done", "table_split", "x_high", "x_split", "fc1_done", "g1_done", "fc2_done", "g2_done", "fc3_done", "tok_done", "tok_stored0",
            "tok_stored1")}
        h_loaded = [s["h_loaded0"], s["h_loaded1"]]
        h_stored = [s["h_stored0"], s["h_stored1"]]
        tok_stored = [s["tok_stored0"], s["tok_stored1"]]

        primed = [(s[n], 1) for n in ("iw_read", "yc_done", "ykt_done", "iw_done", "mix_done", "fw_read", "xout_done",
                                      "xmodes_stored", "h_stored0", "h_stored1", "z_done", "tok_stored0", "tok_stored1")]
        primed += [(s["f_done"], 3), (s["tw_done"], 1), (s["fw_done"], 1)]

        def wait(eng, name, value):
            if isinstance(value, int) and value <= 0:
                return
            which = s[name] if isinstance(name, str) else name
            eng.wait_ge(which, value + sum(start for other, start in primed if other is which))

        def then(eng, name, value):
            wait(eng, name, value)
            if not isinstance(value, int):
                eng.nop(nofuse=True)

        block = ctx.enter_context(nc.Block())

        def run_phase(eng, base, kind, body):
            body(kind, 0, base, first=True, more=True)
            with eng.Fori(1, QUADS - 1) as q:
                body(kind, q, base + q, first=False, more=True)
            body(kind, QUADS - 1, base + QUADS - 1, first=False, more=False)
            body(kind, QUADS, base + QUADS, first=False, more=False, drain=True)

        def there(k, lag, first, drain):
            return not drain if k >= lag else not first

        consts, zeroed = [], []

        free = [0]

        def work(n, rows=128):
            at = free[0]
            free[0] += n
            assert free[0] <= B * MODES, free[0]
            return big[0:rows, at:at + n]

        kept = [0]
        wflat = wslot[:, :, :, :].rearrange("p a o m -> p (a o m)")

        def keep(n, rows=128):
            at = kept[0]
            kept[0] += n
            return wflat[0:rows, at:at + n]

        TOK = PAIRS * 128
        q_wt, k_wt, v_wt, o_wt = (keep(D, D) for _ in range(4))
        q_b, k_b, q_b2 = keep(1, D), keep(1, D), keep(1, D)
        v_b, o_b = keep(D, D), keep(D)
        gamma, beta, r_b, lower = keep(D), keep(D), keep(E), keep(E * E)
        r_w = keep(E, D)
        e_w1, e_w2 = keep(E * H, D).rearrange("p (e h) -> p e h", e=E), keep(E * D).rearrange("p (e d) -> p e d", e=E)
        e_b1, e_b2 = keep(E), keep(D, E)
        pick = keep(E * 128, E).rearrange("p (e h) -> p e h", e=E)
        ones = keep(D, D)

        tok_t, h_tok, cen, sqr, nrm = (work(512) for _ in range(5))
        nrm_t, q2_t, qs_t, k_t, ks_t, v_tok = (work(TOK, D) for _ in range(6))
        d2, dist, prob, pnorm = (work(512) for _ in range(4))
        prob_t, att_t = work(TOK, D), qs_t
        h_res, nrm2, feat = work(512), work(512), work(512)
        feat_t = work(TOK, D)
        logit, expw, mask, wfull = (work(PAIRS * E) for _ in range(4))
        beats, ties = work(512), work(512)
        w_t = work(TOK, E)
        hid = [work(512) for _ in range(2)]
        hidw = [work(512) for _ in range(2)]
        y_t = keep(TOK, D)
        feat_hl = z_hl[:, 0, 0, :]
        w_hl = z_hl[0:40, 0, 1, :]
        pick_hl = x_hl[0:40, :, :].rearrange("p a (e h) -> p (a e) h", h=128)
        w1_hl = z_hl[:, 1, :, :].rearrange("p a (e h) -> p a e h", e=E)
        o_tok = work(512)
        a_mean, a_var, a_nt, a_rs = (work(PAIRS) for _ in range(4))
        a = {n: sem("a_" + n) for n in (
            "const", "in", "h", "nrm", "nrmt", "nrmtc", "q", "k", "v", "qc", "kc", "vc", "s", "d2", "dist", "dm", "p", "pn", "pt",
            "ptc", "at", "atc", "o", "feat", "featt", "feattc", "logit", "ex", "exc", "w", "wt", "wtc", "up", "bc", "g", "gw",
            "down", "yc", "yt", "out", "stored", "step", "ones", "qb2",
            "split", "fhigh", "flow", "wlow")}
        primed += [(a["gw"], 2), (a["down"], 2), (a["out"], 1), (a["yt"], 1), (a["yc"], 1)]
        DVE_STEPS = 70
        a_consts = []

        def attention_load(sp):
            lst = [(q_wt, p["attn_Wq"].rearrange("o i -> i o")), (k_wt, p["attn_Wk"].rearrange("o i -> i o")),
                   (v_wt, p["attn_Wv"].rearrange("o i -> i o")), (o_wt, p["attn_Wo"].rearrange("o i -> i o")),
                   (q_b, p["attn_bq"].unsqueeze(1)), (k_b, p["attn_bk"].unsqueeze(1)),
                   (v_b, p["attn_bv"].unsqueeze(0).to_broadcast([D, D])), (o_b, p["attn_bo"].unsqueeze(0).to_broadcast([128, D])),
                   (gamma, p["ffn_gamma"].unsqueeze(0).to_broadcast([128, D])),
                   (beta, p["ffn_beta"].unsqueeze(0).to_broadcast([128, D])),
                   (r_b, p["ffn_br"].unsqueeze(0).to_broadcast([128, E])), (lower, cst["lower"]),
                   (r_w, p["ffn_Wr"]), (e_w1, p["ffn_W1"].rearrange("e d h -> d e h")),
                   (e_w2, p["ffn_W2"].rearrange("e h d -> h e d")), (e_b1, p["ffn_b1"].rearrange("e h -> h e")),
                   (e_b2, p["ffn_b2"]), (pick, cst["pick"].rearrange("p (e h) -> p e h", e=E))]
            for dst, src in lst:
                sp.dma_start(dst, src, allow_slow_non_contiguous=True).then_inc(a["const"], 16)
            a_consts.append(16 * len(lst))

        def run_steps(eng, attention, experts):
            attention(0, False)
            with eng.Fori(1, STEPS) as it:
                attention(it, True)
            experts(STEPS - 1, 0, 2 * E)

        def attention_sync(sp):
            def load(it):
                then(sp, a["h"], it)
                for i in range(2):
                    sp.dma_start(tok_t[64 * i:64 * i + 64, :].rearrange("w (n h) -> w n h", n=PAIRS),
                                 tok[bass.ds(it * 2 * PAIRS, 2 * PAIRS)].rearrange("(n i) q (w h) -> i (q w) n h", i=2, h=HH)[i]
                                 ).then_inc(a["in"], 16)

            def store(it):
                then(sp, a["out"], it + 1)
                for i in range(2):
                    sp.dma_start(out[bass.ds(it * 2 * PAIRS, 2 * PAIRS)].rearrange("(n i) s d -> i s n d", i=2)[i],
                                 o_tok[64 * i:64 * i + 64, :].rearrange("p (n d) -> p n d", n=PAIRS)
                                 ).then_inc(a["stored"], 16)

            load(0)
            with sp.Fori(1, STEPS) as it:
                load(it)
                store(it - 1)
            store(STEPS - 1)
            wait(sp, a["stored"], 32 * STEPS)

        def attention_pool(pool):
            wait(pool, "mix_done", LAYERS * GROUPS)
            nc.gpsimd.memset(ones, 1.0).then_inc(a["ones"], 1)

        s_flat, f_flat = (t[:, :, :].rearrange("p a n -> p (a n)") for t in (ps_s, ps_f))

        def attention_tensor(pe):
            mm = nc.tensor.matmul
            pe.wait_ge(a["const"], a_consts[0])
            pe.wait_ge(a["ones"], 1)
            pe.wait_ge(a["split"], 3)

            def turn(dst, src, rows, width):
                for n in range(PAIRS):
                    last = mm(dst[0:width, 128 * n:128 * n + 128], src[:, width * n:width * n + width], ident[:, :],
                              start=True, stop=True)
                return last

            def down(i, t):
                c, e = t // E, t % E
                wait(pe, a["gw"], i * 2 * E + t + 1)
                if e == 0:
                    wait(pe, a["yc"], 2 * i + c)
                    mm(ps[3][0:D, :], e_b2, w_t[:, 512 * c:512 * c + 512], start=True, stop=False)
                mm(ps[3][0:D, :], e_w2[:, e, :], hidw[t % 2], start=False, stop=(e == E - 1)).then_inc(a["down"], 1)

            def experts(i, t0, t1):
                for t in range(t0, t1):
                    c, e = t // E, t % E
                    if t == 0:
                        pe.wait_ge(a["flow"], i + 1)
                    wait(pe, a["gw"], i * 2 * E + t - 1)
                    for part in range(2):
                        last = mm(ps[t % 2][:, :], w1_hl[:, part, e, :], feat_hl[:, 512 * c:512 * c + 512],
                                  start=(part == 0), stop=(part == 1))
                    last.then_inc(a["up"], 1)
                    wait(pe, a["gw"], i * 2 * E + t)
                    if t == 0:
                        wait(pe, a["out"], i)
                        pe.wait_ge(a["wlow"], i + 1)
                    mm(ps[2][:, :], pick_hl[:, e, :], w_hl[:, 512 * c:512 * c + 512], start=True, stop=True).then_inc(a["bc"], 1)
                    if t:
                        down(i, t - 1)
                    if t == 2 * E - 1:
                        down(i, t)

            def turn_sum(i):
                wait(pe, a["yc"], 2 * i + 2)
                for n in range(PAIRS):
                    last = mm(ps[2][:, 64 * n:64 * n + 64], y_t[:, 128 * n:128 * n + 128], ident[0:D, 0:D], start=True, stop=True)
                last.then_inc(a["yt"], 1)

            def attention(it, both):
                bank_a, bank_b = ps_s[:, 0, :], ps_f[:, 0, :]
                pe.wait_ge(a["in"], 32 * it + 32)
                then(pe, a["w"], it)
                for n in range(PAIRS):
                    for i in range(2):
                        r = slice(64 * i, 64 * i + 64)
                        last = mm(bank_a[r, 64 * n:64 * n + 64], tok_t[r, 64 * n:64 * n + 64], ident[r, r], start=True, stop=True)
                last.then_inc(a["h"], 1)
                if both:
                    experts(it - 1, 0, 3)
                wait(pe, a["wlow"], it)
                pe.wait_ge(a["nrm"], it + 1)
                turn(f_flat, nrm, 128, D).then_inc(a["nrmt"], 1)
                if both:
                    experts(it - 1, 3, 4)
                then(pe, a["nrmtc"], it + 1)
                for c in range(2):
                    last = mm(ps_s[0:D, c, :], q_wt, nrm_t[:, 512 * c:512 * c + 512], start=True, stop=True)
                last.then_inc(a["q"], 1)
                for c in range(2):
                    last = mm(ps_f[0:D, c, :], k_wt, nrm_t[:, 512 * c:512 * c + 512], start=True, stop=True)
                last.then_inc(a["k"], 1)
                if both:
                    experts(it - 1, 4, 5)
                then(pe, a["qc"], it + 1)
                for i in range(2 * PAIRS):
                    last = mm(s_flat[0:D, 64 * i:64 * i + 64], nrm_t[:, 64 * i:64 * i + 64], v_wt, start=True, stop=True)
                last.then_inc(a["v"], 1)
                then(pe, a["kc"], it + 1)
                for n in range(PAIRS):
                    for i in range(2):
                        c = slice(128 * n + 64 * i, 128 * n + 64 * i + 64)
                        dst = bank_b[64 * i:64 * i + 64, 64 * n:64 * n + 64]
                        mm(dst, q2_t[:, c], k_t[:, c], start=True, stop=False)
                        mm(dst, ones, ks_t[:, c], start=False, stop=False)
                        last = mm(dst, qs_t[:, c], ones, start=False, stop=True)
                last.then_inc(a["s"], 1)
                if both:
                    experts(it - 1, 5, 6)
                pe.wait_ge(a["vc"], it + 1)
                pe.wait_ge(a["pn"], it + 1)
                turn(s_flat, pnorm, 128, 64).then_inc(a["pt"], 1)
                if both:
                    experts(it - 1, 6, 7)
                then(pe, a["ptc"], it + 1)
                for i in range(2 * PAIRS):
                    c = slice(64 * i, 64 * i + 64)
                    last = mm(f_flat[0:D, c], v_tok[:, c], prob_t[:, c], start=True, stop=True)
                last.then_inc(a["at"], 1)
                if both:
                    experts(it - 1, 7, 9)
                pe.wait_ge(a["atc"], it + 1)
                for n in range(PAIRS):
                    last = mm(bank_a[:, 64 * n:64 * n + 64], att_t[:, 128 * n:128 * n + 128], o_wt, start=True, stop=True)
                last.then_inc(a["o"], 1)
                if both:
                    experts(it - 1, 9, 2 * E)
                pe.wait_ge(a["feat"], it + 1)
                turn(f_flat, feat, 128, D).then_inc(a["featt"], 1)
                if both:
                    turn_sum(it - 1)
                pe.wait_ge(a["feattc"], it + 1)
                for n in range(PAIRS):
                    last = mm(bank_a[:, E * n:E * n + E], feat_t[:, 128 * n:128 * n + 128], r_w, start=True, stop=True)
                last.then_inc(a["logit"], 1)
                pe.wait_ge(a["flow"], it + 1)
                pe.wait_ge(a["w"], it + 1)
                turn(f_flat, wfull, 128, E).then_inc(a["wt"], 1)

            run_steps(pe, attention, experts)
            turn_sum(STEPS - 1)

        def attention_scalar(act):
            af = nc.scalar.activation
            act.wait_ge(a["const"], a_consts[0])
            af(q_b2, q_b, ACT.Copy, scale=-2.0).then_inc(a["qb2"], 1)
            act.wait_ge(a["qb2"], 1)

            def experts(i, t0, t1):
                for t in range(t0, t1):
                    act.wait_ge(a["up"], i * 2 * E + t + 1)
                    wait(act, a["gw"], i * 2 * E + t - 1)
                    af(hid[t % 2], ps[t % 2][:, :], ACT.Gelu, bias=e_b1[:, t % E:t % E + 1]).then_inc(a["g"], 1)
                    if t == E:
                        keep_sum(i, 0)
                    if t == 2 * E - 1:
                        keep_sum(i, 1)

            def keep_sum(i, c):
                wait(act, a["down"], (2 * i + c + 1) * E)
                wait(act, a["yt"], i)
                af(y_t[:, 512 * c:512 * c + 512], ps[3][0:D, :], ACT.Copy).then_inc(a["yc"], 1)

            def attention(it, both):
                if both:
                    experts(it - 1, 0, 3)
                act.wait_ge(a["nrmt"], it + 1)
                af(nrm_t, f_flat[0:D, :], ACT.Copy).then_inc(a["nrmtc"], 1)
                if both:
                    experts(it - 1, 3, 4)
                act.wait_ge(a["q"], it + 1)
                af(q2_t, s_flat[0:D, :], ACT.Identity, bias=q_b2, scale=-2.0)
                af(qs_t, s_flat[0:D, :], ACT.Square, bias=q_b).then_inc(a["qc"], 1)
                act.wait_ge(a["k"], it + 1)
                af(k_t, f_flat[0:D, :], ACT.Identity, bias=k_b)
                af(ks_t, f_flat[0:D, :], ACT.Square, bias=k_b).then_inc(a["kc"], 1)
                if both:
                    experts(it - 1, 4, 5)
                act.wait_ge(a["d2"], it + 1)
                af(dist, d2, ACT.Sqrt).then_inc(a["dist"], 1)
                act.wait_ge(a["dm"], it + 1)
                af(prob, d2, ACT.Exp, scale=-1.0 / D ** 0.5).then_inc(a["p"], 1)
                if both:
                    experts(it - 1, 5, 6)
                act.wait_ge(a["pt"], it + 1)
                af(prob_t, s_flat[0:D, :], ACT.Copy).then_inc(a["ptc"], 1)
                if both:
                    experts(it - 1, 6, 7)
                act.wait_ge(a["at"], it + 1)
                af(att_t, f_flat[0:D, :], ACT.Copy).then_inc(a["atc"], 1)
                if both:
                    experts(it - 1, 7, 2 * E)
                act.wait_ge(a["featt"], it + 1)
                wait(act, a["down"], 2 * E * it)
                af(feat_t, f_flat[0:D, :], ACT.Copy).then_inc(a["feattc"], 1)
                af(feat_hl[0:D, :], f_flat[0:D, :], ACT.Copy).then_inc(a["fhigh"], 1)
                act.wait_ge(a["ex"], it + 1)
                af(expw, mask, ACT.Exp).then_inc(a["exc"], 1)
                act.wait_ge(a["wt"], it + 1)
                af(w_t, f_flat[0:E, :], ACT.Copy)
                af(w_hl[0:E, :], f_flat[0:E, :], ACT.Copy).then_inc(a["wtc"], 1)

            run_steps(act, attention, experts)

        def attention_vector(dve, newton):
            v_ = nc.vector

            def groups(t, w=D):
                return t.rearrange("p (n d) -> p n d", d=w)

            def spread(t, w=D):
                return t.unsqueeze(2).to_broadcast([128, PAIRS, w])

            def row(t, rows=128, n=PAIRS):
                return t.unsqueeze(1).to_broadcast([rows, n, t.shape[-1]])

            def experts(i, t0, t1):
                for t in range(t0, t1):
                    dve.wait_ge(a["g"], i * 2 * E + t + 1)
                    dve.wait_ge(a["bc"], i * 2 * E + t + 1)
                    wait(dve, a["down"], i * 2 * E + t - 1)
                    v_.tensor_tensor(hidw[t % 2], hid[t % 2], ps[2][:, :], ALU.mult).then_inc(a["gw"], 1)

            def low_weights(i):
                dve.wait_ge(a["wtc"], i + 1)
                v_.tensor_tensor(w_hl[32:40, :], f_flat[0:E, :], w_hl[0:E, :].bitcast(f32), ALU.subtract).then_inc(a["wlow"], 1)

            def last_experts(i, t0, t1):
                low_weights(i)
                experts(i, t0, t1)

            def add_sum(i):
                wait(dve, a["yt"], i + 1)
                v_.tensor_tensor(o_tok, ps[2][:, :], o_tok, ALU.add).then_inc(a["out"], 1)

            def attention(it, both):
                c = [0]

                def link(ins):
                    c[0] += 1
                    ins.then_inc(a["step"], 1)
                    dve.wait_ge(a["step"], it * DVE_STEPS + c[0])

                def norm(dst, src, t):
                    link(v_.tensor_reduce(a_mean, groups(src), AX.X, ALU.add))
                    link(v_.tensor_scalar(a_mean, a_mean, 1.0 / D, None, ALU.mult))
                    link(v_.tensor_tensor(groups(cen), groups(src), spread(a_mean), ALU.subtract))
                    if both and t is not None:
                        experts(it - 1, t, t + 1)
                    link(v_.tensor_tensor(sqr, cen, cen, ALU.mult))
                    link(v_.tensor_reduce(a_var, groups(sqr), AX.X, ALU.add))
                    if both and t is not None:
                        experts(it - 1, t + 1, t + 2)
                    v_.tensor_scalar(a_var, a_var, 1.0 / D, EPS, ALU.mult, ALU.add).then_inc(a["step"], 1)
                    newton(dve, a["step"], it * DVE_STEPS + c[0] + 1, a_rs, a_nt, a_var)
                    c[0] += 12
                    dve.wait_ge(a["step"], it * DVE_STEPS + c[0])
                    return v_.tensor_tensor(groups(dst), groups(cen), spread(a_rs), ALU.mult)

                if both:
                    low_weights(it - 1)
                wait(dve, a["h"], it + 1)
                link(v_.tensor_copy(h_tok, ps_s[:, 0, :]))
                norm(nrm, h_tok, 0).then_inc(a["nrm"], 1)
                if both:
                    experts(it - 1, 2, 4)
                dve.wait_ge(a["v"], it + 1)
                v_.tensor_tensor(groups(v_tok), groups(s_flat[0:D, :]), row(v_b, D, 2 * PAIRS), ALU.add).then_inc(a["vc"], 1)
                if both:
                    experts(it - 1, 4, 5)
                dve.wait_ge(a["s"], it + 1)
                v_.tensor_scalar(d2, ps_f[:, 0, :], 0.0, None, ALU.max).then_inc(a["d2"], 1)
                dve.wait_ge(a["dist"], it + 1)
                link(v_.tensor_reduce(a_mean, groups(dist), AX.X, ALU.min))
                v_.tensor_tensor(groups(d2), groups(dist), spread(a_mean), ALU.subtract).then_inc(a["dm"], 1)
                dve.wait_ge(a["p"], it + 1)
                link(v_.tensor_reduce(a_var, groups(prob), AX.X, ALU.add))
                link(v_.reciprocal(a_rs, a_var))
                v_.tensor_tensor(groups(pnorm), groups(prob), spread(a_rs), ALU.mult).then_inc(a["pn"], 1)
                if both:
                    experts(it - 1, 5, 9)
                dve.wait_ge(a["o"], it + 1)
                link(v_.tensor_tensor(h_res, ps_s[:, 0, :], h_tok, ALU.add))
                link(v_.tensor_tensor(groups(h_res), groups(h_res), row(o_b), ALU.add))
                link(norm(nrm2, h_res, 9))
                if both:
                    experts(it - 1, 11, 12)
                link(norm(nrm2, nrm2, 12))
                if both:
                    experts(it - 1, 14, 16)
                link(v_.tensor_tensor(groups(feat), groups(nrm2), row(gamma), ALU.mult))
                v_.tensor_tensor(groups(feat), groups(feat), row(beta), ALU.add).then_inc(a["feat"], 1)
                if both:
                    add_sum(it - 1)
                dve.wait_ge(a["fhigh"], it + 1)
                v_.tensor_tensor(feat_hl[D:128, :], f_flat[0:D, :], feat_hl[0:D, :].bitcast(f32), ALU.subtract
                                 ).then_inc(a["flow"], 1)
                dve.wait_ge(a["logit"], it + 1)
                link(v_.tensor_tensor(groups(logit, E), groups(ps_s[:, 0, 0:PAIRS * E], E), row(r_b), ALU.add))
                mine = groups(logit, E).unsqueeze(3).to_broadcast([128, PAIRS, E, E])
                other = groups(logit, E).unsqueeze(2).to_broadcast([128, PAIRS, E, E])
                four = lambda t: t.rearrange("p (n e f) -> p n e f", e=E, f=E)
                v_.tensor_tensor(four(beats), other, mine, ALU.is_gt)
                link(v_.tensor_tensor(four(ties), other, mine, ALU.is_equal))
                link(v_.tensor_tensor(groups(ties, E * E), groups(ties, E * E), row(lower), ALU.mult))
                link(v_.tensor_tensor(beats, beats, ties, ALU.add))
                link(v_.tensor_reduce(wfull, four(beats), AX.X, ALU.add))
                link(v_.tensor_reduce(a_mean, groups(logit, E), AX.X, ALU.max))
                v_.tensor_tensor(groups(mask, E), groups(logit, E), spread(a_mean, E), ALU.subtract).then_inc(a["ex"], 1)
                dve.wait_ge(a["exc"], it + 1)
                link(v_.scalar_tensor_tensor(wfull, wfull, 1.5, expw, ALU.is_lt, ALU.mult))
                link(v_.tensor_reduce(a_var, groups(wfull, E), AX.X, ALU.add))
                link(v_.reciprocal(a_rs, a_var))
                v_.tensor_tensor(groups(wfull, E), groups(wfull, E), spread(a_rs, E), ALU.mult).then_inc(a["w"], 1)
                wait(dve, a["stored"], 32 * it)
                link(v_.tensor_copy(o_tok, h_res))
                assert c[0] == DVE_STEPS, c[0]

            dve.wait_ge(a["const"], a_consts[0])
            dve.wait_ge(s["y_done"], UNITS * QUADS * (LAYERS + 1))
            dve.wait_ge(s["fc1_done"], 4 * UNITS * QUADS)
            v_.memset(w_hl.bitcast(f32), 0.0)
            v_.memset(pick_hl[:, :, :].bitcast(f32), 0.0).then_inc(a["split"], 1)
            dve.wait_ge(a["split"], 1)
            for r in (slice(0, E), slice(32, 32 + E)):
                v_.tensor_copy(pick_hl[r, :, :], pick)
            for r in (slice(0, D), slice(D, 2 * D)):
                last = v_.tensor_copy(w1_hl[r, 0, :, :], e_w1)
            last.then_inc(a["split"], 1)
            dve.wait_ge(a["split"], 2)
            for r in (slice(0, D), slice(D, 2 * D)):
                last = v_.tensor_tensor(w1_hl[r, 1, :, :], e_w1, w1_hl[0:D, 0, :, :].bitcast(f32), ALU.subtract)
            last.then_inc(a["split"], 1)
            run_steps(dve, attention, last_experts)
            add_sum(STEPS - 1)

        @block.sync
        def _(sp):
            plain = [
                (ident[:, :], cst["ident"]), (c_center[:, :], cst["center"]), (c_fwh[:, :], cst["fwd_h"]),
                (c_fww[:, :, :], cst["fwd_w"]), (c_inw[:, :, :], cst["inv_w"]), (c_inh, cst["inv_h"]),
                (c_sign[:, :], cst["sign"]),
                (fc0_t[:, 0:3], p["tok_fc0_w"].rearrange("c o -> o c")), (fc0_t[:, 3:4], p["tok_fc0_b"].unsqueeze(1)),
                (conv_w[:, :, :], p["tok_conv_w"].rearrange("l o c -> o l c")),
                (fc1_b[:, :], p["tok_fc1_b"].unsqueeze(1)), (fc2_w[:, :], p["tok_fc2_w"]),
                (fc2_b[0:64, :], p["tok_fc2_b"].unsqueeze(1)), (fc2_b[64:128, :], p["tok_fc2_b"].unsqueeze(1)),
                (fc3_b[:, :], p["tok_fc3_b"].unsqueeze(0).to_broadcast([64, 1]))]
            for g in range(4):
                r = slice(32 * g, 32 * g + 32)
                plain += [(g_all[r, 0, 0:1], p["tok_ln0_g"].unsqueeze(1)), (g_all[r, 1, 0:1], p["tok_ln0_b"].unsqueeze(1)),
                          (g_all[r, 0, 1:5], p["tok_ln_g"].rearrange("l c -> c l")),
                          (g_all[r, 1, 1:5], p["tok_ln_b"].rearrange("l c -> c l"))]
            plain += [(fc1_w[32 * g:32 * g + 32, :], p["tok_fc1_w"]) for g in range(4)]
            placed = [(bias_raw[0:32, :], p["tok_conv_b"].rearrange("l o -> o l"))]
            placed += [(fc3_w[64 * g:64 * g + 64, g:g + 1], p["tok_fc3_w"]) for g in range(2)]
            for dst, src in plain:
                sp.dma_start(dst, src, allow_slow_non_contiguous=True).then_inc(s["const_in"], 16)
            sp.wait_ge(s["const_zero"], 1)
            for dst, src in placed:
                sp.dma_start(dst, src, allow_slow_non_contiguous=True).then_inc(s["const_in"], 16)
            consts.append(16 * len(plain + placed))
            sp.wait_ge(s["fc0_copied"], 1)
            sp.dma_start(fc0_rows, fc0_c[:, :]).then_inc(s["fc0_stored"], 16)
            sp.wait_ge(s["fc0_stored"], 16)
            for wq in range(4):
                for w in range(4):
                    r, c = (wq * 4 + w) * 3, (w * 4 + wq) * 32
                    sp.dma_start(fc0_bd[r:r + 3, c:c + 32], fc0_rows[0:3, :]).then_inc(s["fc0_placed"], 16)
                    sp.dma_start(fc0_bd[48:49, c:c + 32], fc0_rows[3:4, :]).then_inc(s["fc0_placed"], 16)

            def load_x(n):
                then(sp, "x_ready", n)
                for ip in range(2):
                    sp.dma_start(x_in[:, ip, :], x[bass.ds(4 * n + 2 * ip, 2)].rearrange("i h w c -> (i h) (w c)")
                                 ).then_inc(s["x_loaded"], 16)

            def load_h(q, n, j):
                then(sp, "y_done", (n - 1) * UNITS + 4 * j + 4)
                sp.dma_start(h_in[j], hstore[bass.ds(q, 1), :, j, :].rearrange("a p n -> (a p) n")
                             ).then_inc(h_loaded[j], 16)

            def load_y(q, n):
                then(sp, "yc_done", n - QUADS)
                sp.dma_start(y_raw[:, :], ymodes[bass.ds(q, 1)].rearrange("a p n -> (a p) n")
                             ).then_inc(s["yraw_loaded"], 16)

            def store_h(q, n, j):
                then(sp, s["act_done"], n * UNITS + 4 * j + 4)
                sp.dma_start(hstore[bass.ds(q, 1), :, j, :].rearrange("a p n -> (a p) n"), h_new[j]
                             ).then_inc(h_stored[j], 16)

            def store_modes(q, n):
                then(sp, s["xout_done"], n + 1)
                sp.dma_start(xmodes[bass.ds(q, 1)].rearrange("a p n -> (a p) n"),
                             x_out[:, :, :, :].rearrange("p a k m -> p (a k m)")).then_inc(s["xmodes_stored"], 16)

            def store_tok(q, n, j):
                then(sp, s["tok_done"], (n - LAYERS * QUADS) * UNITS + 4 * j + 4)
                for g in range(2):
                    sp.dma_start(tok[bass.ds(4 * q, 4), 2 * g:2 * g + 2, 512 * j:512 * j + 512].rearrange("i r n -> r i n"),
                                 tok_sb[32 * g:32 * g + 2, :].rearrange("r (i j n) -> r j i n", i=4, j=2)[:, j]
                                 ).then_inc(tok_stored[j], 16)

            def body(kind, q, n, first, more, drain=False):
                if kind == "stem" and more:
                    load_x(n + 1)
                if kind != "stem" and more:
                    load_y(q + 1, n + 1)
                if not first and kind != "head":
                    store_h(q - 1, n - 1, 0)
                if kind != "stem" and not drain:
                    load_h(q, n, 1)
                if kind == "head" and not first:
                    store_tok(q - 1, n - 1, 0)
                if kind != "stem" and more:
                    load_h(q + 1, n + 1, 0)
                if kind == "head" and not first:
                    store_tok(q - 1, n - 1, 1)
                if kind != "head" and not first:
                    store_h(q - 1, n - 1, 1)
                    store_modes(q - 1, n - 1)

            def mix(ph):
                then(sp, s["xmodes_stored"], 16 * QUADS * ph)
                for j in range(2):
                    then(sp, h_stored[j], 16 * QUADS * ph)
                for c in range(COMP):
                    sp.dma_start(modes[32 * c:32 * c + 32, :, :],
                                 xmodes.rearrange("q (i c) (a m) -> a c (q i) m", i=4, a=COMP)[c]
                                 ).then_inc(s["modes_loaded"], 16)
                then(sp, s["mix_act"], 21 * ph)
                then(sp, s["mix_dve"], 19 * ph)
                for c in range(COMP):
                    sp.dma_start(ymodes.rearrange("q (i c) (a m) -> a c (q i) m", i=4, a=COMP)[c],
                                 modes[32 * c:32 * c + 32, :, :]).then_inc(s["ymodes_stored"], 16)
                then(sp, s["ymodes_stored"], 16 * COMP * ph)
                load_y(0, ph * QUADS)
                load_h(0, ph * QUADS, 0)

            load_x(0)
            run_phase(sp, 0, "stem", body)
            with sp.Fori(1, LAYERS) as ph:
                mix(ph)
                run_phase(sp, ph * QUADS, "layer", body)
            mix(LAYERS)
            attention_load(sp)
            run_phase(sp, LAYERS * QUADS, "head", body)
            for j in range(2):
                wait(sp, tok_stored[j], 32 * QUADS)
            attention_sync(sp)

        @block.gpsimd
        def _(pool):
            for which, start in primed:
                pool.sem_inc(which, start)
            for t in (fc3_w[:, :], fc0_bd, bias_raw[:, :], conv_bd[:, :, :], y_kk[:, :]):
                nc.gpsimd.memset(t, 0.0)
            nc.gpsimd.memset(x_tr, 1.0).then_inc(s["const_zero"], 1)

            def weights(l):
                r = 0
                for slots, parts in (((0, 3), "riir"), ((1, 2), "irri")):
                    for oc in range(CH // OCH):
                        o0, rnd = oc * OCH, l * ROUNDS + r
                        for c, part in enumerate(parts):
                            rows = slice(32 * c, 32 * c + 32)
                            for dst, src in ((w1_raw, p[f"tok_w1{part}"]), (w2_raw, p[f"tok_w2{part}"])):
                                pool.dma_start(dst[rows, :, :].rearrange("p o m -> p (o m)"),
                                               src[bass.ds(l, 1), :, o0:o0 + OCH].rearrange("l i o k m -> (l i) (o k m)")
                                               ).then_inc(s["w_raw"], 16)
                        then(pool, s["w_raw"], 128 * rnd + 128)
                        for i, sl in enumerate(slots):
                            dst = wslot[:, sl, o0:o0 + OCH, :]
                            nc.gpsimd.memset(dst[:, :, M * M:MODES], 0.0)
                            nc.gpsimd.tensor_scalar(dst[:, :, 0:M * M], w1_raw[:, :, :], c_sign[:, sl:sl + 1], None, ALU.mult)
                            nc.gpsimd.tensor_scalar(w2_raw[:, :, :], w2_raw[:, :, :], c_sign[:, 4 + sl:5 + sl], None,
                                                    ALU.mult).then_inc(s["w_step"], 1)
                            then(pool, s["w_step"], 4 * rnd + 2 * i + 1)
                            view = dst[:, :, M:MODES].rearrange("p o (k m) -> p o k m", m=M)
                            rev = w2_raw[:, :, :].rearrange("p o (k m) -> p o k m", m=M)[:, :, ::-1, :]
                            nc.gpsimd.tensor_tensor(view, view, rev, ALU.add).then_inc(s["w_step"], 1)
                            then(pool, s["w_step"], 4 * rnd + 2 * i + 2)
                        r += 1

            pool.wait_ge(s["const_in"], consts[0])
            with pool.Fori(0, LAYERS) as l:
                then(pool, s["mix_done"], l * GROUPS)
                weights(l)
            attention_pool(pool)

        @block.tensor
        def _(pe):
            mm = nc.tensor.matmul
            pe.wait_ge(s["const_in"], consts[0])
            pe.wait_ge(s["const_zero"], 1)
            mm(ps_t1[0:4, 0:32], fc0_t[:, :], c_center[0:32, 0:32], start=True, stop=True).then_inc(s["fc0_center"], 1)
            for g in range(4):
                for l in range(LAYERS):
                    last = mm(ps_t2[32 * g:32 * g + 32, 32 * l:32 * l + 32], conv_w[:, l, :], c_center[0:32, 0:32],
                              start=True, stop=True)
            last.then_inc(s["conv_center"], 1)
            pe.wait_ge(s["fc0_placed"], 16 * 32)
            pe.wait_ge(s["conv_placed"], 1)
            pe.wait_ge(s["table_split"], 5)

            def turn_x(n, k):
                g, ip = k // 2, k % 2
                if k == 0:
                    pe.wait_ge(s["x_ready"], n + 1)
                if k == 1:
                    wait(pe, "fw_read", n - 1)
                wait(pe, "x_copied", n * UNITS + k)
                mm(ps_s[0:48, 0, 0:128], x_cur[:, ip, 48 * g:48 * g + 48], ident[:, :], start=True, stop=True).then_inc(s["x_turned"], 1)

            def center(n):
                i = n - QUADS
                wait(pe, "yraw_loaded", 16 * i + 16)
                wait(pe, "iw_read", 2 * i)
                for sx in range(2):
                    last = mm(ps_s[:, sx, 0:312], c_center[:, :], y_raw[:, 312 * sx:312 * sx + 312], start=True, stop=True)
                last.then_inc(s["yc_done"], 1)

            def inv_w(n, j, forward):
                i = n - QUADS
                wait(pe, "ykt_done", i + 1)
                if j == 1:
                    wait(pe, "iw_read", 2 * i + 1)
                    if forward:
                        wait(pe, "fw_read", n - 1)
                for sx in range(2):
                    last = mm(ps_s[:, sx, 0:KX * 32], c_inw[:, j, :], y_kt[:, 512 * sx:512 * sx + KX * 32],
                              start=True, stop=True)
                last.then_inc(s["iw_done"], 1)

            def start_layer(n):
                wait(pe, "fw_read", n)
                center(n)
                inv_w(n, 0, False)

            def body(kind, q, n, first, more, drain=False):
                for k in range(UNITS):
                    u = n * UNITS + k
                    j, g, ip = k // 4, k // 2, k % 2
                    if not drain:
                        if kind == "stem":
                            if k < 7:
                                turn_x(n, k + 1)
                            elif more:
                                turn_x(n + 1, 0)
                            pe.wait_ge(s["x_copied"], u + 1)
                            wait(pe, "y_read", u - 1)
                            mm(ps_y[k % 2][:, :], x_tr[0:49, k % 2, :], fc0_bd[0:49, :],
                               start=True, stop=True).then_inc(s["y_done"], 1)
                        else:
                            if k % 4 == 0:
                                wait(pe, "z_done", 2 * (n - QUADS) + j + 1)
                                wait(pe, h_loaded[j], 16 * (n - QUADS) + 16)
                            wait(pe, "y_read", u - 1)
                            for part in range(2):
                                mm(ps_y[k % 2][:, :], c_inh_hl[:, part, :], z_hl[:, ip, j, 512 * (g % 2):512 * (g % 2) + 512],
                                   start=(part == 0), stop=False)
                            for w in range(4):
                                at = ((g % 2) * 4 + w) * 256 + ip * 128
                                last = mm(ps_y[k % 2][:, 128 * w:128 * w + 128], h_in[j][:, at:at + 128], conv_now[:, :],
                                          start=False, stop=(w == 3))
                            last.then_inc(s["y_done"], 1)
                            if more and k == 2:
                                center(n + 1)
                    if kind != "head" and k % 2 == 0 and not first:
                        pe.wait_ge(s["px_done"], (n - 1) * UNITS + k + 2)
                        if k % 4 == 0:
                            wait(pe, "tw_done", 2 * (n - 1) + k // 4)
                        for i in range(2):
                            mm(ps_f[64 * i:64 * i + 64, (k // 2) % 2, :], c_fwh[:, :], h_px[(k + i) % 4],
                               start=True, stop=True).then_inc(s["f_done"], 1)
                    if kind != "head" and there(k, LAG_T2, first, drain):
                        v, kk = u - LAG_T2, (k - LAG_T2) % 8
                        pe.wait_ge(s["act_done"], v + 1)
                        wait(pe, "px_done", v)
                        for w in range(4):
                            at = (((kk // 2) % 2) * 4 + w) * 256 + (kk % 2) * 128
                            last = nc.tensor.transpose(ps_t2[:, 128 * w:128 * w + 128], h_new[kk // 4][:, at:at + 128],
                                                       ident[:, :])
                        last.then_inc(s["t2_done"], 1)
                    if kind != "stem" and more and k == 5:
                        inv_w(n + 1, 0, False)
                    if there(k, LAG_T1, first, drain):
                        v = u - LAG_T1
                        pe.wait_ge(s["xhat_done"], v + 1)
                        wait(pe, "act_done", v)
                        if kind == "head":
                            wait(pe, "tok_done", v - 2 - UNITS * QUADS * LAYERS)
                        for w in range(4):
                            last = nc.tensor.transpose(ps_t1[:, 128 * w:128 * w + 128],
                                                       xhat[(k - LAG_T1) % 2][:, 128 * w:128 * w + 128], ident[:, :])
                        last.then_inc(s["t1_done"], 1)
                    if kind != "stem" and not drain and k == 0:
                        inv_w(n, 1, kind == "layer")
                    if kind == "head":
                        head_unit(u, k, first, drain)
                        continue
                    if k == 7 and not first:
                        fwd_w(kind, n, u, more, drain)

            def fwd_w(kind, n, u, more, drain):
                wait(pe, "tw_done", 2 * n)
                if kind == "stem":
                    pe.wait_ge(s["x_copied"], u + 2 if more else (UNITS * QUADS if drain else u + 1))
                else:
                    wait(pe, "iw_read", 2 * (n - QUADS) + (3 if more else (0 if drain else 2)))
                wait(pe, "fw_read", n - 1)
                for sx in range(2):
                    for j in range(2):
                        last = mm(ps_s[:, sx, 0:KX * 32], c_fww[:, j, :], t_w[:, j, 512 * sx:512 * sx + KX * 32],
                                  start=(j == 0), stop=(j == 1))
                last.then_inc(s["fw_done"], 1)

            def fc1(v, pr):
                pe.wait_ge(s["x_split"], 2 * v + pr + 1)
                for i in range(2):
                    wait(pe, "g1_done", 4 * v + 2 * pr + i - 1)
                    dst = ps_f[:, 0, :] if i else ps_t2[:, :]
                    for part in range(2):
                        last = mm(dst, fc1_hl[:, i, part, :], x_hl[:, pr, :], start=(part == 0), stop=(part == 1))
                    last.then_inc(s["fc1_done"], 1)

            def fc2(v, pr):
                pe.wait_ge(s["g1_done"], 4 * v + 2 * pr + 2)
                wait(pe, "g2_done", 2 * v + pr)
                for i in range(2):
                    last = mm(ps_f[64 * i:64 * i + 64, 1, :], fc2_w[:, :], gelu1[2 * pr + i], start=True, stop=True)
                last.then_inc(s["fc2_done"], 1)

            def fc3(v, vb):
                pe.wait_ge(s["g2_done"], 2 * v + 2)
                for pr in range(2):
                    last = mm(ps_t1[32 * pr:32 * pr + 32, :], fc3_w[:, :], gelu2[2 * vb + pr], start=True, stop=True)
                last.then_inc(s["fc3_done"], 1)

            def head_unit(u, k, first, drain):
                v = u - LAG_T2 - UNITS * QUADS * LAYERS
                vb = (k - LAG_T2) % 2
                now, before = there(k, LAG_T2, first, drain), there(k, LAG_T2 + 1, first, drain)
                if now:
                    fc1(v, 0)
                if before:
                    fc2(v - 1, 1)
                if now:
                    fc1(v, 1)
                if before:
                    pe.wait_ge(s["act_done"], u - LAG_T1 + 1 - (k - LAG_T1 + 1 if drain and k >= LAG_T1 else 0))
                    wait(pe, "tok_done", v - 1)
                    fc3(v - 1, 1 - vb)
                if now:
                    fc2(v, 0)

            def mix(ph):
                pe.wait_ge(s["modes_loaded"], 16 * COMP * ph)
                pe.wait_ge(s["w_step"], 4 * ROUNDS * ph)
                pe.wait_ge(s["px_done"], UNITS * QUADS * ph)
                for t in range(GROUPS):
                    if t >= 4:
                        if t % 2 == 0:
                            pe.wait_ge(s["mix_act"], (ph - 1) * 21 + t // 2)
                        else:
                            pe.wait_ge(s["mix_dve"], (ph - 1) * 19 + t // 2 - 1)
                    for m in range(4):
                        last = mm(ps[t % 4][:, 128 * m:128 * m + 128], wslot[:, :, :, 4 * t + m], modes[:, :, 4 * t + m],
                                  start=True, stop=True)
                    last.then_inc(s["mix_done"], 1)

            turn_x(0, 0)
            run_phase(pe, 0, "stem", body)
            with pe.Fori(1, LAYERS) as ph:
                mix(ph)
                start_layer(ph * QUADS)
                run_phase(pe, ph * QUADS, "layer", body)
            mix(LAYERS)
            start_layer(LAYERS * QUADS)
            run_phase(pe, LAYERS * QUADS, "head", body)
            attention_tensor(pe)

        @block.scalar
        def _(act):
            af = nc.scalar.activation
            act.wait_ge(s["const_in"], consts[0])

            def take_x(n):
                act.wait_ge(s["x_loaded"], 32 * n + 32)
                wait(act, "x_turned", UNITS * n)
                for ip in range(2):
                    last = af(x_cur[:, ip, :].rearrange("p (g q w) -> p q g w", g=4, q=4),
                              x_in[:, ip, :].rearrange("p (q g w) -> p q g w", g=4, q=4), ACT.Copy)
                last.then_inc(s["x_ready"], 1)

            def order_y(n):
                i = n - QUADS
                wait(act, "yc_done", i + 1)
                wait(act, "ykt_done", i)
                for sx in range(2):
                    dst = y_kk[:, 512 * sx:512 * sx + 512].rearrange("p (k r) -> p k r", r=32)[:, 0:KX, 0:2 * M]
                    last = af(dst.rearrange("p k (a m) -> p a k m", a=2),
                              ps_s[:, sx, 0:312].rearrange("p (a k m) -> p a k m", a=2, k=KX), ACT.Copy)
                last.then_inc(s["ykk_done"], 1)

            def high_z(n, j):
                i = n - QUADS
                wait(act, "iw_read", 2 * i + j + 1)
                act.wait_ge(s["y_done"], (n - 1) * UNITS + 4 * j + 4)
                af(z_hl[0:64, 0, j, :], z_kx[0:64, :], ACT.Copy).then_inc(s["z_high"], 1)

            def body(kind, q, n, first, more, drain=False):
                for k in range(UNITS):
                    u = n * UNITS + k
                    if kind == "stem" and k == 7 and more:
                        take_x(n + 1)
                    if kind != "stem" and k == 2 and not drain:
                        high_z(n, 1)
                    if kind != "stem" and k == 6 and more:
                        high_z(n + 1, 0)
                    if not drain:
                        act.wait_ge(s["y_done"], u + 1)
                        wait(act, "ss_done", u - 1)
                        af(y_sq[k % 2], ps_y[k % 2][:, :], ACT.Square).then_inc(s["sq_done"], 1)
                        wait(act, "xhat_done", u - 7)
                        af(y_sb[k], ps_y[k % 2][:, :], ACT.Copy).then_inc(s["y_read"], 1)
                    if kind != "head" and there(k, LAG_T2, first, drain):
                        v = u - LAG_T2
                        act.wait_ge(s["t2_done"], v + 1)
                        wait(act, "f_done", v - 3)
                        af(h_px[(k - LAG_T2) % 4], ps_t2[:, :], ACT.Copy).then_inc(s["px_done"], 1)
                    if there(k, LAG_T1, first, drain):
                        v, kk = u - LAG_T1, (k - LAG_T1) % 8
                        act.wait_ge(s["t1_done"], v + 1)
                        if kind == "head":
                            wait(act, "x_split", 2 * (v - 1 - UNITS * QUADS * LAYERS))
                            af(h_px[kk % 2], ps_t1[:, :], ACT.Identity, bias=g_now[:, 1:2], scale=g_now[:, 0:1]
                               ).then_inc(s["act_done"], 1)
                        else:
                            if kk % 4 == 0:
                                wait(act, h_stored[kk // 4], 16 * (n if k >= LAG_T1 else n - 1))
                            dst = h_new[kk // 4].rearrange("p (w q) -> p w q", w=8)[:, 4 * ((kk // 2) % 2):4 * ((kk // 2) % 2) + 4,
                                                                                    128 * (kk % 2):128 * (kk % 2) + 128]
                            af(dst, ps_t1[:, :].rearrange("p (w q) -> p w q", w=4), ACT.Identity if kind == "stem" else ACT.Gelu,
                               bias=g_now[:, 1:2], scale=g_now[:, 0:1]).then_inc(s["act_done"], 1)
                    if kind == "head":
                        head_unit(u, k, first, drain)
                        if more and k == 2:
                            order_y(n + 1)
                        continue
                    if kind == "layer" and more and k == 2:
                        order_y(n + 1)

            def head_unit(u, k, first, drain):
                v = u - LAG_T2 - UNITS * QUADS * LAYERS
                now, before = there(k, LAG_T2, first, drain), there(k, LAG_T2 + 1, first, drain)

                def g1(v, pr):
                    wait(act, "fc2_done", 2 * (v - 1) + pr + 1)
                    for i in range(2):
                        act.wait_ge(s["fc1_done"], 4 * v + 2 * pr + i + 1)
                        af(gelu1[2 * pr + i], ps_f[:, 0, :] if i else ps_t2[:, :], ACT.Gelu, bias=fc1_b[:, :]
                           ).then_inc(s["g1_done"], 1)

                def g2(v, vb, pr):
                    act.wait_ge(s["fc2_done"], 2 * v + pr + 1)
                    wait(act, "fc3_done", v - 1)
                    af(gelu2[2 * vb + pr], ps_f[:, 1, :], ACT.Gelu, bias=fc2_b[:, :]).then_inc(s["g2_done"], 1)

                vb = (k - LAG_T2) % 2
                if now:
                    g1(v, 0)
                if before:
                    g2(v - 1, 1 - vb, 1)
                if now:
                    g1(v, 1)
                    g2(v, vb, 0)

            def mix(ph):
                act.wait_ge(s["now_done"], ph)
                base = (ph - 1) * GROUPS
                for t in range(0, GROUPS, 2):
                    wait(act, "mix_done", base + t + 1)
                    src = ps[t % 4][:, :].rearrange("p (m i) -> p i m", m=4)
                    if t == 0:
                        af(modes[:, :, 0:1], src[:, :, 0:1], ACT.Identity, bias=bias_now[:, :]).then_inc(s["mix_act"], 1)
                        af(modes[:, :, 1:4], src[:, :, 1:4], ACT.Copy).then_inc(s["mix_act"], 1)
                    else:
                        af(modes[:, :, 4 * t:4 * t + 4], src, ACT.Copy).then_inc(s["mix_act"], 1)

            take_x(0)
            run_phase(act, 0, "stem", body)
            with act.Fori(1, LAYERS) as ph:
                mix(ph)
                act.wait_ge(s["ymodes_stored"], 16 * COMP * ph)
                order_y(ph * QUADS)
                high_z(ph * QUADS, 0)
                run_phase(act, ph * QUADS, "layer", body)
            mix(LAYERS)
            act.wait_ge(s["ymodes_stored"], 16 * COMP * LAYERS)
            order_y(LAYERS * QUADS)
            high_z(LAYERS * QUADS, 0)
            run_phase(act, LAYERS * QUADS, "head", body)
            attention_scalar(act)

        @block.vector
        def _(dve):
            v_ = nc.vector
            dve.wait_ge(s["const_in"], consts[0])
            dve.wait_ge(s["fc0_center"], 1)
            v_.tensor_copy(c_inh_hl[:, 0, :], c_inh).then_inc(s["table_split"], 1)
            v_.memset(ps_s[:, :, KX * 32:512], 0.0).then_inc(s["table_split"], 1)
            v_.memset(fc1_hl[:, :, :, :].bitcast(f32), 0.0).then_inc(s["table_split"], 1)
            dve.wait_ge(s["table_split"], 3)
            blocks = [(64 * half + 32 * i, i) for half in range(2) for i in range(2)]
            for row, i in blocks:
                last = v_.tensor_copy(fc1_hl[row:row + 32, i, 0, :], fc1_w[row:row + 32, :])
            last.then_inc(s["table_split"], 1)
            dve.wait_ge(s["table_split"], 4)
            for row, i in blocks:
                v_.tensor_tensor(fc1_hl[row:row + 32, i, 1, :], fc1_w[row:row + 32, :],
                                 fc1_hl[row:row + 32, i, 0, :].bitcast(f32), ALU.subtract)
            v_.tensor_tensor(c_inh_hl[:, 1, :], c_inh, c_inh_hl[:, 0, :].bitcast(f32), ALU.subtract
                             ).then_inc(s["table_split"], 1)
            v_.tensor_copy(fc0_c[:, :], ps_t1[0:4, 0:32]).then_inc(s["fc0_copied"], 1)
            dve.wait_ge(s["conv_center"], 1)
            dve.wait_ge(s["const_zero"], 1)
            v_.tensor_copy(g_now[:, :], g_all[:, :, 0])
            for g in range(4):
                r = slice(32 * g, 32 * g + 32)
                last = v_.tensor_copy(conv_bd[r, :, 32 * g:32 * g + 32], ps_t2[r, 0:128].rearrange("p (l o) -> p l o", l=LAYERS))
            last.then_inc(s["conv_placed"], 1)

            def copy_x(n, k):
                u = n * UNITS + k
                dve.wait_ge(s["x_turned"], u + 1)
                wait(dve, "y_done", u - 1)
                v_.tensor_copy(x_tr[0:48, k % 2, :], ps_s[0:48, 0, 0:128]).then_inc(s["x_copied"], 1)

            def turn_y(n):
                i = n - QUADS
                wait(dve, "ykk_done", i + 1)
                wait(dve, "iw_done", 2 * i)
                v_.transpose(y_kt[:, :], y_kk[:, :]).then_inc(s["ykt_done"], 1)

            def turn_z(n, j):
                i = n - QUADS
                wait(dve, "iw_done", 2 * i + j + 1)
                wait(dve, "z_done", 2 * i + j)
                v_.transpose(z_kx.rearrange("p (w o) -> p o w", o=32),
                             ps_s[:, :, :].rearrange("p a n -> p (a n)").rearrange("p (k o) -> p o k", o=32)
                             ).then_inc(s["iw_read"], 1)

            def low_z(n, j):
                i = n - QUADS
                dve.wait_ge(s["y_done"], (n - 1) * UNITS + 4 * j + 4)
                wait(dve, "iw_read", 2 * i + j + 1)
                v_.tensor_copy(z_hl[64:128, 1, j, :], z_kx[64:128, :]).then_inc(s["z_high2"], 1)
                wait(dve, "z_high2", 2 * i + j + 1)
                v_.tensor_tensor(z_hl[0:64, 1, j, :], z_kx[64:128, :], z_hl[64:128, 1, j, :].bitcast(f32), ALU.subtract)
                wait(dve, "z_high", 2 * i + j + 1)
                v_.tensor_tensor(z_hl[64:128, 0, j, :], z_kx[0:64, :], z_hl[0:64, 0, j, :].bitcast(f32), ALU.subtract
                                 ).then_inc(s["z_done"], 1)

            def turn_w(n, j):
                wait(dve, "f_done", n * UNITS + 4 * j + 4)
                wait(dve, "fw_done", n)
                v_.transpose(t_w[:, j, :].rearrange("p (k c) -> p c k", c=32),
                             ps_f[:, :, :].rearrange("p a n -> p (a n)").rearrange("p (w c) -> p c w", c=32)
                             ).then_inc(s["tw_done"], 1)

            def body(kind, q, n, first, more, drain=False):
                for k in range(UNITS):
                    u, j = n * UNITS + k, k // 4
                    if kind == "stem" and not drain:
                        if k < 7:
                            copy_x(n, k + 1)
                        elif more:
                            copy_x(n + 1, 0)
                    if there(k, LAG_XH, first, drain):
                        v, kk = u - LAG_XH, (k - LAG_XH) % 8
                        dve.wait_ge(s["y_read"], v + 1)
                        dve.wait_ge(s["norm_step"], 12 * (2 * n + (1 if k >= LAG_XH else 0)))
                        wait(dve, "t1_done", v - 1)
                        v_.tensor_tensor(xhat[kk % 2].rearrange("p (a c) -> p a c", c=32),
                                         y_sb[kk].rearrange("p (a c) -> p a c", c=32),
                                         rstd[:, kk // 4, 16 * (kk % 4):16 * (kk % 4) + 16].unsqueeze(2).to_broadcast([128, 16, 32]),
                                         ALU.mult).then_inc(s["xhat_done"], 1)
                    if kind != "stem" and not drain and k == 2:
                        low_z(n, 1)
                    if kind != "stem" and more and k == 6:
                        low_z(n + 1, 0)
                    if kind != "head" and not first and k in (2, 6):
                        turn_w(n - 1, k // 4)
                    if kind != "stem" and not drain and k == 1:
                        turn_z(n, 1)
                    if not drain:
                        dve.wait_ge(s["sq_done"], u + 1)
                        v_.tensor_reduce(ss[:, j, 16 * (k % 4):16 * (k % 4) + 16], y_sq[k % 2].rearrange("p (a c) -> p a c", c=32),
                                         AX.X, ALU.add).then_inc(s["ss_done"], 1)
                        if kind != "stem" and more and k == 3:
                            turn_y(n + 1)
                        if k % 4 == 3:
                            rsqrt_half(n, k)
                        if kind != "stem" and more and k == 5:
                            turn_z(n + 1, 0)
                    if kind == "head" and there(k, LAG_T2 + 1, first, drain):
                        v, kk = u - LAG_T2 - 1 - UNITS * QUADS * LAYERS, (k - LAG_T2 - 1) % 8
                        dve.wait_ge(s["fc3_done"], v + 1)
                        if kk % 4 == 0:
                            wait(dve, tok_stored[kk // 4], 32 * ((n if k > LAG_T2 else n - 1) - QUADS * LAYERS))
                        dst = tok_sb[:, :].rearrange("p (q i w h) -> p q w i h", q=2, i=2, w=16)[
                            :, kk % 2, 4 * (kk // 2):4 * (kk // 2) + 4, :, :]
                        v_.tensor_scalar(dst, ps_t1[0:64, :].rearrange("p (w i h) -> p w i h", w=4, i=2), fc3_b[:, :], None,
                                         ALU.add).then_inc(s["tok_done"], 1)
                    if kind == "head" and there(k, LAG_T1, first, drain):
                        split_x(u - LAG_T1, (k - LAG_T1) % 8)
                    if kind != "head" and k == 7 and not first:
                        wait(dve, "fw_done", n)
                        wait(dve, "xout_done", n - 1)
                        v_.transpose(fw_sb[:, :], ps_s[:, :, 0:KX * 32]).then_inc(s["fw_read"], 1)
                        wait(dve, "fw_read", n)
                        wait(dve, "xmodes_stored", 16 * (n - 1))
                        for sx in range(2):
                            src = fw_sb[:, 416 * sx:416 * sx + 416].rearrange("p (k r) -> p k r", r=32)[:, :, 0:2 * M]
                            last = v_.tensor_copy(x_out[:, 2 * sx:2 * sx + 2, :, :], src.rearrange("p k (a m) -> p a k m", a=2))
                        last.then_inc(s["xout_done"], 1)

            def split_x(unit, kk):
                v = unit - UNITS * QUADS * LAYERS
                dve.wait_ge(s["act_done"], unit + 1)
                for pr in range(2):
                    r, other = slice(64 * pr, 64 * pr + 64), slice(64 - 64 * pr, 128 - 64 * pr)
                    wait(dve, "fc1_done", 4 * (v - 1) + 2 * pr + 2)
                    v_.tensor_copy(x_hl[r, pr, :], h_px[kk % 2][r, :]).then_inc(s["x_high"], 1)
                    dve.wait_ge(s["x_high"], 2 * v + pr + 1)
                    v_.tensor_tensor(x_hl[other, pr, :], h_px[kk % 2][r, :], x_hl[r, pr, :].bitcast(f32), ALU.subtract
                                     ).then_inc(s["x_split"], 1)

            def rsqrt_half(n, k):
                j = k // 4
                at = 12 * (2 * n + j)
                dve.wait_ge(s["ss_done"], n * UNITS + k + 1)
                v_.tensor_scalar(var[:, :], ss[:, j, :], 1.0 / CH, EPS, ALU.mult, ALU.add).then_inc(s["norm_step"], 1)
                newton(dve, s["norm_step"], at + 1, rstd[:, j, :], nt[:, :], var[:, :])

            def newton(eng, step, at, r, t, v):
                eng.wait_ge(step, at)
                v_.tensor_scalar(t.bitcast(i32), v.bitcast(i32), 1, None, ALU.logical_shift_right).then_inc(step, 1)
                eng.wait_ge(step, at + 1)
                v_.tensor_scalar(r.bitcast(i32), t.bitcast(i32), -1, 0x5F3759DF, ALU.mult, ALU.add).then_inc(step, 1)
                for i in range(3):
                    eng.wait_ge(step, at + 2 + 3 * i)
                    v_.tensor_tensor(t, r, r, ALU.mult).then_inc(step, 1)
                    eng.wait_ge(step, at + 3 + 3 * i)
                    v_.scalar_tensor_tensor(t, t, -0.5, v, ALU.mult, ALU.mult).then_inc(step, 1)
                    eng.wait_ge(step, at + 4 + 3 * i)
                    v_.scalar_tensor_tensor(r, t, 1.5, r, ALU.add, ALU.mult).then_inc(step, 1)

            def mix(ph):
                dve.wait_ge(s["y_done"], UNITS * QUADS * ph)
                dve.wait_ge(s["act_done"], UNITS * QUADS * ph)
                v_.tensor_copy(conv_now[:, :], conv_bd[:, bass.ds(ph - 1, 1), :].rearrange("p l o -> p (l o)"))
                v_.tensor_copy(g_now[:, :], g_all[:, :, bass.ds(ph, 1)].rearrange("p a l -> p (a l)"))
                v_.tensor_scalar(bias_now[:, :], bias_raw[:, bass.ds(ph - 1, 1)], float(HH * WW), None,
                                 ALU.mult).then_inc(s["now_done"], 1)
                base = (ph - 1) * GROUPS
                for t in range(1, GROUPS, 2):
                    wait(dve, "mix_done", base + t + 1)
                    v_.tensor_copy(modes[:, :, 4 * t:4 * t + 4], ps[t % 4][:, :].rearrange("p (m i) -> p i m", m=4)
                                   ).then_inc(s["mix_dve"], 1)

            def start_layer(ph):
                dve.wait_ge(s["ymodes_stored"], 16 * COMP * ph)
                turn_y(ph * QUADS)
                turn_z(ph * QUADS, 0)
                low_z(ph * QUADS, 0)

            copy_x(0, 0)
            run_phase(dve, 0, "stem", body)
            with dve.Fori(1, LAYERS) as ph:
                mix(ph)
                start_layer(ph)
                run_phase(dve, ph * QUADS, "layer", body)
            mix(LAYERS)
            start_layer(LAYERS)
            run_phase(dve, LAYERS * QUADS, "head", body)
            attention_vector(dve, newton)


def transform_tables():
    import numpy as np
    k, ky, h = np.arange(KX), np.arange(M), np.arange(HH)
    ch, sh = np.cos(2 * np.pi * np.outer(h, k) / HH), np.sin(2 * np.pi * np.outer(h, k) / HH)
    fwd_h, inv_h = np.zeros((2, HH, 2, 32)), np.zeros((4, 32, 2, HH))
    for i in range(2):
        fwd_h[i, :, i, 0:KX], fwd_h[i, :, i, 16:16 + KX] = ch, sh
    for i in range(4):
        inv_h[i, 0:KX, i % 2, :], inv_h[i, 16:16 + KX, i % 2, :] = ch.T, sh.T
    fwd_w, inv_w = np.zeros((4, 32, 2, 4, 32)), np.zeros((4, 32, 2, 4, 32))
    scale = np.where(ky == 0, 1.0, 2.0) / (HH * WW)
    for j in range(2):
        r = np.arange(32)
        w = 16 * (r % 4) + 8 * j + r // 4
        cw, sw = np.cos(2 * np.pi * np.outer(w, ky) / WW), np.sin(2 * np.pi * np.outer(w, ky) / WW)
        for i in range(4):
            fwd_w[i, :, j, i, 0:M], fwd_w[i, :, j, i, M:2 * M] = cw, sw
            inv_w[i, 0:M, j, i, :], inv_w[i, M:2 * M, j, i, :] = (cw * scale).T, (sw * scale).T
    center = np.zeros((4, 32, 4, 32))
    for i in range(4):
        center[i, :, i, :] = np.eye(32) - 1.0 / 32
    s1 = np.array([[1, -1, -1, -1], [1, 1, 1, -1], [1, 1, 1, -1], [-1, 1, 1, 1]])
    s2 = np.array([[1, -1, 1, 1], [1, 1, -1, 1], [-1, -1, 1, -1], [1, -1, 1, 1]])
    s2[:, 3], s2[:, 2] = s2[:, 3] * s2[:, 0], s2[:, 2] * s2[:, 1]
    sign = np.repeat(np.concatenate([s1, s2], 1), 32, 0)
    pick = np.repeat(np.eye(E)[:, :, None], 128, 2)
    lower = np.repeat(np.tril(np.ones((E, E)), -1).reshape(1, -1), 128, 0)
    tables = {"ident": np.eye(128), "center": center, "fwd_h": fwd_h, "fwd_w": fwd_w, "inv_w": inv_w, "inv_h": inv_h,
              "sign": sign, "pick": pick, "lower": lower}
    shapes = {"center": (128, 128), "fwd_h": (128, 64), "fwd_w": (128, 2, 128), "inv_w": (128, 2, 128), "inv_h": (128, 128),
              "pick": (E, E * 128)}
    return {n: np.ascontiguousarray(t.reshape(shapes.get(n, t.shape)), dtype=np.float32) for n, t in tables.items()}


_PARAMS = ["tok_fc0_w", "tok_fc0_b", "tok_ln0_g", "tok_ln0_b", "tok_w1r", "tok_w1i", "tok_w2r", "tok_w2i", "tok_conv_w",
           "tok_conv_b", "tok_ln_g", "tok_ln_b", "tok_fc1_w", "tok_fc1_b", "tok_fc2_w", "tok_fc2_b", "tok_fc3_w", "tok_fc3_b",
           "attn_Wq", "attn_bq", "attn_Wk", "attn_bk", "attn_Wv", "attn_bv", "attn_Wo", "attn_bo",
           "ffn_gamma", "ffn_beta", "ffn_Wr", "ffn_br", "ffn_W1", "ffn_b1", "ffn_W2", "ffn_b2"]


def kernel(**inputs):
    import numpy as _np
    import concourse.bacc as _bacc
    from concourse import mybir as _mybir
    from concourse.bass_utils import run_bass_kernel_spmd as _run

    nc = _bacc.Bacc("TRN2", target_bir_lowering=False, num_devices=1)
    f32 = _mybir.dt.float32
    arrays = {"x_dram": _np.ascontiguousarray(inputs["x"])}
    x = nc.dram_tensor("x_dram", arrays["x_dram"].shape, f32, kind="ExternalInput").ap()
    p, cst = {}, {}
    for name in _PARAMS:
        arr = _np.ascontiguousarray(inputs[f"L0_{name}"])
        arrays[f"in_{name}"] = arr
        p[name] = nc.dram_tensor(f"in_{name}", arr.shape, f32, kind="ExternalInput").ap()
    for name, arr in transform_tables().items():
        arrays[f"table_{name}"] = arr
        cst[name] = nc.dram_tensor(f"table_{name}", arr.shape, f32, kind="ExternalInput").ap()
    out = nc.dram_tensor("out_dram", (B, HH, WW), f32, kind="ExternalOutput").ap()
    scratch = [nc.dram_tensor(n, shape, f32, kind="Internal").ap() for n, shape in (
        ("xmodes", (QUADS, 128, COMP * MODES)), ("ymodes", (QUADS, 128, COMP * MODES)), ("hstore", (QUADS, 128, 2, 2048)),
        ("tok", (B, 4, 16 * HH)), ("fc0_rows", (4, 32)))]
    vit_tower(nc, x, p, cst, out, scratch)
    r = _run(nc, [arrays], core_ids=[0])
    return r.results[0]["out_dram"]
```
